# Optimizing a Trainium2 kernel written in Bass

```python
import numpy as np
import jax
import jax.numpy as jnp

def _softmax(x, axis=-1):
    return jax.nn.softmax(x, axis=axis)

def _gelu(x):
    return jax.nn.gelu(x, approximate=True)

def _silu(x):
    return jax.nn.silu(x)

def _sigmoid(x):
    return jax.nn.sigmoid(x)

def _layernorm(x, axis=-1, eps=1e-05):
    m = jnp.mean(x, axis=axis, keepdims=True)
    v = jnp.var(x, axis=axis, keepdims=True)
    return (x - m) / jnp.sqrt(v + eps)

def _scatter_add(tgt, idx, src, axis=0):
    return tgt.at[idx].add(src)

def _segment_sum(src, seg, n):
    return jax.ops.segment_sum(src, seg, n)
kernel_name = 'mk_gnn_preln_d2_gnn_r32_a455ce'

def setup_inputs(seed: int=0):
    np.random.seed(seed)
    _w = jnp.asarray

    def _rec_inputs():
        import jax
        import jax.numpy as jnp
        _gk = jax.random.key(seed)
        x = -0.0003713 + 1 * jax.random.normal(jax.random.fold_in(_gk, 1), (3125, 256), jnp.float32)
        src = jax.random.randint(jax.random.fold_in(_gk, 2), (50000,), 0, 3125, jnp.int32)
        dst = jax.random.randint(jax.random.fold_in(_gk, 3), (50000,), 0, 3125, jnp.int32)
        _o = jnp.argsort(dst, stable=True)
        src = src[_o]
        dst = dst[_o]
        edge_type_6 = jax.random.randint(jax.random.fold_in(_gk, 13), (50000,), 0, 6, jnp.int32)
        edge_type_64 = jax.random.randint(jax.random.fold_in(_gk, 14), (50000,), 0, 64, jnp.int32)
        node_type_3 = jax.random.randint(jax.random.fold_in(_gk, 15), (3125,), 0, 3, jnp.int32)
        return (x, src, dst, edge_type_6, edge_type_64, node_type_3)
    x, src, dst, edge_type_6, edge_type_64, node_type_3 = _rec_inputs()

    def _L0_gnn_setup():
        import jax, jax.numpy as jnp
        import numpy as np
        N_NODES = 50000
        N_EDGES = 15625
        IN_DIM = 256
        HID = 64
        HEADS = 4
        N_REL = 64
        key = jax.random.key(seed)
        ks = jax.random.split(key, 16)
        s = 0.02
        return {'node_features': jax.random.normal(ks[0], (N_NODES, IN_DIM), jnp.float32), 'edge_index': jax.random.randint(ks[1], (2, N_EDGES), 0, N_NODES, jnp.int32), 'edge_relations': jax.random.randint(ks[2], (N_EDGES,), 0, N_REL, jnp.int32), 'query_emb': jax.random.normal(ks[3], (IN_DIM,), jnp.float32), 'Wq': jax.random.normal(ks[4], (IN_DIM, HID * HEADS), jnp.float32) * s, 'bq': jnp.zeros((HID * HEADS,), jnp.float32), 'Wk': jax.random.normal(ks[5], (IN_DIM, HID * HEADS), jnp.float32) * s, 'bk': jnp.zeros((HID * HEADS,), jnp.float32), 'Wv': jax.random.normal(ks[6], (IN_DIM, HID * HEADS), jnp.float32) * s, 'bv': jnp.zeros((HID * HEADS,), jnp.float32), 'rel_w': jax.random.normal(ks[7], (N_REL, HID), jnp.float32) * s, 'Wo': jax.random.normal(ks[8], (HID * HEADS, IN_DIM), jnp.float32) * s, 'bo': jnp.zeros((IN_DIM,), jnp.float32), 'gamma': jnp.ones((IN_DIM,), jnp.float32), 'beta': jnp.zeros((IN_DIM,), jnp.float32)}
    _L0_gnn_all = _L0_gnn_setup()
    _L0_gnn_in = {k: v for k, v in _L0_gnn_all.items() if k in ('query_emb', 'Wq', 'bq', 'Wk', 'bk', 'Wv', 'bv', 'rel_w', 'Wo', 'bo', 'gamma', 'beta')}
    del _L0_gnn_all

    def _L1_gnn_setup():
        import jax, jax.numpy as jnp
        import numpy as np
        N, E, D, T, R, H = (50000, 12500, 256, 3, 6, 4)
        DK = D // H
        OUT = H * DK
        LN_EPS = 1e-05
        key = jax.random.key(seed)
        ks = jax.random.split(key, 16)
        std = 0.02
        f32 = jnp.float32
        inp = {'x': jax.random.normal(ks[0], (N, D), f32), 'Wk': jax.random.normal(ks[1], (T, D, OUT), f32) * std, 'bk': jnp.zeros((T, OUT), f32), 'Wq': jax.random.normal(ks[2], (T, D, OUT), f32) * std, 'bq': jnp.zeros((T, OUT), f32), 'Wv': jax.random.normal(ks[3], (T, D, OUT), f32) * std, 'bv': jnp.zeros((T, OUT), f32), 'Wa': jax.random.normal(ks[4], (T, OUT, OUT), f32) * std, 'ba': jnp.zeros((T, OUT), f32), 'rel_pri': jnp.ones((R, H), f32), 'rel_att': jax.random.normal(ks[5], (R, H, DK, DK), f32) * (1.0 / np.sqrt(DK)), 'rel_msg': jax.random.normal(ks[6], (R, H, DK, DK), f32) * (1.0 / np.sqrt(DK)), 'skip': jnp.ones((T,), f32), 'ln_g': jnp.ones((T, OUT), f32), 'ln_b': jnp.zeros((T, OUT), f32), 'node_type': jax.random.randint(ks[7], (N,), 0, T), 'edge_src': jax.random.randint(ks[8], (E,), 0, N), 'edge_dst': jax.random.randint(ks[9], (E,), 0, N), 'edge_type': jax.random.randint(ks[10], (E,), 0, R), 'n_heads': H}
        return inp
    _L1_gnn_all = _L1_gnn_setup()
    _L1_gnn_in = {k: v for k, v in _L1_gnn_all.items() if k in ('Wk', 'bk', 'Wq', 'bq', 'Wv', 'bv', 'Wa', 'ba', 'rel_pri', 'rel_att', 'rel_msg', 'skip', 'ln_g', 'ln_b')}
    del _L1_gnn_all
    return {'x': x, 'src': src, 'dst': dst, 'edge_type_6': edge_type_6, 'edge_type_64': edge_type_64, 'node_type_3': node_type_3, 'L0_gnn_query_emb': _L0_gnn_in['query_emb'], 'L0_gnn_Wq': _L0_gnn_in['Wq'], 'L0_gnn_bq': _L0_gnn_in['bq'], 'L0_gnn_Wk': _L0_gnn_in['Wk'], 'L0_gnn_bk': _L0_gnn_in['bk'], 'L0_gnn_Wv': _L0_gnn_in['Wv'], 'L0_gnn_bv': _L0_gnn_in['bv'], 'L0_gnn_rel_w': _L0_gnn_in['rel_w'], 'L0_gnn_Wo': _L0_gnn_in['Wo'], 'L0_gnn_bo': _L0_gnn_in['bo'], 'L0_gnn_gamma': _L0_gnn_in['gamma'], 'L0_gnn_beta': _L0_gnn_in['beta'], 'L1_gnn_Wk': _L1_gnn_in['Wk'], 'L1_gnn_bk': _L1_gnn_in['bk'], 'L1_gnn_Wq': _L1_gnn_in['Wq'], 'L1_gnn_bq': _L1_gnn_in['bq'], 'L1_gnn_Wv': _L1_gnn_in['Wv'], 'L1_gnn_bv': _L1_gnn_in['bv'], 'L1_gnn_Wa': _L1_gnn_in['Wa'], 'L1_gnn_ba': _L1_gnn_in['ba'], 'L1_gnn_rel_pri': _L1_gnn_in['rel_pri'], 'L1_gnn_rel_att': _L1_gnn_in['rel_att'], 'L1_gnn_rel_msg': _L1_gnn_in['rel_msg'], 'L1_gnn_skip': _L1_gnn_in['skip'], 'L1_gnn_ln_g': _L1_gnn_in['ln_g'], 'L1_gnn_ln_b': _L1_gnn_in['ln_b']}

def reference(x, src, dst, edge_type_6, edge_type_64, node_type_3, L0_gnn_query_emb, L0_gnn_Wq, L0_gnn_bq, L0_gnn_Wk, L0_gnn_bk, L0_gnn_Wv, L0_gnn_bv, L0_gnn_rel_w, L0_gnn_Wo, L0_gnn_bo, L0_gnn_gamma, L0_gnn_beta, L1_gnn_Wk, L1_gnn_bk, L1_gnn_Wq, L1_gnn_bq, L1_gnn_Wv, L1_gnn_bv, L1_gnn_Wa, L1_gnn_ba, L1_gnn_rel_pri, L1_gnn_rel_att, L1_gnn_rel_msg, L1_gnn_skip, L1_gnn_ln_g, L1_gnn_ln_b):
    import jax
    import jax.numpy as jnp

    def _L0_gnn_ref(node_features, edge_index, edge_relations, query_emb, Wq, bq, Wk, bk, Wv, bv, rel_w, Wo, bo, gamma, beta):
        import jax, jax.numpy as jnp
        import numpy as np
        N_NODES = 50000
        N_EDGES = 15625
        IN_DIM = 256
        HID = 64
        HEADS = 4
        N_REL = 64
        N = node_features.shape[0]
        D = rel_w.shape[1]
        H = Wq.shape[1] // D
        enh = node_features + 0.1 * query_emb[None, :]
        Q = (enh @ Wq + bq).reshape(N, H, D)
        K = (enh @ Wk + bk).reshape(N, H, D)
        V = (enh @ Wv + bv).reshape(N, H, D)
        src, dst = (edge_index[0], edge_index[1])
        rel = rel_w[edge_relations]
        mod_k = K[src] + 0.2 * rel[:, None, :]
        scores = jnp.einsum('ehd,ehd->eh', Q[dst], mod_k) / D ** 0.5
        seg_max = jax.ops.segment_max(scores, dst, num_segments=N)
        ex = jnp.exp(scores - seg_max[dst])
        denom = jax.ops.segment_sum(ex, dst, num_segments=N)
        w = ex / denom[dst]
        agg = jax.ops.segment_sum(w[:, :, None] * V[src], dst, num_segments=N)
        deg = jax.ops.segment_sum(jnp.ones((src.shape[0],), jnp.float32), dst, num_segments=N)
        msgs = jnp.where(deg[:, None, None] > 0, agg, V)
        out = msgs.reshape(N, H * D) @ Wo + bo
        x = out + node_features
        mu = jnp.mean(x, axis=-1, keepdims=True)
        var = jnp.var(x, axis=-1, keepdims=True)
        return (x - mu) / jnp.sqrt(var + 1e-05) * gamma + beta

    def _L1_gnn_ref(x, Wk, bk, Wq, bq, Wv, bv, Wa, ba, rel_pri, rel_att, rel_msg, skip, ln_g, ln_b, node_type, edge_src, edge_dst, edge_type, n_heads):
        import jax, jax.numpy as jnp
        import numpy as np
        N, E, D, T, R, H = (50000, 12500, 256, 3, 6, 4)
        DK = D // H
        OUT = H * DK
        LN_EPS = 1e-05
        n, d = x.shape
        r, h = rel_pri.shape
        dk = rel_att.shape[-1]
        out_dim = h * dk
        ar = jnp.arange(n)

        def typed_linear(inp_, W, b):
            y = jnp.einsum('ni,tio->tno', inp_, W) + b[:, None, :]
            return y[node_type, ar]
        k = typed_linear(x, Wk, bk).reshape(n, h, dk)
        q = typed_linear(x, Wq, bq).reshape(n, h, dk)
        v = typed_linear(x, Wv, bv).reshape(n, h, dk)
        k_rel = jnp.einsum('nhd,rhde->rnhe', k, rel_att)
        v_rel = jnp.einsum('nhd,rhde->rnhe', v, rel_msg)
        key_e = k_rel[edge_type, edge_src]
        val_e = v_rel[edge_type, edge_src]
        att = (q[edge_dst] * key_e).sum(-1) * rel_pri[edge_type] / jnp.sqrt(jnp.float32(dk))
        seg = edge_dst * r + edge_type
        S = n * r
        amax = jax.ops.segment_max(att, seg, num_segments=S)
        amax = jax.lax.stop_gradient(jnp.where(jnp.isfinite(amax), amax, 0.0))
        ex = jnp.exp(att - amax[seg])
        denom = jax.ops.segment_sum(ex, seg, num_segments=S)
        w = ex / denom[seg]
        hsum = jax.ops.segment_sum(w[:, :, None] * val_e, seg, num_segments=S)
        cnt = jax.ops.segment_sum(jnp.ones((seg.shape[0],), x.dtype), seg, num_segments=S)
        t_rel = hsum.reshape(n, r, out_dim)
        present = cnt.reshape(n, r) > 0
        nrel = jnp.maximum(present.sum(-1), 1).astype(x.dtype)
        t = (t_rel * present[..., None].astype(x.dtype)).sum(1) / nrel[:, None]
        trans = typed_linear(t, Wa, ba)
        alpha = jax.nn.sigmoid(skip)[node_type][:, None]
        out = trans * alpha + x * (1.0 - alpha)
        mu = out.mean(-1, keepdims=True)
        var = out.var(-1, keepdims=True)
        normed = (out - mu) * jax.lax.rsqrt(var + LN_EPS) * ln_g[node_type] + ln_b[node_type]
        has_msg = present.any(-1)[:, None]
        return jnp.where(has_msg, normed, x)
    edge_index = jnp.stack([src, dst])
    h = jnp.maximum(_layernorm(x, axis=-1), 0.0)
    x = x + _L0_gnn_ref(h, edge_index, edge_type_64, L0_gnn_query_emb, L0_gnn_Wq, L0_gnn_bq, L0_gnn_Wk, L0_gnn_bk, L0_gnn_Wv, L0_gnn_bv, L0_gnn_rel_w, L0_gnn_Wo, L0_gnn_bo, L0_gnn_gamma, L0_gnn_beta)
    h = jnp.maximum(_layernorm(x, axis=-1), 0.0)
    x = x + _L1_gnn_ref(h, L1_gnn_Wk, L1_gnn_bk, L1_gnn_Wq, L1_gnn_bq, L1_gnn_Wv, L1_gnn_bv, L1_gnn_Wa, L1_gnn_ba, L1_gnn_rel_pri, L1_gnn_rel_att, L1_gnn_rel_msg, L1_gnn_skip, L1_gnn_ln_g, L1_gnn_ln_b, node_type_3, src, dst, edge_type_6, 4)
    return x

_drawn_inputs = setup_inputs


def setup_inputs(seed=0):
    import zlib

    import numpy as np

    out = dict(_drawn_inputs(seed))
    spreads = {'L0_gnn_bq': (0.0, 2.0),
     'L0_gnn_bk': (0.0, 2.0),
     'L0_gnn_bv': (0.0, 0.318),
     'L0_gnn_bo': (0.0, 0.1),
     'L0_gnn_gamma': (1.0, 0.2),
     'L0_gnn_beta': (0.0, 0.1),
     'L1_gnn_bk': (0.0, 0.8),
     'L1_gnn_bq': (0.0, 0.8),
     'L1_gnn_bv': (0.0, 0.509),
     'L1_gnn_ba': (0.0, 0.1),
     'L1_gnn_rel_pri': (1.0, 0.6),
     'L1_gnn_skip': (1.0, 0.2),
     'L1_gnn_ln_g': (1.0, 0.2),
     'L1_gnn_ln_b': (0.0, 0.1)}
    factors = {'L0_gnn_query_emb': 8.0,
     'L0_gnn_Wq': 8.0,
     'L0_gnn_Wk': 8.0,
     'L0_gnn_rel_w': 200.0,
     'L1_gnn_Wk': 8.0,
     'L1_gnn_Wq': 8.0,
     'L1_gnn_rel_att': 8.0}
    for name, (base, spread) in spreads.items():
        noise = np.random.default_rng([zlib.crc32(name.encode()), seed]).standard_normal(out[name].shape)
        drawn = base * np.exp(spread * noise) if base else spread * noise
        out[name] = jnp.asarray(drawn.astype(out[name].dtype))
    for name, factor in factors.items():
        out[name] = (out[name] * factor).astype(out[name].dtype)
    return out
```

```python
import concourse.bass as bass
from concourse import mybir
from contextlib import ExitStack

FP = mybir.dt.float32
BF = mybir.dt.bfloat16
I32 = mybir.dt.int32
ALU = mybir.AluOpType
ACT = mybir.ActivationFunctionType
AX = mybir.AxisListType

N = 3125
E = 50000
D = 256
H = 4
DK = D // H
NR = 6
NREL = 64
NTY = 3
P = 125
NT = N // P
EW = 256
NROW = -(-E // EW)
STEPS = NROW + NT - 1
Q = STEPS // 2
SLOTS = 2 * EW
U = 4
ITERS = STEPS // U
C = H * NR
ACCW = D + NR
BIG = 1.0e30
EPS = 1e-05
FAR = 100000
assert NT * P == N and STEPS % 2 == 0 and ITERS * U == STEPS and Q <= 128


class Tally:

    def __init__(self, eng, sem):
        self.eng, self.sem, self.n, self.at = eng, sem, 0, 0

    def done(self, ins):
        self.n += 1
        ins.then_inc(self.sem, 1)
        self.eng.wait_ge(self.sem, self.at + self.n)

    def turn(self, i, each):
        self.at, self.n = i * each, 0


def sbuf(ctx, nc, name, shape, dt):
    return ctx.enter_context(nc.sbuf_tensor(name, shape, dt))


def semaphores(ctx, nc, prefix):
    made = []

    def sem(name):
        made.append(nc.alloc_semaphore(prefix + name))
        return made[-1]

    def give_back():
        nc.clear_and_free_semaphores(made)
        nc.all_engine_barrier()

    ctx.callback(give_back)
    return sem


class Persistent:

    def __init__(self, ctx, nc):
        self.ident = sbuf(ctx, nc, "ident_wide", [128, 132], FP)
        self.part = sbuf(ctx, nc, "part", [128, 1], FP)
        self.negpart = sbuf(ctx, nc, "negpart", [128, 1], FP)
        self.iota = sbuf(ctx, nc, "iota", [128, 2 * P], FP)
        self.ones = sbuf(ctx, nc, "ones", [128, 128], FP)
        self.eps = sbuf(ctx, nc, "eps", [128, 1], FP)
        self.tile_q = sbuf(ctx, nc, "tile_q", [1, STEPS], I32)
        self.tile_acc = sbuf(ctx, nc, "tile_acc", [1, STEPS], I32)
        self.idx0 = sbuf(ctx, nc, "idx0", [128, STEPS, 2], I32)
        self.idx1 = sbuf(ctx, nc, "idx1", [128, STEPS, 2], I32)
        self.dcol = sbuf(ctx, nc, "dcol", [128, STEPS, 2], FP)
        self.ecol = sbuf(ctx, nc, "ecol", [128, STEPS, 2], FP)
        self.same = sbuf(ctx, nc, "same", [Q, SLOTS], BF)
        self.same_b = sbuf(ctx, nc, "same_b", [Q, SLOTS], BF)
        self.next_b = sbuf(ctx, nc, "next_b", [Q, SLOTS], BF)
        self.next_in = sbuf(ctx, nc, "next_in", [Q, SLOTS], BF)
        self.next_out = sbuf(ctx, nc, "next_out", [Q, SLOTS], BF)
        self.pm = sbuf(ctx, nc, "pm", [Q, SLOTS], BF)
        self.sm = sbuf(ctx, nc, "sm", [Q, SLOTS], BF)
        self.pm_b = sbuf(ctx, nc, "pm_b", [Q, SLOTS], BF)
        self.sm_b = sbuf(ctx, nc, "sm_b", [Q, SLOTS], BF)
        self.etm = sbuf(ctx, nc, "etm", [Q, NR * SLOTS], BF)
        self.whole = sbuf(ctx, nc, "whole", [32, 4, Q], FP)
        self.Hn = sbuf(ctx, nc, "Hn", [P, NT, D], FP)
        self.X1 = sbuf(ctx, nc, "X1", [P, NT, D], FP)
        self.Qs = sbuf(ctx, nc, "Qs", [128, NT, 3, D], BF)
        self.acc = sbuf(ctx, nc, "acc", [P, NT, ACCW], FP)
        self.cnt = sbuf(ctx, nc, "cnt", [P, NT, NR], FP)
        dram = lambda name, shape, dt: nc.dram_tensor(name, shape, dt, kind="Internal").ap()
        self.edges = dram("edges", [NROW, 4, EW], I32)
        self.meta = dram("meta", [STEPS, 2, EW], BF)
        self.kv0 = dram("kv0", [N, 2 * D], FP)
        self.kv1 = dram("kv1", [N * NR, 2 * D], FP)
        self.vst = dram("vst", [STEPS, 128, 2, D], FP)

    def edge_tensors(self, ctx, nc, layer):
        self.S = sbuf(ctx, nc, f"S{layer}", [128, STEPS, 2, H], FP)
        self.W = sbuf(ctx, nc, f"W{layer}", [128, STEPS, 2, H], FP)

    def eye(self, n):
        return self.ident[0:n, 1:1 + n]


def setup_phase(nc, g, x, src, dst, et6, et64):
    with ExitStack() as ctx:
        sb = lambda name, shape, dt: sbuf(ctx, nc, name, shape, dt)
        ps = lambda name, shape: ctx.enter_context(nc.psum_tensor(name, shape, FP))
        sem = semaphores(ctx, nc, "e_")
        padi = sb("padi", [1, 2, EW], I32)
        lasti = sb("lasti", [1, NROW], I32)
        last = sb("last", [1, NROW], FP)
        below = sb("below", [NT, NROW], FP)
        thr = sb("thr", [NT, 1], FP)
        start = sb("start", [NT, 1], FP)
        kio = sb("kio", [NT, STEPS], FP)
        M = sb("M", [NT, STEPS], FP)
        krow = sb("krow", [Q, 2], FP)
        jcol = sb("jcol", [Q, 2], FP)
        jP = sb("jP", [Q, 2], FP)
        jf = sb("jf", [1, STEPS], FP)
        rowi = sb("rowi", [Q, 2], I32)
        rowf = sb("rowf", [Q, 2], FP)
        ER = sb("ER", [Q, 2, 4, EW], I32)
        EF = sb("EF", [Q, 4, 2, EW], FP)
        dloc = sb("dloc", [Q, 2, EW], FP)
        valid = sb("valid", [Q, 2, EW], FP)
        key = sb("key", [Q, SLOTS], FP)
        se = sb("se", [Q, SLOTS], FP)
        ne = sb("ne", [Q, SLOTS], FP)
        metab = sb("metab", [Q, 2, 2, EW], BF)
        wcol = sb("wcol", [Q, 2], FP)
        wbc = sb("wbc", [Q, 2, 32], FP)
        psA = ps("psA", [128, 512])
        psB = ps("psB", [128, 512])
        psC = ps("psC", [128, 512])
        psT = [ps(f"psT{n}", [128, 512]) for n in range(4)]
        const_ready = sem("const_ready")
        pad_ready = sem("pad_ready")
        last_loaded = sem("last_loaded")
        last_ready = sem("last_ready")
        last_bc = sem("last_bc")
        m_ready = sem("m_ready")
        j_ready = sem("j_ready")
        rowi_ready = sem("rowi_ready")
        edges_stored = sem("edges_stored")
        rows_loaded = [sem("rows_loaded0"), sem("rows_loaded1")]
        key_ready = sem("key_ready")
        key_shifted = sem("key_shifted")
        cols_in_ready = sem("cols_in_ready")
        cols_ready = sem("cols_ready")
        wbc_ready = sem("wbc_ready")
        whole_ready = sem("whole_ready")
        meta_ready = sem("meta_ready")
        meta_stored = sem("meta_stored")
        x_loaded = sem("x_loaded")
        pool_own = sem("pool_own")
        dve_own = sem("dve_own")
        block = ctx.enter_context(nc.Block())
        full = NROW - 1
        rest = E - full * EW

        @block.gpsimd
        def _(pool):
            t = Tally(pool, pool_own)
            t.done(nc.gpsimd.memset(g.ident[:, :], 0.0))
            t.done(nc.gpsimd.affine_select(out=g.ident[:, :], in_=g.ident[:, :], compare_op=ALU.not_equal, fill=1.0,
                                           base=1, pattern=[[-1, 132]], channel_multiplier=1))
            t.done(nc.gpsimd.iota(g.part[:, :], pattern=[[0, 1]], base=0, channel_multiplier=1,
                                  allow_small_or_imprecise_dtypes=True))
            t.done(nc.gpsimd.iota(g.iota[:, :], pattern=[[0, 2], [1, P]], base=0, channel_multiplier=0,
                                  allow_small_or_imprecise_dtypes=True))
            t.done(nc.gpsimd.iota(thr[:, :], pattern=[[0, 1]], base=0, channel_multiplier=P,
                                  allow_small_or_imprecise_dtypes=True))
            t.done(nc.gpsimd.iota(kio[:, :], pattern=[[1, STEPS]], base=0, channel_multiplier=0,
                                  allow_small_or_imprecise_dtypes=True))
            nc.gpsimd.iota(krow[:, :], pattern=[[1, 2]], base=0, channel_multiplier=2,
                           allow_small_or_imprecise_dtypes=True).then_inc(const_ready, 1)
            pool.wait_ge(edges_stored, 16 * 11)
            for b in range(2):
                pool.wait_ge(rowi_ready, 1)
                nc.gpsimd.indirect_dma_start(
                    out=ER[:, b, :, :].rearrange("q a e -> q (a e)"), out_offset=None,
                    in_=g.edges.rearrange("r a e -> r (a e)"),
                    in_offset=bass.IndirectOffsetOnAxis(ap=rowi[:, b:b + 1], axis=0)).then_inc(rows_loaded[b], 16)

        @block.sync
        def _(sp):
            sp.dma_start(lasti[0:1, 0:full], dst[0:full * EW].rearrange("(a r e) -> a r e", a=1, e=EW)[:, :, EW - 1],
                         allow_slow_non_contiguous=True).then_inc(last_loaded, 16)
            for a, arr in enumerate((dst, src, et64, et6)):
                sp.dma_start(g.edges[0:full, a, :], arr[0:full * EW].rearrange("(r e) -> r e", e=EW)).then_inc(edges_stored, 16)
                sp.dma_start(g.edges[full:NROW, a, 0:rest], arr[full * EW:E].rearrange("(r e) -> r e", r=1)) \
                    .then_inc(edges_stored, 16)
            sp.wait_ge(pad_ready, 1)
            sp.dma_start(g.edges[full:NROW, 0, rest:EW], padi[0:1, 0, rest:EW]).then_inc(edges_stored, 16)
            sp.dma_start(g.edges[full:NROW, 1:3, rest:EW],
                         padi[0:1, 1:2, rest:EW].to_broadcast([1, 2, EW - rest])).then_inc(edges_stored, 16)
            sp.dma_start(g.edges[full:NROW, 3, rest:EW], padi[0:1, 1, rest:EW]).then_inc(edges_stored, 16)
            sp.wait_ge(meta_ready, 1)
            for b in range(2):
                sp.dma_start(g.meta.rearrange("(q b) a e -> b q a e", b=2)[b], metab[:, b, :, :]).then_inc(meta_stored, 16)
            sp.wait_ge(meta_stored, 32)

        @block.scalar
        def _(act):
            act.dma_start(g.X1[:, :, :], x.rearrange("(t p) d -> p t d", p=P)).then_inc(x_loaded, 16)
            act.wait_ge(x_loaded, 16)

        @block.tensor
        def _(pe):
            pe.wait_ge(last_ready, 1)
            nc.tensor.matmul(psA[:, 0:NROW], g.ones[0:1, :], last[0:1, :], start=True, stop=True).then_inc(last_bc, 1)
            pe.wait_ge(m_ready, 1)
            Mb = M[:, :].rearrange("n (q b) -> n b q", b=2)
            for b in range(2):
                nc.tensor.matmul(psB[0:Q, b:b + 1], Mb[:, b, :], g.ones[0:NT, 0:1], start=True, stop=True)
            nc.tensor.matmul(psC[:, 0:STEPS], g.ones[0:NT, :], M[:, :], start=True, stop=True).then_inc(j_ready, 1)
            pe.wait_ge(key_ready, 1)
            nc.tensor.matmul(psA[0:Q, 0:1], g.ident[0:Q, 0:Q], key[:, SLOTS - 1:SLOTS], start=True, stop=True)
            nc.tensor.matmul(psA[0:Q, 1:2], g.ident[0:Q, 2:2 + Q], key[:, 0:1], start=True, stop=True) \
                .then_inc(key_shifted, 1)
            pe.wait_ge(cols_in_ready, 1)
            for n, rows in enumerate((EF[:, 1], EF[:, 0], dloc, EF[:, 3])):
                rows = rows[:, :, :]
                for b in range(2):
                    for f in range(2):
                        ins = nc.tensor.transpose(psT[n][:, (2 * b + f) * Q:(2 * b + f + 1) * Q],
                                                  rows[:, b, f * 128:f * 128 + 128], g.eye(Q))
            ins.then_inc(cols_ready, 1)
            pe.wait_ge(wbc_ready, 1)
            for n in range(2):
                ins = nc.tensor.transpose(psB[0:32, 128 * n:128 * n + Q], wbc[:, n, :], g.eye(Q))
            ins.then_inc(whole_ready, 1)

        @block.vector
        def _(dve):
            t = Tally(dve, dve_own)
            t.done(nc.vector.memset(g.ones[:, :], 1.0))
            t.done(nc.vector.memset(g.eps[:, :], EPS))
            t.done(nc.vector.memset(g.acc[:, :, :], 0.0))
            t.done(nc.vector.memset(padi[:, 0, :], FAR))
            nc.vector.memset(padi[:, 1, :], 0).then_inc(pad_ready, 1)
            t.done(nc.vector.memset(last[:, :], float(FAR)))
            dve.wait_ge(last_loaded, 16)
            t.done(nc.vector.tensor_copy(last[0:1, 0:full], lasti[0:1, 0:full]))
            nc.vector.memset(ne[:, :], 0.0).then_inc(last_ready, 1)
            dve.wait_ge(const_ready, 1)
            dve.wait_ge(last_bc, 1)
            t.done(nc.vector.tensor_scalar(g.negpart[:, :], g.part[:, :], -1.0, None, ALU.mult))
            t.done(nc.vector.tensor_scalar(below[:, :], psA[0:NT, 0:NROW], thr[:, 0:1], None, ALU.is_lt))
            t.done(nc.vector.reduce_sum(start[:, :], below[:, :], axis=AX.X))
            t.done(nc.vector.tensor_tensor(start[:, :], start[:, :], g.part[0:NT, :], ALU.add))
            nc.vector.tensor_scalar(M[:, :], kio[:, :], start[:, 0:1], None, ALU.is_ge).then_inc(m_ready, 1)
            dve.wait_ge(j_ready, 1)
            t.done(nc.vector.tensor_scalar(jcol[:, :], psB[0:Q, 0:2], -1.0, None, ALU.add))
            t.done(nc.vector.tensor_tensor(rowf[:, :], krow[:, :], jcol[:, :], ALU.subtract))
            nc.vector.tensor_copy(rowi[:, :], rowf[:, :]).then_inc(rowi_ready, 1)
            t.done(nc.vector.tensor_scalar(jP[:, :], jcol[:, :], float(P), None, ALU.mult))
            t.done(nc.vector.tensor_scalar(jf[:, :], psC[0:1, 0:STEPS], -1.0, float(3 * D), ALU.add, ALU.mult))
            t.done(nc.vector.tensor_copy(g.tile_q[:, :], jf[:, :]))
            t.done(nc.vector.tensor_scalar(jf[:, :], psC[0:1, 0:STEPS], -1.0, float(ACCW), ALU.add, ALU.mult))
            t.done(nc.vector.tensor_copy(g.tile_acc[:, :], jf[:, :]))
            for b in range(2):
                dve.wait_ge(rows_loaded[b], 16)
                t.done(nc.vector.tensor_copy(EF[:, :, b, :], ER[:, b, :, :]))
            for b in range(2):
                t.done(nc.vector.tensor_scalar(dloc[:, b, :], EF[:, 0, b, :], jP[:, b:b + 1], None, ALU.subtract))
            t.done(nc.vector.tensor_scalar(valid[:, :, :], dloc[:, :, :], 0.0, None, ALU.is_ge))
            t.done(nc.vector.scalar_tensor_tensor(valid[:, :, :], dloc[:, :, :], float(P - 1), valid[:, :, :],
                                                  ALU.is_le, ALU.mult))
            t.done(nc.vector.tensor_copy(metab[:, :, 0, :], dloc[:, :, :]))
            nc.vector.tensor_copy(metab[:, :, 1, :], EF[:, 2, :, :]).then_inc(meta_ready, 1)
            kv = key[:, :].rearrange("q (b e) -> q b e", b=2)
            t.done(nc.vector.scalar_tensor_tensor(kv, EF[:, 0, :, :], 2.0, valid[:, :, :], ALU.add, ALU.mult))
            t.done(nc.vector.tensor_scalar(key[:, :], key[:, :], -1.0, None, ALU.add))
            nc.vector.memset(se[:, 0:1], 0.0).then_inc(key_ready, 1)
            t.done(nc.vector.scalar_tensor_tensor(EF[:, 0, :, :], EF[:, 1, :, :], float(NR), EF[:, 3, :, :],
                                                  ALU.mult, ALU.add))
            nc.vector.memset(wbc[:, :, :], 0.0).then_inc(cols_in_ready, 1)
            for r in range(NR):
                er = EF[:, 3, :, :].rearrange("q b e -> q (b e)")
                t.done(nc.vector.tensor_scalar(g.etm[:, r * SLOTS:(r + 1) * SLOTS], er, float(r), None, ALU.is_equal))
            dve.wait_ge(key_shifted, 1)
            t.done(nc.vector.tensor_tensor(se[:, 1:SLOTS], key[:, 1:SLOTS], key[:, 0:SLOTS - 1], ALU.is_equal))
            t.done(nc.vector.tensor_tensor(se[:, 0:1], psA[0:Q, 0:1], key[:, 0:1], ALU.is_equal))
            t.done(nc.vector.tensor_copy(ne[:, 0:SLOTS - 1], se[:, 1:SLOTS]))
            t.done(nc.vector.tensor_copy(g.next_in[:, :], ne[:, :]))
            t.done(nc.vector.tensor_scalar(g.next_out[:, :], ne[:, :], -1.0, 1.0, ALU.mult, ALU.add))
            t.done(nc.vector.tensor_tensor(ne[:, SLOTS - 1:SLOTS], psA[0:Q, 1:2], key[:, SLOTS - 1:SLOTS], ALU.is_equal))
            t.done(nc.vector.tensor_copy(g.same[:, :], se[:, :]))
            t.done(nc.vector.tensor_scalar(g.same_b[:, :], se[:, :], BIG, -BIG, ALU.mult, ALU.add))
            t.done(nc.vector.tensor_scalar(g.next_b[:, :], ne[:, :], BIG, -BIG, ALU.mult, ALU.add))
            t.done(nc.vector.tensor_tensor_scan(g.pm[:, :], se[:, :], se[:, :], 1.0, ALU.mult, ALU.min))
            t.done(nc.vector.tensor_tensor_scan(g.sm[:, ::-1], ne[:, ::-1], ne[:, ::-1], 1.0, ALU.mult, ALU.min))
            t.done(nc.vector.tensor_scalar(g.pm_b[:, :], g.pm[:, :], BIG, -BIG, ALU.mult, ALU.add))
            t.done(nc.vector.tensor_scalar(g.sm_b[:, :], g.sm[:, :], BIG, -BIG, ALU.mult, ALU.add))
            t.done(nc.vector.tensor_copy(wbc[:, 0, :], g.pm[:, SLOTS - 1:SLOTS].to_broadcast([Q, 32])))
            nc.vector.tensor_copy(wbc[:, 1, :], g.sm[:, 0:1].to_broadcast([Q, 32])).then_inc(wbc_ready, 1)
            dve.wait_ge(cols_ready, 1)
            for n, col in enumerate((g.idx0, g.idx1, g.dcol, g.ecol)):
                t.done(nc.vector.tensor_copy(col[:, :, :].rearrange("p (q b) f -> p b f q", b=2),
                                             psT[n][:, 0:4 * Q].rearrange("p (b f q) -> p b f q", b=2, f=2)))
            dve.wait_ge(whole_ready, 1)
            whole = psB[0:32, 0:256].rearrange("p (n q) -> p n q", n=2)[:, :, 0:Q]
            t.done(nc.vector.tensor_copy(g.whole[:, 0:2, :], whole))
            t.done(nc.vector.tensor_scalar(g.whole[:, 2:4, :], whole, BIG, -BIG, ALU.mult, ALU.add))




NU = 5
NIT = NT // NU


def back(u):
    return {0: 1, 1: 3}.get(u, 2)


def flat(ap):
    return ap.rearrange("p a b -> p (a b)")


def tile(t2d, t, width):
    return t2d[:, bass.ds(t * width, width)]


def loop(eng, count, body):
    body(0, True)
    with eng.Fori(1, count) as i:
        body(i, False)


def row_bc(vec, n):
    return vec.rearrange("(a d) -> a d", a=1).partition_broadcast(n)


def project_phase(nc, g, query, Wq, bq, Wk, bk, Wv, bv):
    with ExitStack() as ctx:
        sb = lambda name, shape, dt: sbuf(ctx, nc, name, shape, dt)
        sem = semaphores(ctx, nc, "")
        Wt = sb("p_W", [128, 2, 3, D], FP)
        bias = sb("p_bias", [P, 3 * D], FP)
        qe = sb("p_qe", [P, D], FP)
        stats = sb("p_stats", [P, NU, 6], FP)
        mv = sb("p_mv", [P, NU, 2], FP)
        std = sb("p_std", [P, NU], FP)
        rstd = sb("p_rstd", [P, NU], FP)
        norm = sb("p_norm", [P, NU, D], FP)
        enh = sb("p_enh", [P, NU, D], FP)
        enhT = sb("p_enhT", [128, NU, 2, P], FP)
        qkv = sb("p_qkv", [P, NU, 3 * D], FP)
        rest = sb("p_rest", [P, NU, D], FP)
        psT = [ctx.enter_context(nc.psum_tensor(f"p_psT{s}", [128, 512], FP)) for s in range(2)]
        psM = [[ctx.enter_context(nc.psum_tensor(f"p_psM{s}{c}", [128, 512], FP)) for c in range(2)] for s in range(2)]
        w_loaded = sem("p_w_loaded")
        var_ready = sem("p_var_ready")
        std_ready = sem("p_std_ready")
        norm_ready = sem("p_norm_ready")
        h_ready = sem("p_h_ready")
        enh_ready = sem("p_enh_ready")
        enhT_in_psum = sem("p_enhT_in_psum")
        enhT_ready = sem("p_enhT_ready")
        product_ready = sem("p_product_ready")
        qkv_ready = sem("p_qkv_ready")
        q1_ready = sem("p_q1_ready")
        rest_ready = sem("p_rest_ready")
        q2_ready = sem("p_q2_ready")
        q3_ready = sem("p_q3_ready")
        kv_stored = [sem(f"p_kv_stored{u}") for u in range(NU)]
        waited = sem("p_waited")
        query_ready = sem("p_query_ready")
        dve_own = sem("p_dve_own")
        block = ctx.enter_context(nc.Block())
        HALF = 3 * D // 2
        X2, H2, Q2 = flat(g.X1[:, :, :]), flat(g.Hn[:, :, :]), g.Qs[0:P, :, :, :].rearrange("p t s d -> p (t s d)")
        kvt = g.kv0.rearrange("(t p) d -> p t d", p=P)

        @block.sync
        def _(sp):
            for n, (W, b) in enumerate(((Wq, bq), (Wk, bk), (Wv, bv))):
                sp.dma_start(Wt[:, :, n, :], W.rearrange("(c k) n -> k c n", c=2)).then_inc(w_loaded, 16)
                sp.dma_start(bias[:, n * D:(n + 1) * D], row_bc(b, P)).then_inc(w_loaded, 16)
            sp.dma_start(qe[:, :], row_bc(query, P)).then_inc(w_loaded, 16)

            with sp.Fori(0, NIT) as i:
                for u in range(NU):
                    sp.wait_ge(qkv_ready, i * NU + u + 1)
                    sp.dma_start(kvt[:, bass.ds(i * NU + u, 1), :], qkv[:, u:u + 1, D:3 * D]).then_inc(kv_stored[u], 16)
            for u in range(NU):
                sp.wait_ge(kv_stored[u], 16 * NIT)

        @block.scalar
        def _(act):
            def moments(i):
                act.wait_ge(var_ready, i + 1)
                nc.scalar.activation(std[:, :], mv[:, :, 1], ACT.Sqrt, bias=g.eps[0:P, :]).then_inc(std_ready, 1)

            def relu(i, u):
                act.wait_ge(norm_ready, i * NU + u + 1)
                nc.scalar.activation(tile(H2, i * NU + u, D), norm[:, u, :], ACT.Relu).then_inc(h_ready, 1)

            def move(i, u, first):
                k = i * NU + u
                act.wait_ge(enhT_in_psum, k + 1)
                if not first:
                    act.wait_ge(product_ready, k - NU + 1)
                nc.scalar.copy(flat(enhT[:, u, :, :]), psT[u % 2][:, 0:2 * P]).then_inc(enhT_ready, 1)
                act.wait_ge(qkv_ready, k + 1)
                nc.scalar.copy(Q2[:, bass.ds(k * 3 * D, D)], qkv[:, u, 0:D]).then_inc(q1_ready, 1)
                act.wait_ge(rest_ready, k + 1)
                nc.scalar.copy(Q2[:, bass.ds(k * 3 * D + D, D)], rest[:, u, :]).then_inc(q2_ready, 1)

            def turn(i, first, last):
                if not last:
                    moments(i + 1)
                for u in range(NU):
                    if not last:
                        relu(i + 1, u)
                    move(i, u, first)

            moments(0)
            for u in range(NU):
                relu(0, u)
            turn(0, True, False)
            with act.Fori(1, NIT - 1) as i:
                turn(i, False, False)
            turn(NIT - 1, False, True)

        @block.gpsimd
        def _(pool):
            with pool.Fori(0, NIT) as i:
                for u in range(NU):
                    k = i * NU + u
                    pool.wait_ge(q1_ready, k + 1)
                    nc.gpsimd.tensor_tensor(rest[:, u, :], qkv[:, u, 0:D], Q2[:, bass.ds(k * 3 * D, D)],
                                            ALU.subtract).then_inc(rest_ready, 1)
                    pool.wait_ge(q2_ready, k + 1)
                    nc.gpsimd.tensor_tensor(Q2[:, bass.ds(k * 3 * D + 2 * D, D)], rest[:, u, :],
                                            Q2[:, bass.ds(k * 3 * D + D, D)], ALU.subtract).then_inc(q3_ready, 1)

        @block.vector
        def _(dve):
            t = Tally(dve, dve_own)
            LN = 2

            def moments(i):
                t.turn(i, LN)
                for u in range(NU):
                    ins = nc.vector.bn_stats(stats[:, u, :], tile(X2, i * NU + u, D))
                t.done(ins)
                dve.sem_inc(waited, 1)
                for u in range(NU):
                    ins = nc.vector.bn_aggr(mv[:, u, :], stats[:, u, :])
                ins.then_inc(var_ready, 1)
                dve.wait_ge(std_ready, i + 1)
                t.done(nc.vector.reciprocal(rstd[:, :], std[:, :]))

            def normalise(i, u, first):
                k = i * NU + u
                if not first:
                    dve.wait_ge(h_ready, k - NU + 1)
                nc.vector.tensor_scalar(norm[:, u, :], tile(X2, k, D), mv[:, u, 0:1], rstd[:, u:u + 1],
                                        ALU.subtract, ALU.mult).then_inc(norm_ready, 1)
                dve.wait_ge(norm_ready, k + 1)
                if not first:
                    dve.wait_ge(enhT_in_psum, k - NU + 1)
                nc.vector.scalar_tensor_tensor(enh[:, u, :], norm[:, u, :], 0.0, qe[:, :], ALU.max,
                                               ALU.add).then_inc(enh_ready, 1)

            def move(i, u, first):
                k = i * NU + u
                dve.wait_ge(product_ready, k + 1)
                if not first:
                    dve.wait_ge(kv_stored[u], 16 * i)
                    dve.wait_ge(q3_ready, k - NU + 1)
                for c in range(2):
                    cols = slice(c * HALF, (c + 1) * HALF)
                    ins = nc.vector.tensor_tensor(qkv[:, u, cols], psM[u % 2][c][0:P, 0:HALF], bias[:, cols], ALU.add)
                ins.then_inc(qkv_ready, 1)

            def turn(i, first, last):
                if not last:
                    moments(i + 1)
                for u in range(NU):
                    if not last:
                        normalise(i + 1, u, False)
                    move(i, u, first)

            dve.wait_ge(w_loaded, 16 * 7)
            nc.vector.tensor_scalar(qe[:, :], qe[:, :], 0.1, None, ALU.mult).then_inc(query_ready, 1)
            dve.wait_ge(query_ready, 1)
            moments(0)
            for u in range(NU):
                normalise(0, u, True)
            turn(0, True, False)
            with dve.Fori(1, NIT - 1) as i:
                turn(i, False, False)
            turn(NIT - 1, False, True)

        @block.tensor
        def _(pe):
            pe.wait_ge(w_loaded, 16 * 7)

            def project(i, first):
                for u in range(NU):
                    k = i * NU + u
                    pe.wait_ge(enh_ready, k + 1)
                    if not first or u >= 2:
                        pe.wait_ge(enhT_ready, k - back(u) + 1)
                    for c in range(2):
                        ins = nc.tensor.transpose(psT[u % 2][:, c * P:(c + 1) * P], enh[:, u, c * 128:(c + 1) * 128],
                                                  g.eye(P))
                    ins.then_inc(enhT_in_psum, 1)
                    pe.wait_ge(enhT_ready, k + 1)
                    if not first or u >= 2:
                        pe.wait_ge(qkv_ready, k - back(u) + 1)
                    for b in range(2):
                        for c in range(2):
                            ins = nc.tensor.matmul(psM[u % 2][b][0:P, 0:HALF], enhT[:, u, c, :],
                                                   Wt[:, c, :, :].rearrange("k n d -> k (n d)")[:, b * HALF:(b + 1) * HALF],
                                                   start=(c == 0), stop=(c == 1))
                    ins.then_inc(product_ready, 1)

            loop(pe, NIT, project)


def score_phase(nc, g, layer, table, rel_w):
    L = f"s{layer}_"
    with ExitStack() as ctx:
        sb = lambda name, shape, dt: sbuf(ctx, nc, L + name, shape, dt)
        sem = semaphores(ctx, nc, L)
        parts = 2 if layer == 0 else 1
        kv = sb("kv", [128, U, 2, 2 * D], FP)
        idx = sb("idx", [128, U, 2], I32)
        mb = sb("mb", [P, U, parts * EW], BF)
        dist = sb("dist", [P, U, parts * EW], BF)
        hot = sb("hot", [P, U, parts * EW], BF)
        keyr = sb("keyr", [128, 2, 2 * D], FP) if layer == 0 else None
        prod = sb("prod", [128, 2, 2 * D], FP)
        relf = sb("relf", [NREL, DK], FP) if layer == 0 else None
        rel = sb("rel", [NREL, 3, D], BF) if layer == 0 else None
        psQ = [ctx.enter_context(nc.psum_tensor(f"{L}psQ{s}", [128, 512], FP)) for s in range(2)]
        psR = [ctx.enter_context(nc.psum_tensor(f"{L}psR{s}", [128, 512], FP)) for s in range(2)]
        gathered = [sem(f"gathered{u}") for u in range(U)]
        meta_loaded = [sem(f"meta_loaded{u}") for u in range(U)]
        v_stored = [sem(f"v_stored{u}") for u in range(U)]
        idx_ready = sem("idx_ready")
        waited = sem("waited")
        dist_ready = sem("dist_ready")
        hot_ready = sem("hot_ready")
        query_ready = sem("query_ready")
        key_read = sem("key_read")
        keyr_ready = sem("keyr_ready")
        prod_ready = sem("prod_ready")
        score_ready = sem("score_ready")
        rel_loaded = sem("rel_loaded")
        rel_ready = sem("rel_ready")
        dve_own = sem("dve_own")
        block = ctx.enter_context(nc.Block())
        idx_all = flat((g.idx0 if layer == 0 else g.idx1)[:, :, :])
        meta2 = g.meta.rearrange("k a e -> k (a e)")
        S2 = g.S[:, :, :, :].rearrange("p k f h -> p (k f h)")
        Q2 = g.Qs[0:P, :, :, :].rearrange("p t s d -> p (t s d)")
        vst = g.vst.rearrange("k p f d -> p k f d")

        @block.gpsimd
        def _(pool):
            def gather(i, first):
                for u in range(U):
                    k = i * U + u
                    if not first:
                        pool.wait_ge(v_stored[u], 16 * i)
                        pool.wait_ge(key_read if layer == 0 else prod_ready, k - U + 1)
                    nc.gpsimd.tensor_copy(idx[:, u, :], idx_all[:, bass.ds(k * 2, 2)]).then_inc(idx_ready, 1)
                    pool.wait_ge(idx_ready, k + 1)
                    pool.sem_inc(waited, 1)
                    for f in range(2):
                        nc.gpsimd.indirect_dma_start(
                            out=kv[:, u, f, :], out_offset=None, in_=table[:, :],
                            in_offset=bass.IndirectOffsetOnAxis(ap=idx[:, u, f:f + 1], axis=0)).then_inc(gathered[u], 16)

            loop(pool, ITERS, gather)

        @block.sync
        def _(sp):
            if layer == 0:
                sp.dma_start(relf[:, :], rel_w).then_inc(rel_loaded, 16)

            def move(i, first):
                for u in range(U):
                    k = i * U + u
                    if not first:
                        sp.wait_ge(dist_ready, k - U + 1)
                    sp.dma_start(mb[:, u, :], meta2[bass.ds(k, 1), 0:parts * EW].partition_broadcast(P)
                                 if False else meta2[bass.ds(k, 1), 0:parts * EW].to_broadcast([P, parts * EW])) \
                        .then_inc(meta_loaded[u], 16)
                for u in range(U):
                    k = i * U + u
                    sp.wait_ge(gathered[u], 32 * (i + 1))
                    sp.dma_start(vst[:, bass.ds(k, 1), :, :].rearrange("p k f d -> p (k f) d"), kv[:, u, :, D:2 * D]) \
                        .then_inc(v_stored[u], 16)

            loop(sp, ITERS, move)
            for u in range(U):
                sp.wait_ge(v_stored[u], 16 * ITERS)

        @block.scalar
        def _(act):
            def one_hot(i, first):
                for u in range(U):
                    k = i * U + u
                    act.wait_ge(meta_loaded[u], 16 * (i + 1))
                    nc.scalar.activation(dist[:, u, :], mb[:, u, :], ACT.Abs, bias=g.negpart[0:P, :]) \
                        .then_inc(dist_ready, 1)
                    act.wait_ge(dist_ready, k + 1)
                    if not first:
                        act.wait_ge(query_ready, k - U + 1)
                    nc.scalar.activation(hot[:, u, :], dist[:, u, :], ACT.Relu, bias=g.ones[0:P, 0:1], scale=-1.0) \
                        .then_inc(hot_ready, 1)

            loop(act, ITERS, one_hot)

        @block.tensor
        def _(pe):
            if layer == 0:
                pe.wait_ge(rel_ready, 1)

            def look_up(i, first):
                for u in range(U):
                    k = i * U + u
                    base = pe.value_load(g.tile_q[0:1, bass.ds(k, 1)], min_val=0, max_val=(NT - 1) * 3 * D)
                    pe.wait_ge(hot_ready, k + 1)
                    if not first or u >= 2:
                        pe.wait_ge(prod_ready, k - 1)
                    for f in range(2):
                        cols = slice(f * 128, f * 128 + 128)
                        if layer == 0:
                            for s in range(3):
                                nc.tensor.matmul(psR[u % 2][:, f * D:(f + 1) * D],
                                                 hot[0:NREL, u, EW + f * 128:EW + f * 128 + 128], rel[:, s, :],
                                                 start=(s == 0), stop=(s == 2))
                        for s in range(3):
                            ins = nc.tensor.matmul(psQ[u % 2][:, f * D:(f + 1) * D], hot[:, u, cols],
                                                   Q2[:, bass.ds(base + s * D, D)], start=(s == 0), stop=(s == 2))
                    ins.then_inc(query_ready, 1)

            loop(pe, ITERS, look_up)

        @block.vector
        def _(dve):
            if layer == 0:
                t = Tally(dve, dve_own)
                dve.wait_ge(rel_loaded, 16)
                t.done(nc.vector.tensor_scalar(relf[:, :], relf[:, :], 0.2, None, ALU.mult))
                for s in range(3):
                    t.done(nc.vector.tensor_copy(rel[:, s, 0:DK], relf[:, :]))
                    if s < 2:
                        t.done(nc.vector.tensor_tensor(relf[:, :], relf[:, :], rel[:, s, 0:DK], ALU.subtract))
                for h in range(1, H):
                    ins = nc.vector.tensor_copy(rel[:, :, h * DK:(h + 1) * DK], rel[:, :, 0:DK])
                ins.then_inc(rel_ready, 1)

            def score(i, first):
                for u in range(U):
                    k = i * U + u
                    s = u % 2
                    keys = kv[:, u, :, 0:D]
                    dve.wait_ge(gathered[u], 32 * (i + 1))
                    dve.wait_ge(query_ready, k + 1)
                    q = psQ[s][:, :].rearrange("p (f d) -> p f d", f=2)
                    k3 = keyr[:, s, :].rearrange("p (f d) -> p f d", f=2) if layer == 0 else None
                    p3 = prod[:, s, :].rearrange("p (f d) -> p f d", f=2)
                    if layer == 0:
                        nc.vector.tensor_tensor(k3, keys, psR[s][:, :].rearrange("p (f d) -> p f d", f=2), ALU.add) \
                            .then_inc(key_read, 1)
                        dve.wait_ge(key_read, k + 1)
                        nc.vector.tensor_tensor(p3, k3, q, ALU.mult).then_inc(prod_ready, 1)
                        dve.wait_ge(prod_ready, k + 1)
                    else:
                        nc.vector.tensor_tensor(p3, keys, q, ALU.mult).then_inc(prod_ready, 1)
                        dve.wait_ge(prod_ready, k + 1)
                    nc.vector.reduce_sum(S2[:, bass.ds(k * 2 * H, 2 * H)],
                                         prod[:, s, :].rearrange("p (c e) -> p c e", e=DK), axis=AX.X) \
                        .then_inc(score_ready, 1)

            loop(dve, ITERS, score)


def softmax_phase(nc, g, layer, pri):
    L = f"m{layer}_"
    rels = NR if layer == 1 else 1
    with ExitStack() as ctx:
        sb = lambda name, shape, dt: sbuf(ctx, nc, L + name, shape, dt)
        sem = semaphores(ctx, nc, L)
        row = lambda h: slice(h * SLOTS, (h + 1) * SLOTS)
        sc = sb("sc", [Q, H * SLOTS], FP)
        sel = sb("sel", [Q, H * SLOTS], FP)
        part = sb("part", [Q, SLOTS], FP)
        fwd = sb("fwd", [Q, SLOTS], FP)
        seg = sb("seg", [Q, SLOTS], FP)
        cf = sb("cf", [Q, SLOTS], FP)
        cb = sb("cb", [Q, SLOTS], FP)
        etm_b = sb("etm_b", [Q, NR * SLOTS], BF) if layer == 1 else None
        prib = sb("prib", [Q, C], FP) if layer == 1 else None
        ends = sb("ends", [Q, 2, 32], FP)
        endsT = sb("endsT", [32, 2, Q], FP)
        carry = sb("carry", [32, 2, Q + 2], FP)
        into = sb("into", [Q, 2, 32], FP)
        psS = [ctx.enter_context(nc.psum_tensor(f"{L}psS{h}", [128, 512], FP)) for h in range(H)]
        psE = ctx.enter_context(nc.psum_tensor(f"{L}psE", [128, 512], FP))
        psI = ctx.enter_context(nc.psum_tensor(f"{L}psI", [128, 512], FP))
        psW = [ctx.enter_context(nc.psum_tensor(f"{L}psW{n}", [128, 512], FP)) for n in range(2)]
        pri_loaded = sem("pri_loaded")
        rows_ready = sem("rows_ready")
        ends_ready = sem("ends_ready")
        ends_turned = sem("ends_turned")
        carry_ready = sem("carry_ready")
        carry_turned = sem("carry_turned")
        shifted = sem("shifted")
        exp_ready = sem("exp_ready")
        weights_ready = sem("weights_ready")
        w_turned = sem("w_turned")
        w_moved = sem("w_moved")
        dve_own = sem("dve_own")
        block = ctx.enter_context(nc.Block())
        Sv = g.S[:, :, :, :].rearrange("p (q b) f h -> p h b f q", b=2)
        Wv = g.W[:, :, :, :].rearrange("p (q b) f h -> p h b f q", b=2)

        if layer == 1:
            @block.sync
            def _(sp):
                sp.dma_start(prib[:, :], pri.rearrange("r h -> (r h)").rearrange("(a c) -> a c", a=1)
                             .partition_broadcast(Q)).then_inc(pri_loaded, 16)
                sp.wait_ge(pri_loaded, 16)

        @block.tensor
        def _(pe):
            for h in range(H):
                for b in range(2):
                    for f in range(2):
                        n = 2 * b + f
                        ins = nc.tensor.transpose(psS[h][0:Q, n * 128:(n + 1) * 128], Sv[:, h, b, f, :], g.eye(128))
                ins.then_inc(rows_ready, 1)
            for turn in range(2):
                pe.wait_ge(ends_ready, turn + 1)
                for n in range(2):
                    ins = nc.tensor.transpose(psE[0:32, n * 128:n * 128 + Q], ends[:, n, :], g.eye(Q))
                ins.then_inc(ends_turned, 1)
                pe.wait_ge(carry_ready, turn + 1)
                for n in range(2):
                    ins = nc.tensor.transpose(psI[0:Q, n * 32:(n + 1) * 32], carry[:, n, 1:1 + Q], g.eye(32))
                ins.then_inc(carry_turned, 1)
            for h in range(H):
                pe.wait_ge(weights_ready, h + 1)
                if h >= 2:
                    pe.wait_ge(w_moved, h - 1)
                for n in range(4):
                    ins = nc.tensor.transpose(psW[h % 2][:, n * Q:(n + 1) * Q],
                                              sc[:, h * SLOTS + n * 128:h * SLOTS + (n + 1) * 128], g.eye(Q))
                ins.then_inc(w_turned, 1)

        @block.scalar
        def _(act):
            for h in range(H):
                act.wait_ge(shifted, h + 1)
                nc.scalar.activation(sc[:, row(h)], sel[:, row(h)], ACT.Exp).then_inc(exp_ready, 1)
            for h in range(H):
                act.wait_ge(w_turned, h + 1)
                nc.scalar.copy(Wv[:, h], psW[h % 2][:, 0:4 * Q].rearrange("p (b f q) -> p b f q", b=2, f=2)) \
                    .then_inc(w_moved, 1)

        @block.vector
        def _(dve):
            t = Tally(dve, dve_own)

            def reduce_rows(kind, first):
                least = -BIG if kind == "max" else 0.0

                def column(r, h, start):
                    mask = g.etm[:, bass.ds(r * SLOTS, SLOTS)]
                    if layer == 0:
                        x = sc[:, row(h)]
                    else:
                        x = part[:, :]
                        if kind == "max":
                            t.done(nc.vector.tensor_tensor(x, sc[:, row(h)], etm_b[:, bass.ds(r * SLOTS, SLOTS)], ALU.add))
                        else:
                            t.done(nc.vector.tensor_tensor(x, sc[:, row(h)], mask, ALU.mult))
                    out = sel[:, row(h)] if layer == 0 else seg[:, :]
                    if kind == "max":
                        t.done(nc.vector.tensor_tensor_scan(fwd[:, :], g.same_b[:, :], x, -BIG, ALU.add, ALU.max))
                        t.done(nc.vector.tensor_tensor_scan(out[:, ::-1], g.next_b[:, ::-1], fwd[:, ::-1], -BIG,
                                                            ALU.add, ALU.max))
                    else:
                        t.done(nc.vector.tensor_tensor_scan(fwd[:, :], g.same[:, :], x, 0.0, ALU.mult, ALU.add))
                        t.done(nc.vector.tensor_tensor(fwd[:, :], fwd[:, :], g.next_out[:, :], ALU.mult))
                        t.done(nc.vector.tensor_tensor_scan(out[:, ::-1], g.next_in[:, ::-1], fwd[:, ::-1], 0.0,
                                                            ALU.mult, ALU.add))
                    t.done(nc.vector.tensor_copy(ends[:, :, bass.ds(r * H + h, 1)],
                                                 out[:, 0:SLOTS:SLOTS - 1].rearrange("q (n a) -> q n a", a=1)))
                    if layer == 1:
                        if start:
                            t.done(nc.vector.tensor_tensor(sel[:, row(h)], seg[:, :], mask, ALU.mult))
                        else:
                            t.done(nc.vector.tensor_tensor(seg[:, :], seg[:, :], mask, ALU.mult))
                            t.done(nc.vector.tensor_tensor(sel[:, row(h)], sel[:, row(h)], seg[:, :], ALU.add))

                for r in range(rels):
                    for h in range(H):
                        column(r, h, r == 0)
                ins = nc.vector.memset(part[:, 0:1], 0.0)
                ins.then_inc(ends_ready, 1)
                dve.wait_ge(ends_turned, 1 if kind == "max" else 2)
                t.done(nc.vector.tensor_copy(endsT[:, :, :],
                                             psE[0:32, 0:256].rearrange("c (n q) -> c n q", n=2)[:, :, 0:Q]))
                t.done(nc.vector.memset(carry[:, :, :], least))
                op = (ALU.add, ALU.max) if kind == "max" else (ALU.mult, ALU.add)
                w = 2 if kind == "max" else 0
                t.done(nc.vector.tensor_tensor_scan(carry[:, 0, 0:Q][:, ::-1], g.whole[:, w + 1, ::-1], endsT[:, 0, ::-1],
                                                    least, op[0], op[1]))
                nc.vector.tensor_tensor_scan(carry[:, 1, 2:Q + 2], g.whole[:, w, :], endsT[:, 1, :],
                                             least, op[0], op[1]).then_inc(carry_ready, 1)
                dve.wait_ge(carry_turned, 1 if kind == "max" else 2)
                t.done(nc.vector.tensor_copy(flat(into[:, :, :]), psI[0:Q, 0:64]))

            def add_carries(kind, h):
                s = sel[:, row(h)]
                if layer == 0:
                    for n, (m, mbias) in enumerate(((g.sm, g.sm_b), (g.pm, g.pm_b))):
                        if kind == "max":
                            t.done(nc.vector.scalar_tensor_tensor(s, mbias[:, :], into[:, n, h:h + 1], s, ALU.add, ALU.max))
                        else:
                            t.done(nc.vector.scalar_tensor_tensor(s, m[:, :], into[:, n, h:h + 1], s, ALU.mult, ALU.add))
                    return
                for n, (m, mbias, c) in enumerate(((g.sm, g.sm_b, cb), (g.pm, g.pm_b, cf))):
                    t.done(nc.vector.tensor_scalar(c[:, :], g.etm[:, 0:SLOTS], into[:, n, h:h + 1], None, ALU.mult))
                    for r in range(1, NR):
                        t.done(nc.vector.scalar_tensor_tensor(c[:, :], g.etm[:, r * SLOTS:(r + 1) * SLOTS],
                                                              into[:, n, r * H + h:r * H + h + 1], c[:, :],
                                                              ALU.mult, ALU.add))
                    if kind == "max":
                        t.done(nc.vector.tensor_tensor(c[:, :], c[:, :], mbias[:, :], ALU.add))
                        t.done(nc.vector.tensor_tensor(s, s, c[:, :], ALU.max))
                    else:
                        t.done(nc.vector.tensor_tensor(c[:, :], c[:, :], m[:, :], ALU.mult))
                        t.done(nc.vector.tensor_tensor(s, s, c[:, :], ALU.add))

            t.done(nc.vector.memset(ends[:, :, :], 0.0))
            if layer == 1:
                t.done(nc.vector.tensor_scalar(etm_b[:, :], g.etm[:, :], BIG, -BIG, ALU.mult, ALU.add))
                dve.wait_ge(pri_loaded, 16)
                t.done(nc.vector.tensor_scalar(prib[:, :], prib[:, :], DK ** -0.5, None, ALU.mult))
            for h in range(H):
                dve.wait_ge(rows_ready, h + 1)
                if layer == 0:
                    t.done(nc.vector.tensor_scalar(sc[:, row(h)], psS[h][0:Q, :], DK ** -0.5, None, ALU.mult))
                else:
                    t.done(nc.vector.tensor_scalar(part[:, :], g.etm[:, 0:SLOTS], prib[:, h:h + 1], None, ALU.mult))
                    for r in range(1, NR):
                        t.done(nc.vector.scalar_tensor_tensor(part[:, :], g.etm[:, r * SLOTS:(r + 1) * SLOTS],
                                                              prib[:, r * H + h:r * H + h + 1], part[:, :],
                                                              ALU.mult, ALU.add))
                    t.done(nc.vector.tensor_tensor(sc[:, row(h)], psS[h][0:Q, :], part[:, :], ALU.mult))
            reduce_rows("max", True)
            for h in range(H):
                add_carries("max", h)
                nc.vector.tensor_tensor(sel[:, row(h)], sc[:, row(h)], sel[:, row(h)], ALU.subtract).then_inc(shifted, 1)
            dve.wait_ge(exp_ready, H)
            reduce_rows("sum", False)
            for h in range(H):
                add_carries("sum", h)
                t.done(nc.vector.reciprocal(sel[:, row(h)], sel[:, row(h)]))
                nc.vector.tensor_tensor(sc[:, row(h)], sc[:, row(h)], sel[:, row(h)], ALU.mult).then_inc(weights_ready, 1)


def aggregate_phase(nc, g, layer):
    L = f"a{layer}_"
    with ExitStack() as ctx:
        sb = lambda name, shape, dt: sbuf(ctx, nc, L + name, shape, dt)
        sem = semaphores(ctx, nc, L)
        width = ACCW if layer == 0 else D
        v = sb("v", [128, U, 2, D], FP)
        wv = sb("wv", [128, U, 2, ACCW], FP)
        diff = sb("diff", [128, U, 2, P], FP)
        dist = sb("dist", [128, U, 2, P], FP)
        hot = sb("hot", [128, U, 2, P], FP)
        psA = [ctx.enter_context(nc.psum_tensor(f"{L}psA{s}", [128, 512], FP)) for s in range(2)]
        v_loaded = [sem(f"v_loaded{u}") for u in range(U)]
        diff_ready = sem("diff_ready")
        dist_ready = sem("dist_ready")
        hot_ready = sem("hot_ready")
        wv_ready = sem("wv_ready")
        sum_ready = sem("sum_ready")
        added = sem("added")
        zeroed = sem("zeroed")
        block = ctx.enter_context(nc.Block())
        vst = g.vst.rearrange("k p f d -> p k f d")
        acc2 = flat(g.acc[:, :, :])
        W3 = g.W[:, :, :, :].rearrange("p k f h -> p (k f h)")
        dcol, ecol = flat(g.dcol[:, :, :]), flat(g.ecol[:, :, :])
        iota = g.iota[:, :].rearrange("p (f n) -> p f n", f=2)

        @block.sync
        def _(sp):
            def load(i, first):
                for u in range(U):
                    k = i * U + u
                    if not first:
                        sp.wait_ge(wv_ready, k - U + 1)
                    sp.dma_start(v[:, u, :, :], vst[:, bass.ds(k, 1), :, :].rearrange("p k f d -> p (k f) d")) \
                        .then_inc(v_loaded[u], 16)

            loop(sp, ITERS, load)

        @block.gpsimd
        def _(pool):
            def distance(i, first):
                for u in range(U):
                    k = i * U + u
                    if not first:
                        pool.wait_ge(dist_ready, k - U + 1)
                    nc.gpsimd.tensor_tensor(diff[:, u, :, :], iota,
                                            dcol[:, bass.ds(k * 2, 2)].unsqueeze(2).to_broadcast([128, 2, P]),
                                            ALU.subtract).then_inc(diff_ready, 1)

            loop(pool, ITERS, distance)

        @block.scalar
        def _(act):
            def one_hot(i, first):
                for u in range(U):
                    k = i * U + u
                    act.wait_ge(diff_ready, k + 1)
                    if not first:
                        act.wait_ge(hot_ready, k - U + 1)
                    nc.scalar.activation(dist[:, u, :, :], diff[:, u, :, :], ACT.Abs).then_inc(dist_ready, 1)
                    act.wait_ge(dist_ready, k + 1)
                    if not first:
                        act.wait_ge(sum_ready, k - U + 1)
                    nc.scalar.activation(hot[:, u, :, :], dist[:, u, :, :], ACT.Relu, bias=g.ones[:, 0:1], scale=-1.0) \
                        .then_inc(hot_ready, 1)

            loop(act, ITERS, one_hot)

        @block.tensor
        def _(pe):
            def add_up(i, first):
                for u in range(U):
                    k = i * U + u
                    pe.wait_ge(hot_ready, k + 1)
                    pe.wait_ge(wv_ready, k + 1)
                    if not first or u >= 2:
                        pe.wait_ge(added, k - 1)
                    for f in range(2):
                        ins = nc.tensor.matmul(psA[u % 2][0:P, 0:width], hot[:, u, f, :], wv[:, u, f, 0:width],
                                               start=(f == 0), stop=(f == 1))
                    ins.then_inc(sum_ready, 1)

            loop(pe, ITERS, add_up)

        @block.vector
        def _(dve):
            nc.vector.memset(acc2, 0.0).then_inc(zeroed, 1)
            dve.wait_ge(zeroed, 1)

            def add(k, s, start):
                base = dve.value_load(g.tile_acc[0:1, bass.ds(k, 1)], min_val=0, max_val=(NT - 1) * ACCW)
                dve.wait_ge(sum_ready, k + 1)
                if not start:
                    dve.wait_ge(added, k)
                nc.vector.tensor_tensor(acc2[:, bass.ds(base, width)], acc2[:, bass.ds(base, width)],
                                        psA[s][0:P, 0:width], ALU.add).then_inc(added, 1)

            def weigh(i, first):
                for u in range(U):
                    k = i * U + u
                    dve.wait_ge(v_loaded[u], 16 * (i + 1))
                    if not first:
                        dve.wait_ge(sum_ready, k - U + 1)
                    if layer == 0:
                        nc.vector.tensor_tensor(wv[:, u, :, D:ACCW], iota[:, :, 0:NR],
                                                ecol[:, bass.ds(k * 2, 2)].unsqueeze(2).to_broadcast([128, 2, NR]),
                                                ALU.is_equal)
                    nc.vector.tensor_tensor(wv[:, u, :, 0:D].rearrange("p f (h e) -> p f h e", h=H),
                                            v[:, u, :, :].rearrange("p f (h e) -> p f h e", h=H),
                                            W3[:, bass.ds(k * 2 * H, 2 * H)].rearrange("p (f h) -> p f h", f=2)
                                            .unsqueeze(3).to_broadcast([128, 2, H, DK]),
                                            ALU.mult).then_inc(wv_ready, 1)
                    if not (first and u == 0):
                        add(k - 1, (u - 1) % 2, first and u == 1)

            loop(dve, ITERS, weigh)
            add(STEPS - 1, (U - 1) % 2, False)


class Types:

    def __init__(self, ctx, nc):
        self.hot = sbuf(ctx, nc, "type_hot", [NTY, N], FP)
        self.row = sbuf(ctx, nc, "type_row", [128, N], BF)


def layer0_output_phase(nc, g, ty, Wo, bo, gamma, beta, node_type):
    with ExitStack() as ctx:
        sb = lambda name, shape, dt: sbuf(ctx, nc, "o_" + name, shape, dt)
        sem = semaphores(ctx, nc, "o_")
        Wt = sb("W", [128, 2, D], FP)
        bob, gab, beb = sb("bo", [P, D], FP), sb("gamma", [P, D], FP), sb("beta", [P, D], FP)
        types = g.Qs[:, :, :, :].rearrange("p t s d -> p (t s d)")[:, 0:2 * N].bitcast(I32)
        deg = sb("deg", [P, NT], FP)
        alone = sb("alone", [P, NT], FP)
        v0 = sb("v0", [P, NU, D], FP)
        msg = sb("msg", [P, NU, D], FP)
        msgT = sb("msgT", [128, NU, 2, P], FP)
        hb = sb("hb", [P, NU, D], FP)
        xb = sb("xb", [P, NU, D], FP)
        y = sb("y", [P, NU, D], FP)
        stats = sb("stats", [P, NU, 6], FP)
        mv = sb("mv", [P, NU, 2], FP)
        std = sb("std", [P, NU], FP)
        rstd = sb("rstd", [P, NU], FP)
        psT = [ctx.enter_context(nc.psum_tensor(f"o_psT{s}", [128, 512], FP)) for s in range(2)]
        psO = [ctx.enter_context(nc.psum_tensor(f"o_psO{s}", [128, 512], FP)) for s in range(2)]
        loaded = sem("loaded")
        types_loaded = sem("types_loaded")
        v_loaded = sem("v_loaded")
        msg_ready = sem("msg_ready")
        msgT_in_psum = sem("msgT_in_psum")
        msgT_ready = sem("msgT_ready")
        out_in_psum = sem("out_in_psum")
        y_ready = sem("y_ready")
        hb_ready = sem("hb_ready")
        xb_ready = sem("xb_ready")
        var_ready = sem("var_ready")
        std_ready = sem("std_ready")
        x1_ready = sem("x1_ready")
        norm_ready = sem("norm_ready")
        h_ready = sem("h_ready")
        waited = sem("waited")
        start_own = sem("start_own")
        dve_own = sem("dve_own")
        block = ctx.enter_context(nc.Block())
        X2, H2, A2 = flat(g.X1[:, :, :]), flat(g.Hn[:, :, :]), flat(g.acc[:, :, :])
        v0t = g.kv0.rearrange("(t p) d -> p t d", p=P)

        @block.sync
        def _(sp):
            sp.dma_start(Wt[:, :, :], Wo.rearrange("(c k) n -> k c n", c=2)).then_inc(loaded, 16)
            for dst_, vec in ((bob, bo), (gab, gamma), (beb, beta)):
                sp.dma_start(dst_[:, :], row_bc(vec, P)).then_inc(loaded, 16)
            sp.dma_start(types, row_bc(node_type, 128)).then_inc(types_loaded, 16)

            def load(i, first):
                if not first:
                    sp.wait_ge(msg_ready, i * NU)
                sp.dma_start(v0[:, :, :], v0t[:, bass.ds(i * NU, NU), D:2 * D]).then_inc(v_loaded, 16)

            loop(sp, NIT, load)

        @block.gpsimd
        def _(pool):
            pool.wait_ge(loaded, 64)

            def add(i, first):
                for u in range(NU):
                    k = i * NU + u
                    if not first:
                        pool.wait_ge(y_ready, k - NU + 1)
                    nc.gpsimd.tensor_tensor(hb[:, u, :], tile(H2, k, D), bob[:, :], ALU.add).then_inc(hb_ready, 1)
                    if not first:
                        pool.wait_ge(x1_ready, k - NU + 1)
                    nc.gpsimd.tensor_tensor(xb[:, u, :], tile(X2, k, D), beb[:, :], ALU.add).then_inc(xb_ready, 1)

            loop(pool, NIT, add)

        @block.scalar
        def _(act):
            def turn(i, first):
                for u in range(NU):
                    k = i * NU + u
                    act.wait_ge(msgT_in_psum, k + 1)
                    if not first:
                        act.wait_ge(out_in_psum, k - NU + 1)
                    nc.scalar.copy(flat(msgT[:, u, :, :]), psT[u % 2][:, 0:2 * P]).then_inc(msgT_ready, 1)
                for n in range(2):
                    act.wait_ge(var_ready, i * 2 + n + 1)
                    nc.scalar.activation(std[:, :], mv[:, :, 1], ACT.Sqrt, bias=g.eps[0:P, :]).then_inc(std_ready, 1)
                for u in range(NU):
                    k = i * NU + u
                    act.wait_ge(norm_ready, k + 1)
                    nc.scalar.activation(tile(H2, k, D), y[:, u, :], ACT.Relu).then_inc(h_ready, 1)

            loop(act, NIT, turn)

        @block.tensor
        def _(pe):
            pe.wait_ge(loaded, 64)

            def turn(i, first):
                for u in range(NU):
                    k = i * NU + u
                    pe.wait_ge(msg_ready, k + 1)
                    if not first or u >= 2:
                        pe.wait_ge(msgT_ready, k - back(u) + 1)
                    for c in range(2):
                        ins = nc.tensor.transpose(psT[u % 2][:, c * P:(c + 1) * P], msg[:, u, c * 128:(c + 1) * 128],
                                                  g.eye(P))
                    ins.then_inc(msgT_in_psum, 1)
                    pe.wait_ge(msgT_ready, k + 1)
                    if not first or u >= 2:
                        pe.wait_ge(y_ready, k - back(u) + 1)
                    for c in range(2):
                        ins = nc.tensor.matmul(psO[u % 2][0:P, 0:D], msgT[:, u, c, :], Wt[:, c, :],
                                               start=(c == 0), stop=(c == 1))
                    ins.then_inc(out_in_psum, 1)

            loop(pe, NIT, turn)

        @block.vector
        def _(dve):
            s = Tally(dve, start_own)
            t = Tally(dve, dve_own)
            dve.wait_ge(types_loaded, 16)
            s.done(nc.vector.tensor_copy(ty.row[:, :], types))
            s.done(nc.vector.tensor_scalar(ty.hot[:, :], ty.row[0:NTY, :], g.part[0:NTY, :], None, ALU.is_equal))
            s.done(nc.vector.tensor_copy(g.cnt[:, :, :], g.acc[:, :, D:ACCW]))
            s.done(nc.vector.reduce_sum(deg[:, :], g.cnt[:, :, :], axis=AX.X))
            s.done(nc.vector.tensor_scalar(alone[:, :], deg[:, :], 0.5, None, ALU.is_lt))
            dve.wait_ge(loaded, 64)

            def statistics(i, n):
                for u in range(NU):
                    ins = nc.vector.bn_stats(stats[:, u, :], y[:, u, :] if n == 0 else tile(X2, i * NU + u, D))
                t.done(ins)
                dve.sem_inc(waited, 1)
                for u in range(NU):
                    ins = nc.vector.bn_aggr(mv[:, u, :], stats[:, u, :])
                ins.then_inc(var_ready, 1)
                dve.wait_ge(std_ready, i * 2 + n + 1)
                t.done(nc.vector.reciprocal(rstd[:, :], std[:, :]))

            def turn(i, first):
                t.turn(i, 2 * 2 + 2)
                dve.wait_ge(v_loaded, 16 * (i + 1))
                for u in range(NU):
                    k = i * NU + u
                    if not first:
                        dve.wait_ge(msgT_in_psum, k - NU + 1)
                    nc.vector.scalar_tensor_tensor(msg[:, u, :], v0[:, u, :], alone[:, bass.ds(k, 1)],
                                                   A2[:, bass.ds(k * ACCW, D)], ALU.mult, ALU.add).then_inc(msg_ready, 1)
                for u in range(NU):
                    k = i * NU + u
                    dve.wait_ge(out_in_psum, k + 1)
                    dve.wait_ge(hb_ready, k + 1)
                    if not first:
                        dve.wait_ge(h_ready, k - NU + 1)
                    nc.vector.tensor_tensor(y[:, u, :], psO[u % 2][0:P, 0:D], hb[:, u, :], ALU.add).then_inc(y_ready, 1)
                dve.wait_ge(y_ready, i * NU + NU)
                dve.sem_inc(waited, 1)
                statistics(i, 0)
                for u in range(NU):
                    ins = nc.vector.scalar_tensor_tensor(msg[:, u, :], y[:, u, :], mv[:, u, 0:1], gab[:, :],
                                                         ALU.subtract, ALU.mult)
                t.done(ins)
                for u in range(NU):
                    k = i * NU + u
                    dve.wait_ge(xb_ready, k + 1)
                    nc.vector.scalar_tensor_tensor(tile(X2, k, D), msg[:, u, :], rstd[:, u:u + 1], xb[:, u, :],
                                                   ALU.mult, ALU.add).then_inc(x1_ready, 1)
                dve.wait_ge(x1_ready, i * NU + NU)
                dve.sem_inc(waited, 1)
                statistics(i, 1)
                for u in range(NU):
                    nc.vector.tensor_scalar(y[:, u, :], tile(X2, i * NU + u, D), mv[:, u, 0:1], rstd[:, u:u + 1],
                                            ALU.subtract, ALU.mult).then_inc(norm_ready, 1)
                t.done(nc.vector.memset(deg[:, 0:1], 0.0))

            loop(dve, NIT, turn)


def typed_project_phase(nc, g, ty, Wk, bk, Wq, bq, Wv, bv, rel_att, rel_msg):
    with ExitStack() as ctx:
        sb = lambda name, shape, dt: sbuf(ctx, nc, "t_" + name, shape, dt)
        sem = semaphores(ctx, nc, "t_")
        HALF = 3 * D // 2
        KC = D // 128
        Wt = sb("W", [128, KC, NTY, 3 * D], FP)
        bt = sb("b", [NTY, 3 * D], FP)
        R = sb("R", [128, 2, H // 2, NR * DK], FP)
        hm = sb("hm", [128, 2, NTY, KC * P], FP)
        hs = sb("hs", [P, 2, D], FP)
        types = sb("types", [NTY, 2, P], FP)
        qkv = sb("qkv", [P, 2, 3 * D], FP)
        rest = sb("rest", [P, 2, D], FP)
        kvT = sb("kvT", [128, 2, 4 * P], FP)
        T = flat(g.acc[:, :, :])[:, 0:2 * NR * 2 * D].rearrange("p (s n) -> p s n", s=2)
        psH = ctx.enter_context(nc.psum_tensor("t_psH", [128, 512], FP))
        psM = [ctx.enter_context(nc.psum_tensor(f"t_psM{c}", [128, 512], FP)) for c in range(2)]
        psK = ctx.enter_context(nc.psum_tensor("t_psK", [128, 512], FP))
        psR = [ctx.enter_context(nc.psum_tensor(f"t_psR{c}", [128, 512], FP)) for c in range(4)]
        loaded = sem("loaded")
        hs_ready = sem("hs_ready")
        hT_in_psum = sem("hT_in_psum")
        hm_ready = sem("hm_ready")
        product_ready = sem("product_ready")
        qkv_ready = sem("qkv_ready")
        q1_ready = sem("q1_ready")
        rest_ready = sem("rest_ready")
        q2_ready = sem("q2_ready")
        q3_ready = sem("q3_ready")
        kvT_in_psum = sem("kvT_in_psum")
        kvT_ready = sem("kvT_ready")
        rel_in_psum = sem("rel_in_psum")
        rel_by_dve = sem("rel_by_dve")
        rel_by_act = sem("rel_by_act")
        stored = [sem(f"stored{u}") for u in range(NU)]
        block = ctx.enter_context(nc.Block())
        H2, Q2 = flat(g.Hn[:, :, :]), g.Qs[0:P, :, :, :].rearrange("p t s d -> p (t s d)")
        table = g.kv1.rearrange("(t p r) d -> p t (r d)", p=P, r=NR)
        n_loads = 3 * (NTY + 1) + 2 * H

        def turns(eng, body):
            body(0, True, False)
            with eng.Fori(1, NIT - 1) as i:
                body(i, False, False)
            body(NIT - 1, False, True)

        def rel_out(s, m):
            return T[:, s, :].rearrange("p (r c h e) -> p c h r e", r=NR, c=2, h=H)[:, m // H, m % H]

        def rel_in(m):
            return psR[m % 4][0:P, 0:NR * DK].rearrange("p (r e) -> p r e", r=NR)

        @block.sync
        def _(sp):
            for n, (W, b) in enumerate(((Wq, bq), (Wk, bk), (Wv, bv))):
                for ty_ in range(NTY):
                    sp.dma_start(Wt[:, :, ty_, n * D:(n + 1) * D], W[ty_].rearrange("(c k) n -> k c n", c=KC)) \
                        .then_inc(loaded, 16)
                sp.dma_start(bt[:, n * D:(n + 1) * D], b).then_inc(loaded, 16)
            for n, rel in enumerate((rel_att, rel_msg)):
                for h in range(H):
                    sp.dma_start(R[(h % 2) * DK:(h % 2 + 1) * DK, n, h // 2, :].rearrange("d (r e) -> d r e", r=NR),
                                 rel[:, h, :, :].rearrange("r d e -> d r e")).then_inc(loaded, 16)

            with sp.Fori(0, NIT) as i:
                for u in range(NU):
                    k = i * NU + u
                    sp.wait_ge(rel_by_dve, 4 * k + 4)
                    sp.wait_ge(rel_by_act, 4 * k + 4)
                    sp.dma_start(table[:, bass.ds(k, 1), :], T[:, u % 2, :].rearrange("p (a n) -> p a n", a=1)) \
                        .then_inc(stored[u], 16)
            for u in range(NU):
                sp.wait_ge(stored[u], 16 * NIT)

        def table_slot_free(eng, i, u, first):
            if u >= 2:
                eng.wait_ge(stored[u - 2], 16 * (i + 1))
            elif not first:
                eng.wait_ge(stored[(u - back(u)) % NU], 16 * i)

        @block.gpsimd
        def _(pool):
            def stage(i, u, first):
                k = i * NU + u
                if not first or u >= 2:
                    pool.wait_ge(product_ready, k - back(u) + 1)
                nc.gpsimd.tensor_copy(types[:, u % 2, :], ty.hot[:, bass.ds(k * P, P)])
                nc.gpsimd.tensor_copy(hs[:, u % 2, :], tile(H2, k, D)).then_inc(hs_ready, 1)

            def body(i, first, last):
                for u in range(NU):
                    k = i * NU + u
                    if u < NU - 1:
                        stage(i, u + 1, first)
                    elif not last:
                        stage(i + 1, 0, False)
                    pool.wait_ge(q1_ready, k + 1)
                    nc.gpsimd.tensor_tensor(rest[:, u % 2, :], qkv[:, u % 2, 0:D], Q2[:, bass.ds(k * 3 * D, D)],
                                            ALU.subtract).then_inc(rest_ready, 1)
                    pool.wait_ge(q2_ready, k + 1)
                    nc.gpsimd.tensor_tensor(Q2[:, bass.ds(k * 3 * D + 2 * D, D)], rest[:, u % 2, :],
                                            Q2[:, bass.ds(k * 3 * D + D, D)], ALU.subtract).then_inc(q3_ready, 1)

            stage(0, 0, True)
            turns(pool, body)

        @block.tensor
        def _(pe):
            pe.wait_ge(loaded, 16 * n_loads)

            def turn_input(i, u, first):
                k = i * NU + u
                if not (first and u == 0):
                    pe.wait_ge(hm_ready, k)
                pe.wait_ge(hs_ready, k + 1)
                for c in range(KC):
                    ins = nc.tensor.transpose(psH[:, c * P:(c + 1) * P], hs[:, u % 2, c * 128:(c + 1) * 128], g.eye(P))
                ins.then_inc(hT_in_psum, 1)

            def relate(k, s, start):
                pe.wait_ge(kvT_ready, k + 1)
                for m in range(2 * H):
                    h = m % H
                    if not start or m >= 4:
                        (pe.wait_ge(rel_by_dve, 4 * k + m // 2 - 1) if m % 2 == 0 else
                         pe.wait_ge(rel_by_act, 4 * k + m // 2 - 1))
                    rows = slice((h % 2) * DK, (h % 2 + 1) * DK)
                    col = (m // H) * 2 + h // 2
                    nc.tensor.matmul(psR[m % 4][0:P, 0:NR * DK], kvT[rows, s, col * P:(col + 1) * P],
                                     R[rows, m // H, h // 2, :], start=True, stop=True).then_inc(rel_in_psum, 1)

            def body(i, first, last):
                for u in range(NU):
                    k = i * NU + u
                    pe.wait_ge(hm_ready, k + 1)
                    if not (first and u == 0):
                        pe.wait_ge(qkv_ready, k)
                    for b in range(2):
                        cols = slice(b * HALF, (b + 1) * HALF)
                        nc.tensor.matmul(psM[b][0:P, 0:HALF], types[:, u % 2, :], bt[:, cols],
                                         start=True, stop=False)
                        for n in range(NTY):
                            for c in range(KC):
                                ins = nc.tensor.matmul(psM[b][0:P, 0:HALF], hm[:, u % 2, n, c * P:(c + 1) * P],
                                                       Wt[:, c, n, cols], start=False,
                                                       stop=(n == NTY - 1 and c == KC - 1))
                    ins.then_inc(product_ready, 1)
                    if not (first and u == 0):
                        relate(k - 1, 1 if u in (2, 4) else 0, first and u == 1)
                    if u < NU - 1:
                        turn_input(i, u + 1, first)
                    elif not last:
                        turn_input(i + 1, 0, False)
                    pe.wait_ge(qkv_ready, k + 1)
                    if not (first and u == 0):
                        pe.wait_ge(kvT_ready, k)
                    for c in range(4):
                        ins = nc.tensor.transpose(psK[:, c * P:(c + 1) * P],
                                                  qkv[:, u % 2, D + c * 128:D + (c + 1) * 128], g.eye(P))
                    ins.then_inc(kvT_in_psum, 1)

            turn_input(0, 0, True)
            turns(pe, body)
            relate(NT - 1, 0, False)

        @block.vector
        def _(dve):
            def mask(i, u, first):
                k = i * NU + u
                dve.wait_ge(hT_in_psum, k + 1)
                if not first or u >= 2:
                    dve.wait_ge(product_ready, k - back(u) + 1)
                row = ty.row[:, bass.ds(k * P, P)].unsqueeze(1).to_broadcast([128, KC, P])
                for n in range(NTY):
                    ins = nc.vector.scalar_tensor_tensor(hm[:, u % 2, n, :].rearrange("p (c n) -> p c n", c=KC), row,
                                                         float(n), psH[:, 0:KC * P].rearrange("p (c n) -> p c n", c=KC),
                                                         ALU.is_equal, ALU.mult)
                ins.then_inc(hm_ready, 1)

            def related(i, u, first):
                k = i * NU + u
                table_slot_free(dve, i, u, first)
                for j in range(4):
                    dve.wait_ge(rel_in_psum, 8 * k + 2 * j + 1)
                    nc.vector.tensor_copy(rel_out(u % 2, 2 * j), rel_in(2 * j)).then_inc(rel_by_dve, 1)

            def body(i, first, last):
                for u in range(NU):
                    k = i * NU + u
                    if u > 0:
                        related(i, u - 1, first)
                    elif not first:
                        related(i - 1, NU - 1, False)
                    if u < NU - 1:
                        mask(i, u + 1, first)
                    elif not last:
                        mask(i + 1, 0, False)
                    dve.wait_ge(kvT_in_psum, k + 1)
                    if not first or u >= 2:
                        dve.wait_ge(rel_in_psum, 8 * (k - back(u)) + 8)
                    nc.vector.tensor_copy(kvT[:, u % 2, :], psK[:, 0:4 * P]).then_inc(kvT_ready, 1)

            mask(0, 0, True)
            turns(dve, body)
            related(NIT - 1, NU - 1, False)

        @block.scalar
        def _(act):
            def related(i, u, first):
                k = i * NU + u
                table_slot_free(act, i, u, first)
                for j in range(4):
                    act.wait_ge(rel_in_psum, 8 * k + 2 * j + 2)
                    nc.scalar.copy(rel_out(u % 2, 2 * j + 1), rel_in(2 * j + 1)).then_inc(rel_by_act, 1)

            def body(i, first, last):
                for u in range(NU):
                    k = i * NU + u
                    act.wait_ge(product_ready, k + 1)
                    if not first or u >= 2:
                        act.wait_ge(q3_ready, k - back(u) + 1)
                        act.wait_ge(kvT_in_psum, k - back(u) + 1)
                    for b in range(2):
                        ins = nc.scalar.copy(qkv[:, u % 2, b * HALF:(b + 1) * HALF], psM[b][0:P, 0:HALF])
                    ins.then_inc(qkv_ready, 1)
                    act.wait_ge(qkv_ready, k + 1)
                    nc.scalar.copy(Q2[:, bass.ds(k * 3 * D, D)], qkv[:, u % 2, 0:D]).then_inc(q1_ready, 1)
                    if u > 0:
                        related(i, u - 1, first)
                    elif not first:
                        related(i - 1, NU - 1, False)
                    act.wait_ge(rest_ready, k + 1)
                    nc.scalar.copy(Q2[:, bass.ds(k * 3 * D + D, D)], rest[:, u % 2, :]).then_inc(q2_ready, 1)

            turns(act, body)
            related(NIT - 1, NU - 1, False)


def layer1_output_phase(nc, g, ty, Wa, ba, skip, ln_g, ln_b, out):
    with ExitStack() as ctx:
        sb = lambda name, shape, dt: sbuf(ctx, nc, "f_" + name, shape, dt)
        sem = semaphores(ctx, nc, "f_")
        KC = D // 128
        Wt = sb("W", [128, KC, NTY, D], FP)
        bt = sb("b", [NTY, D], FP)
        gb = sb("gb", [NTY, 2 * D], FP)
        gate = sb("gate", [NTY, 1], FP)
        some = sb("some", [P, NT, NR], FP)
        nrel = sb("nrel", [P, NT], FP)
        rn = sb("rn", [P, NT], FP)
        has = sb("has", [P, NT], FP)
        alone = sb("alone", [P, NT], FP)
        alpha = sb("alpha", [P, NT], FP)
        keep = sb("keep", [P, NT], FP)
        types = sb("types", [NTY, NU, P], FP)
        agg = sb("agg", [P, NU, D], FP)
        free = g.Qs[:, :, :, :].rearrange("p t s d -> p (t s d)").bitcast(FP)
        n_am = NU * NTY * KC * P
        am = free[:, 0:n_am].rearrange("p (u n m) -> p u n m", u=NU, n=NTY)
        hk = sb("hk", [P, NU, D], FP)
        hx = sb("hx", [P, NU, D], FP)
        y = free[0:P, n_am:n_am + NU * D].rearrange("p (u d) -> p u d", u=NU)
        z = free[0:P, n_am + NU * D:n_am + 2 * NU * D].rearrange("p (u d) -> p u d", u=NU)
        stats = sb("stats", [P, NU, 6], FP)
        mv = sb("mv", [P, NU, 2], FP)
        std = sb("std", [P, NU], FP)
        rstd = sb("rstd", [P, NU], FP)
        psT = [ctx.enter_context(nc.psum_tensor(f"f_psT{s}", [128, 512], FP)) for s in range(2)]
        psO = [ctx.enter_context(nc.psum_tensor(f"f_psO{s}", [128, 512], FP)) for s in range(2)]
        psG = [ctx.enter_context(nc.psum_tensor(f"f_psG{s}", [128, 512], FP)) for s in range(2)]
        psA = ctx.enter_context(nc.psum_tensor("f_psA", [128, 512], FP))
        loaded = sem("loaded")
        skip_exp = sem("skip_exp")
        gate_ready = sem("gate_ready")
        alpha_in_psum = sem("alpha_in_psum")
        scalars_ready = sem("scalars_ready")
        types_ready = sem("types_ready")
        agg_ready = sem("agg_ready")
        hk_ready = sem("hk_ready")
        hx_ready = sem("hx_ready")
        aggT_in_psum = sem("aggT_in_psum")
        am_ready = sem("am_ready")
        out_in_psum = sem("out_in_psum")
        gb_in_psum = sem("gb_in_psum")
        y_ready = sem("y_ready")
        var_ready = sem("var_ready")
        std_ready = sem("std_ready")
        scaled = sem("scaled")
        z_ready = sem("z_ready")
        result_ready = sem("result_ready")
        stored = sem("stored")
        waited = sem("waited")
        start_own = sem("start_own")
        dve_own = sem("dve_own")
        block = ctx.enter_context(nc.Block())
        X2, H2, A2 = flat(g.X1[:, :, :]), flat(g.Hn[:, :, :]), flat(g.acc[:, :, :])
        outt = out.rearrange("(t p) d -> p t d", p=P)

        @block.sync
        def _(sp):
            for n in range(NTY):
                sp.dma_start(Wt[:, :, n, :], Wa[n].rearrange("(c k) n -> k c n", c=KC)).then_inc(loaded, 16)
            sp.dma_start(bt[:, :], ba).then_inc(loaded, 16)
            sp.dma_start(gb[:, 0:D], ln_g).then_inc(loaded, 16)
            sp.dma_start(gb[:, D:2 * D], ln_b).then_inc(loaded, 16)
            sp.dma_start(gate[:, :], skip.rearrange("(n a) -> n a", a=1)).then_inc(loaded, 16)

            with sp.Fori(0, NIT) as i:
                sp.wait_ge(result_ready, i * NU + NU)
                sp.dma_start(outt[:, bass.ds(i * NU, NU), :], z[:, :, :]).then_inc(stored, 16)
            sp.wait_ge(stored, 16 * NIT)

        @block.gpsimd
        def _(pool):
            def turn(i, first):
                for u in range(NU):
                    k = i * NU + u
                    if not first:
                        pool.wait_ge(gb_in_psum, k - NU + 1)
                    nc.gpsimd.tensor_copy(types[:, u, :], ty.hot[:, bass.ds(k * P, P)]).then_inc(types_ready, 1)

            loop(pool, NIT, turn)

        @block.scalar
        def _(act):
            act.wait_ge(loaded, 16 * (NTY + 4))
            nc.scalar.activation(gate[:, :], gate[:, :], ACT.Exp, scale=-1.0).then_inc(skip_exp, 1)
            act.wait_ge(scalars_ready, 1)

            def turn(i, first):
                for u in range(NU):
                    k = i * NU + u
                    if not first:
                        act.wait_ge(aggT_in_psum, k - NU + 1)
                        act.wait_ge(y_ready, k - NU + 1)
                    nc.scalar.activation(agg[:, u, :], A2[:, bass.ds(k * ACCW, D)], ACT.Copy,
                                         scale=rn[:, bass.ds(k, 1)]).then_inc(agg_ready, 1)
                    nc.scalar.activation(hk[:, u, :], tile(H2, k, D), ACT.Copy, scale=keep[:, bass.ds(k, 1)]) \
                        .then_inc(hk_ready, 1)
                act.wait_ge(var_ready, i + 1)
                nc.scalar.activation(std[:, :], mv[:, :, 1], ACT.Sqrt, bias=g.eps[0:P, :]).then_inc(std_ready, 1)

            loop(act, NIT, turn)

        @block.tensor
        def _(pe):
            pe.wait_ge(gate_ready, 1)
            for k in range(NT):
                ins = nc.tensor.matmul(psA[0:P, k:k + 1], ty.hot[:, k * P:(k + 1) * P], gate[:, :], start=True, stop=True)
            ins.then_inc(alpha_in_psum, 1)

            def turn(i, first):
                for u in range(NU):
                    k = i * NU + u
                    pe.wait_ge(agg_ready, k + 1)
                    if not first or u >= 2:
                        pe.wait_ge(am_ready, k - back(u) + 1)
                    for c in range(KC):
                        ins = nc.tensor.transpose(psT[u % 2][:, c * P:(c + 1) * P], agg[:, u, c * 128:(c + 1) * 128],
                                                  g.eye(P))
                    ins.then_inc(aggT_in_psum, 1)
                for u in range(NU):
                    k = i * NU + u
                    pe.wait_ge(am_ready, k + 1)
                    if not first or u >= 2:
                        pe.wait_ge(y_ready, k - back(u) + 1)
                    pe.wait_ge(types_ready, k + 1)
                    nc.tensor.matmul(psO[u % 2][0:P, 0:D], types[:, u, :], bt[:, :], start=True, stop=False)
                    for n in range(NTY):
                        for c in range(KC):
                            ins = nc.tensor.matmul(psO[u % 2][0:P, 0:D], am[:, u, n, c * P:(c + 1) * P], Wt[:, c, n, :],
                                                   start=False, stop=(n == NTY - 1 and c == KC - 1))
                    ins.then_inc(out_in_psum, 1)
                for u in range(NU):
                    k = i * NU + u
                    if not first or u >= 2:
                        pe.wait_ge(z_ready, k - back(u) + 1)
                    nc.tensor.matmul(psG[u % 2][0:P, :], types[:, u, :], gb[:, :], start=True, stop=True) \
                        .then_inc(gb_in_psum, 1)

            loop(pe, NIT, turn)

        @block.vector
        def _(dve):
            s = Tally(dve, start_own)
            t = Tally(dve, dve_own)
            dve.wait_ge(skip_exp, 1)
            s.done(nc.vector.tensor_scalar(gate[:, :], gate[:, :], 1.0, None, ALU.add))
            nc.vector.reciprocal(gate[:, :], gate[:, :]).then_inc(gate_ready, 1)
            s.done(nc.vector.tensor_scalar(some[:, :, :], g.cnt[:, :, :], 0.5, None, ALU.is_ge))
            s.done(nc.vector.reduce_sum(nrel[:, :], some[:, :, :], axis=AX.X))
            s.done(nc.vector.tensor_scalar(has[:, :], nrel[:, :], 0.5, None, ALU.is_ge))
            s.done(nc.vector.tensor_scalar(alone[:, :], has[:, :], -1.0, 1.0, ALU.mult, ALU.add))
            s.done(nc.vector.tensor_scalar(nrel[:, :], nrel[:, :], 1.0, None, ALU.max))
            s.done(nc.vector.reciprocal(rn[:, :], nrel[:, :]))
            dve.wait_ge(alpha_in_psum, 1)
            s.done(nc.vector.tensor_copy(alpha[:, :], psA[0:P, 0:NT]))
            nc.vector.tensor_scalar(keep[:, :], alpha[:, :], -1.0, 1.0, ALU.mult, ALU.add).then_inc(scalars_ready, 1)

            def turn(i, first):
                t.turn(i, 3)
                for u in range(NU):
                    k = i * NU + u
                    dve.wait_ge(aggT_in_psum, k + 1)
                    if not first:
                        dve.wait_ge(out_in_psum, k - NU + 1)
                    row = ty.row[:, bass.ds(k * P, P)].unsqueeze(1).to_broadcast([128, KC, P])
                    for n in range(NTY):
                        ins = nc.vector.scalar_tensor_tensor(am[:, u, n, :].rearrange("p (c n) -> p c n", c=KC), row,
                                                             float(n),
                                                             psT[u % 2][:, 0:KC * P].rearrange("p (c n) -> p c n", c=KC),
                                                             ALU.is_equal, ALU.mult)
                    ins.then_inc(am_ready, 1)
                for u in range(NU):
                    k = i * NU + u
                    dve.wait_ge(out_in_psum, k + 1)
                    dve.wait_ge(hk_ready, k + 1)
                    nc.vector.scalar_tensor_tensor(y[:, u, :], psO[u % 2][0:P, 0:D], alpha[:, bass.ds(k, 1)], hk[:, u, :],
                                                   ALU.mult, ALU.add).then_inc(y_ready, 1)
                for u in range(NU):
                    k = i * NU + u
                    nc.vector.scalar_tensor_tensor(hx[:, u, :], tile(H2, k, D), alone[:, bass.ds(k, 1)], tile(X2, k, D),
                                                   ALU.mult, ALU.add).then_inc(hx_ready, 1)
                dve.wait_ge(y_ready, i * NU + NU)
                dve.sem_inc(waited, 1)
                for u in range(NU):
                    ins = nc.vector.bn_stats(stats[:, u, :], y[:, u, :])
                t.done(ins)
                dve.sem_inc(waited, 1)
                for u in range(NU):
                    ins = nc.vector.bn_aggr(mv[:, u, :], stats[:, u, :])
                ins.then_inc(var_ready, 1)
                dve.wait_ge(std_ready, i + 1)
                t.done(nc.vector.reciprocal(rstd[:, :], std[:, :]))
                for u in range(NU):
                    ins = nc.vector.tensor_scalar(y[:, u, :], y[:, u, :], mv[:, u, 0:1], rstd[:, u:u + 1],
                                                  ALU.subtract, ALU.mult)
                t.done(ins)
                if not first:
                    dve.wait_ge(stored, 16 * i)
                for u in range(NU):
                    k = i * NU + u
                    dve.wait_ge(gb_in_psum, k + 1)
                    nc.vector.tensor_tensor(y[:, u, :], y[:, u, :], psG[u % 2][0:P, 0:D], ALU.mult).then_inc(scaled, 1)
                    dve.wait_ge(scaled, k + 1)
                    nc.vector.tensor_tensor(z[:, u, :], y[:, u, :], psG[u % 2][0:P, D:2 * D], ALU.add).then_inc(z_ready, 1)
                    dve.wait_ge(z_ready, k + 1)
                    dve.wait_ge(hx_ready, k + 1)
                    nc.vector.scalar_tensor_tensor(z[:, u, :], z[:, u, :], has[:, bass.ds(k, 1)], hx[:, u, :],
                                                   ALU.mult, ALU.add).then_inc(result_ready, 1)

            loop(dve, NIT, turn)


def gnn(nc, x, src, dst, et6, et64, node_type, query, Wq0, bq0, Wk0, bk0, Wv0, bv0, rel_w, Wo, bo, gamma, beta,
        Wk1, bk1, Wq1, bq1, Wv1, bv1, Wa, ba, rel_pri, rel_att, rel_msg, skip, ln_g, ln_b, out):
    with ExitStack() as ctx:
        g = Persistent(ctx, nc)
        setup_phase(nc, g, x, src, dst, et6, et64)
        project_phase(nc, g, query, Wq0, bq0, Wk0, bk0, Wv0, bv0)
        with ExitStack() as edges:
            g.edge_tensors(edges, nc, 0)
            score_phase(nc, g, 0, g.kv0, rel_w)
            softmax_phase(nc, g, 0, None)
            aggregate_phase(nc, g, 0)
        ty = Types(ctx, nc)
        layer0_output_phase(nc, g, ty, Wo, bo, gamma, beta, node_type)
        typed_project_phase(nc, g, ty, Wk1, bk1, Wq1, bq1, Wv1, bv1, rel_att, rel_msg)
        with ExitStack() as edges:
            g.edge_tensors(edges, nc, 1)
            score_phase(nc, g, 1, g.kv1, None)
            softmax_phase(nc, g, 1, rel_pri)
            aggregate_phase(nc, g, 1)
        layer1_output_phase(nc, g, ty, Wa, ba, skip, ln_g, ln_b, out)


_INS = ['x', 'src', 'dst', 'edge_type_6', 'edge_type_64', 'node_type_3', 'L0_gnn_query_emb', 'L0_gnn_Wq', 'L0_gnn_bq',
        'L0_gnn_Wk', 'L0_gnn_bk', 'L0_gnn_Wv', 'L0_gnn_bv', 'L0_gnn_rel_w', 'L0_gnn_Wo', 'L0_gnn_bo', 'L0_gnn_gamma',
        'L0_gnn_beta', 'L1_gnn_Wk', 'L1_gnn_bk', 'L1_gnn_Wq', 'L1_gnn_bq', 'L1_gnn_Wv', 'L1_gnn_bv', 'L1_gnn_Wa',
        'L1_gnn_ba', 'L1_gnn_rel_pri', 'L1_gnn_rel_att', 'L1_gnn_rel_msg', 'L1_gnn_skip', 'L1_gnn_ln_g', 'L1_gnn_ln_b']


def kernel(**inputs):
    import numpy as _np
    import concourse.bacc as _bacc
    from concourse import mybir as _mybir
    from concourse.bass_utils import run_bass_kernel_spmd as _run

    nc = _bacc.Bacc("TRN2", target_bir_lowering=False, num_devices=1)
    arrays, args = {}, []
    for name in _INS:
        a = _np.ascontiguousarray(inputs[name])
        arrays[f"in_{name}_dram"] = a
        args.append(nc.dram_tensor(f"in_{name}_dram", a.shape, _mybir.dt.from_np(a.dtype), kind="ExternalInput").ap())
    args.append(nc.dram_tensor("out_0_dram", (N, D), _mybir.dt.float32, kind="ExternalOutput").ap())
    gnn(nc, *args)
    r = _run(nc, [arrays], core_ids=[0])
    return r.results[0]["out_0_dram"]
```

```python
import concourse.bass as bass
from concourse import mybir
from contextlib import ExitStack

FP = mybir.dt.float32
BF = mybir.dt.bfloat16
I32 = mybir.dt.int32
ALU = mybir.AluOpType
ACT = mybir.ActivationFunctionType
AX = mybir.AxisListType

N = 3125
E = 50000
D = 256
H = 4
DK = D // H
NR = 6
NREL = 64
NTY = 3
P = 125
NT = N // P
EW = 256
NROW = -(-E // EW)
STEPS = NROW + NT - 1
Q = STEPS // 2
SLOTS = 2 * EW
U = 4
ITERS = STEPS // U
RING = 10
HOTS = 5
RING_BIT = 13
LAG = 2
C = H * NR
ACCW = D + NR
BIG = 1.0e30
EPS = 1e-05
FAR = 4000
assert FAR >= N + P and NT * P == N and STEPS % 2 == 0 and ITERS * U == STEPS and Q <= 128
assert STEPS % RING == 0 and RING % HOTS == 0 and LAG < HOTS
assert NT * (D + NR) < 2 ** RING_BIT and RING_BIT + RING < 24


class Tally:

    def __init__(self, eng, sem):
        self.eng, self.sem, self.n, self.at = eng, sem, 0, 0

    def done(self, ins):
        self.n += 1
        ins.then_inc(self.sem, 1)
        self.eng.wait_ge(self.sem, self.at + self.n)

    def turn(self, i, each):
        self.at, self.n = i * each, 0


def sbuf(ctx, nc, name, shape, dt):
    return ctx.enter_context(nc.sbuf_tensor(name, shape, dt))


def semaphores(ctx, nc, prefix):
    made = []

    def sem(name):
        made.append(nc.alloc_semaphore(prefix + name))
        return made[-1]

    def give_back():
        nc.clear_and_free_semaphores(made)
        nc.all_engine_barrier()

    ctx.callback(give_back)
    return sem


class Persistent:

    def __init__(self, ctx, nc):
        self.ident = sbuf(ctx, nc, "ident_wide", [128, 132], FP)
        self.part = sbuf(ctx, nc, "part", [128, 1], FP)
        self.negpart = sbuf(ctx, nc, "negpart", [128, 1], FP)
        self.iota = sbuf(ctx, nc, "iota", [128, 2 * P], FP)
        self.ones = sbuf(ctx, nc, "ones", [128, 128], FP)
        self.eps = sbuf(ctx, nc, "eps", [128, 1], FP)
        self.tile_q = sbuf(ctx, nc, "tile_q", [1, STEPS], I32)
        self.tiles_acc = sbuf(ctx, nc, "tiles_acc", [1, STEPS // RING + 1], I32)
        self.idx0 = sbuf(ctx, nc, "idx0", [128, STEPS, 2], I32)
        self.idx1 = sbuf(ctx, nc, "idx1", [128, STEPS, 2], I32)
        self.dcol = sbuf(ctx, nc, "dcol", [128, STEPS, 2], FP)
        self.ecol = sbuf(ctx, nc, "ecol", [128, STEPS, 2], FP)
        self.same = sbuf(ctx, nc, "same", [Q, SLOTS], BF)
        self.same_b = sbuf(ctx, nc, "same_b", [Q, SLOTS], BF)
        self.next_b = sbuf(ctx, nc, "next_b", [Q, SLOTS], BF)
        self.next_in = sbuf(ctx, nc, "next_in", [Q, SLOTS], BF)
        self.next_out = sbuf(ctx, nc, "next_out", [Q, SLOTS], BF)
        self.pm = sbuf(ctx, nc, "pm", [Q, SLOTS], BF)
        self.sm = sbuf(ctx, nc, "sm", [Q, SLOTS], BF)
        self.pm_b = sbuf(ctx, nc, "pm_b", [Q, SLOTS], BF)
        self.sm_b = sbuf(ctx, nc, "sm_b", [Q, SLOTS], BF)
        self.etm = sbuf(ctx, nc, "etm", [Q, NR * SLOTS], BF)
        self.whole = sbuf(ctx, nc, "whole", [32, 4, Q], FP)
        self.Hn = sbuf(ctx, nc, "Hn", [P, NT, D], FP)
        self.X1 = sbuf(ctx, nc, "X1", [P, NT, D], FP)
        self.Qs = sbuf(ctx, nc, "Qs", [128, NT, 3, D], BF)
        self.acc = sbuf(ctx, nc, "acc", [P, NT, ACCW], FP)
        self.cnt = sbuf(ctx, nc, "cnt", [P, NT, NR], FP)
        dram = lambda name, shape, dt: nc.dram_tensor(name, shape, dt, kind="Internal").ap()
        self.edges = dram("edges", [NROW, 4, EW], I32)
        self.meta = dram("meta", [STEPS, 2, EW], BF)
        self.kv0 = dram("kv0", [N, 2 * D], FP)
        self.kv1 = dram("kv1", [N * NR, 2 * D], FP)
        self.vst = dram("vst", [STEPS, 128, 2, D], FP)

    def edge_tensors(self, ctx, nc, layer):
        self.S = sbuf(ctx, nc, f"S{layer}", [128, STEPS, 2, H], FP)
        self.W = sbuf(ctx, nc, f"W{layer}", [128, STEPS, 2, H], FP)

    def eye(self, n):
        return self.ident[0:n, 1:1 + n]


NU = 5
NIT = NT // NU


def back(u):
    return {0: 1, 1: 3}.get(u, 2)


def flat(ap):
    return ap.rearrange("p a b -> p (a b)")


def tile(t2d, t, width):
    return t2d[:, bass.ds(t * width, width)]


def loop(eng, count, body):
    body(0, True)
    with eng.Fori(1, count) as i:
        body(i, False)


def row_bc(vec, n):
    return vec.rearrange("(a d) -> a d", a=1).partition_broadcast(n)


def order_phase(nc, g, src, dst, et6, et64):
    with ExitStack() as ctx:
        sb = lambda name, shape, dt: sbuf(ctx, nc, "r_" + name, shape, dt)
        sem = semaphores(ctx, nc, "r_")
        W2 = 400
        PE_ = E // W2
        QF = NROW // 2
        CROWS = 7
        CH, CHUNKS = CROWS * EW, NROW // CROWS
        GRID = 2048.0
        JB = 4
        assert PE_ * W2 == E and CHUNKS * CROWS == NROW and NROW % 2 == 0 and CH < GRID and FAR <= 4096
        padi = sb("padi", [1, 2, EW], I32)
        here = sb("here", [PE_, W2], I32)
        after = sb("after", [PE_, W2], I32)
        falls = sb("falls", [PE_, W2], FP)
        fall = sb("fall", [PE_, 1], FP)
        ones = sb("ones", [PE_, 1], FP)
        unsorted = sb("unsorted", [1, 1], I32)
        fields = sb("fields", [QF, 2, 4, EW], I32)
        fieldsT = sb("fieldsT", [QF, 4, SLOTS], I32)
        dstf = sb("dstf", [QF, SLOTS], FP)
        chunk = sb("chunk", [QF, CROWS, EW], I32)
        keys = sb("keys", [QF, CH], FP)
        place = sb("place", [QF, CH], FP)
        ahead = sb("ahead", [QF, SLOTS], FP)
        thr = sb("thr", [QF, SLOTS], FP)
        less = g.Qs[0:QF, :, :, :].rearrange("p t s d -> p (t s d)").bitcast(FP)[:, 0:JB * CH] \
            .rearrange("p (j e) -> p j e", j=JB)
        count = sb("count", [QF, JB], FP)
        rank = sb("rank", [QF, SLOTS], FP)
        row = sb("row", [QF, SLOTS], FP)
        where = sb("where", [QF, 4, SLOTS], I32)
        where1 = sb("where1", [QF, 4], I32)
        value1 = sb("value1", [QF, 4], I32)
        psF = ctx.enter_context(nc.psum_tensor("r_psF", [128, 512], FP))
        pad_ready = sem("pad_ready")
        after_padded = sem("after_padded")
        dst_loaded = sem("dst_loaded")
        edges_stored = sem("edges_stored")
        fall_ready = sem("fall_ready")
        falls_counted = sem("falls_counted")
        flag_ready = sem("flag_ready")
        fields_loaded = sem("fields_loaded")
        chunk_loaded = sem("chunk_loaded")
        places_ready = sem("places_ready")
        chunk_used = sem("chunk_used")
        where_ready = sem("where_ready")
        picked = sem("picked")
        scattered = sem("scattered")
        waited = sem("waited")
        dve_own = sem("dve_own")
        turn_own = sem("turn_own")
        rank_own = sem("rank_own")
        end_own = sem("end_own")
        block = ctx.enter_context(nc.Block())
        full = NROW - 1
        rest = E - full * EW
        where2, fields2 = where[:, :, :], fields[:, :, :, :]

        @block.sync
        def _(sp):
            sp.dma_start(here[:, :], dst.rearrange("(p w) -> p w", w=W2)).then_inc(dst_loaded, 16)
            sp.wait_ge(after_padded, 1)
            sp.dma_start(after[0:PE_ - 1, :], dst[1:1 + (PE_ - 1) * W2].rearrange("(p w) -> p w", w=W2)) \
                .then_inc(dst_loaded, 16)
            sp.dma_start(after[PE_ - 1:PE_, 0:W2 - 1], dst[1 + (PE_ - 1) * W2:E].rearrange("(p w) -> p w", p=1)) \
                .then_inc(dst_loaded, 16)
            for a, arr in enumerate((dst, src, et64, et6)):
                sp.dma_start(g.edges[0:full, a, :], arr[0:full * EW].rearrange("(r e) -> r e", e=EW)).then_inc(edges_stored, 16)
                sp.dma_start(g.edges[full:NROW, a, 0:rest], arr[full * EW:E].rearrange("(r e) -> r e", r=1)) \
                    .then_inc(edges_stored, 16)
            sp.wait_ge(pad_ready, 1)
            sp.dma_start(g.edges[full:NROW, 0, rest:EW], padi[0:1, 0, rest:EW]).then_inc(edges_stored, 16)
            sp.dma_start(g.edges[full:NROW, 1:3, rest:EW],
                         padi[0:1, 1:2, rest:EW].to_broadcast([1, 2, EW - rest])).then_inc(edges_stored, 16)
            sp.dma_start(g.edges[full:NROW, 3, rest:EW], padi[0:1, 1, rest:EW]).then_inc(edges_stored, 16)
            sp.wait_ge(edges_stored, 16 * 11)
            sp.wait_ge(flag_ready, 1)
            sort = sp.value_load(unsorted[0:1, 0:1], min_val=0, max_val=1)
            with sp.If(sort > 0):
                sp.dma_start(fields[:, :, :, :], g.edges.rearrange("(q b) a e -> q b a e", b=2)).then_inc(fields_loaded, 16)

                def load(c, first):
                    if not first:
                        sp.wait_ge(chunk_used, c)
                    sp.dma_start(chunk[:, :, :], g.edges[bass.ds(c * CROWS, CROWS), 0, :].partition_broadcast(QF)) \
                        .then_inc(chunk_loaded, 16)

                loop(sp, CHUNKS, load)

        @block.tensor
        def _(pe):
            pe.wait_ge(fall_ready, 1)
            nc.tensor.matmul(psF[0:1, 0:1], fall[:, :], ones[:, :], start=True, stop=True).then_inc(falls_counted, 1)

        @block.gpsimd
        def _(pool):
            pool.wait_ge(flag_ready, 1)
            sort = pool.value_load(unsorted[0:1, 0:1], min_val=0, max_val=1)
            with pool.If(sort > 0):
                nc.gpsimd.iota(place[:, :], pattern=[[1, CH]], base=0, channel_multiplier=0,
                               allow_small_or_imprecise_dtypes=True)
                nc.gpsimd.iota(ahead[:, :], pattern=[[1, SLOTS]], base=0, channel_multiplier=SLOTS,
                               allow_small_or_imprecise_dtypes=True).then_inc(places_ready, 1)
                pool.wait_ge(where_ready, 1)

                def scatter(j, first):
                    if not first:
                        pool.wait_ge(scattered, 64 * j)
                    nc.gpsimd.tensor_copy(where1[:, :], where2[:, :, bass.ds(j, 1)].rearrange("q a e -> q (a e)")) \
                        .then_inc(picked, 1)
                    nc.gpsimd.tensor_copy(value1[:, :], column(j)).then_inc(picked, 1)
                    pool.wait_ge(picked, 2 * j + 2)
                    pool.sem_inc(waited, 1)
                    for a in range(4):
                        nc.gpsimd.indirect_dma_start(
                            out=g.edges.rearrange("r a (e o) -> (r a e) o", o=1),
                            out_offset=bass.IndirectOffsetOnAxis(ap=where1[:, a:a + 1], axis=0),
                            in_=value1[:, a:a + 1], in_offset=None).then_inc(scattered, 16)

                def column(j):
                    return fieldsT[:, :, bass.ds(j, 1)].rearrange("q a e -> q (a e)")

                loop(pool, SLOTS, scatter)
                pool.wait_ge(scattered, 64 * SLOTS)

        @block.vector
        def _(dve):
            t = Tally(dve, dve_own)
            t.done(nc.vector.memset(after[:, :], FAR))
            nc.vector.memset(ones[:, :], 1.0).then_inc(after_padded, 1)
            t.done(nc.vector.memset(padi[:, 0, :], FAR))
            nc.vector.memset(padi[:, 1, :], 0).then_inc(pad_ready, 1)
            dve.wait_ge(dst_loaded, 48)
            t.done(nc.vector.tensor_tensor(falls[:, :], here[:, :], after[:, :], ALU.is_gt))
            nc.vector.reduce_sum(fall[:, :], falls[:, :], axis=AX.X).then_inc(fall_ready, 1)
            dve.wait_ge(falls_counted, 1)
            nc.vector.tensor_scalar(unsorted[:, :], psF[0:1, 0:1], 1.0, None, ALU.min).then_inc(flag_ready, 1)
            dve.wait_ge(flag_ready, 1)
            sort = dve.value_load(unsorted[0:1, 0:1], min_val=0, max_val=1)
            with dve.If(sort > 0):
                dve.wait_ge(fields_loaded, 16)
                dve.wait_ge(places_ready, 1)
                e = Tally(dve, end_own)
                for b in range(2):
                    ins = nc.vector.tensor_copy(fieldsT[:, :, b * EW:(b + 1) * EW], fields2[:, b, :, :])
                e.done(ins)
                e.done(nc.vector.tensor_copy(dstf[:, :], fieldsT[:, 0, :]))
                e.done(nc.vector.tensor_scalar(place[:, :], place[:, :], 1.0 / GRID, None, ALU.mult))
                e.done(nc.vector.memset(rank[:, :], 0.0))

                def turn(c, first):
                    m = Tally(dve, turn_own)
                    m.turn(c, 5)
                    dve.wait_ge(chunk_loaded, 16 * c + 16)
                    nc.vector.tensor_tensor(keys[:, :], chunk[:, :, :].rearrange("q r e -> q (r e)"), place[:, :],
                                            ALU.add).then_inc(chunk_used, 1)
                    m.done(nc.vector.tensor_scalar(thr[:, :], ahead[:, :], 0.0, float(CH), ALU.max, ALU.min))
                    m.done(nc.vector.tensor_scalar(thr[:, :], thr[:, :], 1.0 / GRID, None, ALU.mult))
                    m.done(nc.vector.tensor_tensor(thr[:, :], thr[:, :], dstf[:, :], ALU.add))
                    m.done(nc.vector.tensor_scalar(ahead[:, :], ahead[:, :], -float(CH), None, ALU.add))
                    dve.wait_ge(chunk_used, c + 1)
                    dve.sem_inc(turn_own, 1)
                    m.n += 1

                    with dve.Fori(0, SLOTS // JB) as j:
                        r = Tally(dve, rank_own)
                        r.turn(c * (SLOTS // JB) + j, 3)
                        r.done(nc.vector.tensor_tensor(
                            less[:, :, :], keys[:, :].unsqueeze(1).to_broadcast([QF, JB, CH]),
                            thr[:, bass.ds(j * JB, JB)].unsqueeze(2).to_broadcast([QF, JB, CH]), ALU.is_lt))
                        r.done(nc.vector.reduce_sum(count[:, :], less[:, :, :], axis=AX.X))
                        r.done(nc.vector.tensor_tensor(rank[:, bass.ds(j * JB, JB)], rank[:, bass.ds(j * JB, JB)],
                                                       count[:, :], ALU.add))

                loop(dve, CHUNKS, turn)
                e.done(nc.vector.tensor_scalar(row[:, :], rank[:, :], -(EW - 1) / 2, 1.0 / EW, ALU.add, ALU.mult))
                e.done(nc.vector.tensor_scalar(row[:, :], row[:, :], 1.5 * 2 ** 23, 1.5 * 2 ** 23, ALU.add, ALU.subtract))
                e.done(nc.vector.scalar_tensor_tensor(rank[:, :], row[:, :], 3.0 * EW, rank[:, :], ALU.mult, ALU.add))
                for a in range(4):
                    e.done(nc.vector.tensor_scalar(where[:, a, :], rank[:, :], float(a * EW), None, ALU.add))
                dve.sem_inc(where_ready, 1)


def setup_phase(nc, g, x):
    with ExitStack() as ctx:
        sb = lambda name, shape, dt: sbuf(ctx, nc, name, shape, dt)
        ps = lambda name, shape: ctx.enter_context(nc.psum_tensor(name, shape, FP))
        sem = semaphores(ctx, nc, "e_")
        lasti = sb("lasti", [1, NROW], I32)
        last = sb("last", [1, NROW], FP)
        below = sb("below", [NT, NROW], FP)
        thr = sb("thr", [NT, 1], FP)
        start = sb("start", [NT, 1], FP)
        kio = sb("kio", [NT, STEPS], FP)
        M = sb("M", [NT, STEPS], FP)
        krow = sb("krow", [Q, 2], FP)
        jcol = sb("jcol", [Q, 2], FP)
        jP = sb("jP", [Q, 2], FP)
        jf = sb("jf", [1, STEPS], FP)
        jlag = sb("jlag", [1, STEPS + RING + 1], FP)
        jstep = sb("jstep", [1, STEPS + RING], FP)
        word = sb("word", [1, STEPS // RING + 1], FP)
        rowi = sb("rowi", [Q, 2], I32)
        rowf = sb("rowf", [Q, 2], FP)
        ER = sb("ER", [Q, 2, 4, EW], I32)
        EF = sb("EF", [Q, 4, 2, EW], FP)
        dloc = sb("dloc", [Q, 2, EW], FP)
        valid = sb("valid", [Q, 2, EW], FP)
        key = sb("key", [Q, SLOTS], FP)
        se = sb("se", [Q, SLOTS], FP)
        ne = sb("ne", [Q, SLOTS], FP)
        metab = sb("metab", [Q, 2, 2, EW], BF)
        wcol = sb("wcol", [Q, 2], FP)
        wbc = sb("wbc", [Q, 2, 32], FP)
        psA = ps("psA", [128, 512])
        psB = ps("psB", [128, 512])
        psC = ps("psC", [128, 512])
        psT = [ps(f"psT{n}", [128, 512]) for n in range(4)]
        const_ready = sem("const_ready")
        last_loaded = sem("last_loaded")
        last_ready = sem("last_ready")
        last_bc = sem("last_bc")
        m_ready = sem("m_ready")
        j_ready = sem("j_ready")
        rowi_ready = sem("rowi_ready")
        rows_loaded = [sem("rows_loaded0"), sem("rows_loaded1")]
        key_ready = sem("key_ready")
        key_shifted = sem("key_shifted")
        cols_in_ready = sem("cols_in_ready")
        cols_ready = sem("cols_ready")
        wbc_ready = sem("wbc_ready")
        whole_ready = sem("whole_ready")
        meta_ready = sem("meta_ready")
        meta_stored = sem("meta_stored")
        x_loaded = sem("x_loaded")
        pool_own = sem("pool_own")
        dve_own = sem("dve_own")
        block = ctx.enter_context(nc.Block())
        full = NROW - 1

        @block.gpsimd
        def _(pool):
            t = Tally(pool, pool_own)
            t.done(nc.gpsimd.memset(g.ident[:, :], 0.0))
            t.done(nc.gpsimd.affine_select(out=g.ident[:, :], in_=g.ident[:, :], compare_op=ALU.not_equal, fill=1.0,
                                           base=1, pattern=[[-1, 132]], channel_multiplier=1))
            t.done(nc.gpsimd.iota(g.part[:, :], pattern=[[0, 1]], base=0, channel_multiplier=1,
                                  allow_small_or_imprecise_dtypes=True))
            t.done(nc.gpsimd.iota(g.iota[:, :], pattern=[[0, 2], [1, P]], base=0, channel_multiplier=0,
                                  allow_small_or_imprecise_dtypes=True))
            t.done(nc.gpsimd.iota(thr[:, :], pattern=[[0, 1]], base=0, channel_multiplier=P,
                                  allow_small_or_imprecise_dtypes=True))
            t.done(nc.gpsimd.iota(kio[:, :], pattern=[[1, STEPS]], base=0, channel_multiplier=0,
                                  allow_small_or_imprecise_dtypes=True))
            nc.gpsimd.iota(krow[:, :], pattern=[[1, 2]], base=0, channel_multiplier=2,
                           allow_small_or_imprecise_dtypes=True).then_inc(const_ready, 1)
            for b in range(2):
                pool.wait_ge(rowi_ready, 1)
                nc.gpsimd.indirect_dma_start(
                    out=ER[:, b, :, :].rearrange("q a e -> q (a e)"), out_offset=None,
                    in_=g.edges.rearrange("r a e -> r (a e)"),
                    in_offset=bass.IndirectOffsetOnAxis(ap=rowi[:, b:b + 1], axis=0)).then_inc(rows_loaded[b], 16)

        @block.sync
        def _(sp):
            sp.dma_start(lasti[0:1, 0:full], g.edges[0:full, 0, EW - 1:EW].rearrange("r a -> a r"),
                         allow_slow_non_contiguous=True).then_inc(last_loaded, 16)
            sp.wait_ge(meta_ready, 1)
            for b in range(2):
                sp.dma_start(g.meta.rearrange("(q b) a e -> b q a e", b=2)[b], metab[:, b, :, :]).then_inc(meta_stored, 16)
            sp.wait_ge(meta_stored, 32)

        @block.scalar
        def _(act):
            act.dma_start(g.X1[:, :, :], x.rearrange("(t p) d -> p t d", p=P)).then_inc(x_loaded, 16)
            act.wait_ge(x_loaded, 16)

        @block.tensor
        def _(pe):
            pe.wait_ge(last_ready, 1)
            nc.tensor.matmul(psA[:, 0:NROW], g.ones[0:1, :], last[0:1, :], start=True, stop=True).then_inc(last_bc, 1)
            pe.wait_ge(m_ready, 1)
            Mb = M[:, :].rearrange("n (q b) -> n b q", b=2)
            for b in range(2):
                nc.tensor.matmul(psB[0:Q, b:b + 1], Mb[:, b, :], g.ones[0:NT, 0:1], start=True, stop=True)
            nc.tensor.matmul(psC[:, 0:STEPS], g.ones[0:NT, :], M[:, :], start=True, stop=True).then_inc(j_ready, 1)
            pe.wait_ge(key_ready, 1)
            nc.tensor.matmul(psA[0:Q, 0:1], g.ident[0:Q, 0:Q], key[:, SLOTS - 1:SLOTS], start=True, stop=True)
            nc.tensor.matmul(psA[0:Q, 1:2], g.ident[0:Q, 2:2 + Q], key[:, 0:1], start=True, stop=True) \
                .then_inc(key_shifted, 1)
            pe.wait_ge(cols_in_ready, 1)
            for n, rows in enumerate((EF[:, 1], EF[:, 0], dloc, EF[:, 3])):
                rows = rows[:, :, :]
                for b in range(2):
                    for f in range(2):
                        ins = nc.tensor.transpose(psT[n][:, (2 * b + f) * Q:(2 * b + f + 1) * Q],
                                                  rows[:, b, f * 128:f * 128 + 128], g.eye(Q))
            ins.then_inc(cols_ready, 1)
            pe.wait_ge(wbc_ready, 1)
            for n in range(2):
                ins = nc.tensor.transpose(psB[0:32, 128 * n:128 * n + Q], wbc[:, n, :], g.eye(Q))
            ins.then_inc(whole_ready, 1)

        @block.vector
        def _(dve):
            t = Tally(dve, dve_own)
            t.done(nc.vector.memset(g.ones[:, :], 1.0))
            t.done(nc.vector.memset(g.eps[:, :], EPS))
            t.done(nc.vector.memset(g.acc[:, :, :], 0.0))
            t.done(nc.vector.memset(last[:, :], float(FAR)))
            dve.wait_ge(last_loaded, 16)
            t.done(nc.vector.tensor_copy(last[0:1, 0:full], lasti[0:1, 0:full]))
            nc.vector.memset(ne[:, :], 0.0).then_inc(last_ready, 1)
            dve.wait_ge(const_ready, 1)
            dve.wait_ge(last_bc, 1)
            t.done(nc.vector.tensor_scalar(g.negpart[:, :], g.part[:, :], -1.0, None, ALU.mult))
            t.done(nc.vector.tensor_scalar(below[:, :], psA[0:NT, 0:NROW], thr[:, 0:1], None, ALU.is_lt))
            t.done(nc.vector.reduce_sum(start[:, :], below[:, :], axis=AX.X))
            t.done(nc.vector.tensor_tensor(start[:, :], start[:, :], g.part[0:NT, :], ALU.add))
            nc.vector.tensor_scalar(M[:, :], kio[:, :], start[:, 0:1], None, ALU.is_ge).then_inc(m_ready, 1)
            dve.wait_ge(j_ready, 1)
            t.done(nc.vector.tensor_scalar(jcol[:, :], psB[0:Q, 0:2], -1.0, None, ALU.add))
            t.done(nc.vector.tensor_tensor(rowf[:, :], krow[:, :], jcol[:, :], ALU.subtract))
            nc.vector.tensor_copy(rowi[:, :], rowf[:, :]).then_inc(rowi_ready, 1)
            t.done(nc.vector.tensor_scalar(jP[:, :], jcol[:, :], float(P), None, ALU.mult))
            t.done(nc.vector.tensor_scalar(jf[:, :], psC[0:1, 0:STEPS], -1.0, float(3 * D), ALU.add, ALU.mult))
            t.done(nc.vector.tensor_copy(g.tile_q[:, :], jf[:, :]))
            t.done(nc.vector.memset(jlag[:, :], 0.0))
            t.done(nc.vector.memset(jlag[:, LAG + STEPS:], NT - 1.0))
            t.done(nc.vector.tensor_scalar(jlag[:, LAG:LAG + STEPS], psC[0:1, 0:STEPS], -1.0, None, ALU.add))
            t.done(nc.vector.tensor_tensor(jstep[:, :], jlag[:, 1:], jlag[:, 0:-1], ALU.subtract))
            t.done(nc.vector.tensor_scalar(word[:, :], jlag[:, 0:-1:RING], float(ACCW), None, ALU.mult))
            for u in range(1, RING):
                t.done(nc.vector.scalar_tensor_tensor(word[:, :], jstep[:, u - 1::RING], 2.0 ** (RING_BIT + u - 1),
                                                      word[:, :], ALU.mult, ALU.add))
            t.done(nc.vector.tensor_copy(g.tiles_acc[:, :], word[:, :]))
            for b in range(2):
                dve.wait_ge(rows_loaded[b], 16)
                t.done(nc.vector.tensor_copy(EF[:, :, b, :], ER[:, b, :, :]))
            for b in range(2):
                t.done(nc.vector.tensor_scalar(dloc[:, b, :], EF[:, 0, b, :], jP[:, b:b + 1], None, ALU.subtract))
            t.done(nc.vector.tensor_scalar(valid[:, :, :], dloc[:, :, :], 0.0, None, ALU.is_ge))
            t.done(nc.vector.scalar_tensor_tensor(valid[:, :, :], dloc[:, :, :], float(P - 1), valid[:, :, :],
                                                  ALU.is_le, ALU.mult))
            t.done(nc.vector.tensor_copy(metab[:, :, 0, :], dloc[:, :, :]))
            nc.vector.tensor_copy(metab[:, :, 1, :], EF[:, 2, :, :]).then_inc(meta_ready, 1)
            kv = key[:, :].rearrange("q (b e) -> q b e", b=2)
            t.done(nc.vector.scalar_tensor_tensor(kv, EF[:, 0, :, :], 2.0, valid[:, :, :], ALU.add, ALU.mult))
            t.done(nc.vector.tensor_scalar(key[:, :], key[:, :], -1.0, None, ALU.add))
            nc.vector.memset(se[:, 0:1], 0.0).then_inc(key_ready, 1)
            t.done(nc.vector.scalar_tensor_tensor(EF[:, 0, :, :], EF[:, 1, :, :], float(NR), EF[:, 3, :, :],
                                                  ALU.mult, ALU.add))
            nc.vector.memset(wbc[:, :, :], 0.0).then_inc(cols_in_ready, 1)
            for r in range(NR):
                er = EF[:, 3, :, :].rearrange("q b e -> q (b e)")
                t.done(nc.vector.tensor_scalar(g.etm[:, r * SLOTS:(r + 1) * SLOTS], er, float(r), None, ALU.is_equal))
            dve.wait_ge(key_shifted, 1)
            t.done(nc.vector.tensor_tensor(se[:, 1:SLOTS], key[:, 1:SLOTS], key[:, 0:SLOTS - 1], ALU.is_equal))
            t.done(nc.vector.tensor_tensor(se[:, 0:1], psA[0:Q, 0:1], key[:, 0:1], ALU.is_equal))
            t.done(nc.vector.tensor_copy(ne[:, 0:SLOTS - 1], se[:, 1:SLOTS]))
            t.done(nc.vector.tensor_copy(g.next_in[:, :], ne[:, :]))
            t.done(nc.vector.tensor_scalar(g.next_out[:, :], ne[:, :], -1.0, 1.0, ALU.mult, ALU.add))
            t.done(nc.vector.tensor_tensor(ne[:, SLOTS - 1:SLOTS], psA[0:Q, 1:2], key[:, SLOTS - 1:SLOTS], ALU.is_equal))
            t.done(nc.vector.tensor_copy(g.same[:, :], se[:, :]))
            t.done(nc.vector.tensor_scalar(g.same_b[:, :], se[:, :], BIG, -BIG, ALU.mult, ALU.add))
            t.done(nc.vector.tensor_scalar(g.next_b[:, :], ne[:, :], BIG, -BIG, ALU.mult, ALU.add))
            t.done(nc.vector.tensor_tensor_scan(g.pm[:, :], se[:, :], se[:, :], 1.0, ALU.mult, ALU.min))
            t.done(nc.vector.tensor_tensor_scan(g.sm[:, ::-1], ne[:, ::-1], ne[:, ::-1], 1.0, ALU.mult, ALU.min))
            t.done(nc.vector.tensor_scalar(g.pm_b[:, :], g.pm[:, :], BIG, -BIG, ALU.mult, ALU.add))
            t.done(nc.vector.tensor_scalar(g.sm_b[:, :], g.sm[:, :], BIG, -BIG, ALU.mult, ALU.add))
            t.done(nc.vector.tensor_copy(wbc[:, 0, :], g.pm[:, SLOTS - 1:SLOTS].to_broadcast([Q, 32])))
            nc.vector.tensor_copy(wbc[:, 1, :], g.sm[:, 0:1].to_broadcast([Q, 32])).then_inc(wbc_ready, 1)
            dve.wait_ge(cols_ready, 1)
            for n, col in enumerate((g.idx0, g.idx1, g.dcol, g.ecol)):
                t.done(nc.vector.tensor_copy(col[:, :, :].rearrange("p (q b) f -> p b f q", b=2),
                                             psT[n][:, 0:4 * Q].rearrange("p (b f q) -> p b f q", b=2, f=2)))
            dve.wait_ge(whole_ready, 1)
            whole = psB[0:32, 0:256].rearrange("p (n q) -> p n q", n=2)[:, :, 0:Q]
            t.done(nc.vector.tensor_copy(g.whole[:, 0:2, :], whole))
            t.done(nc.vector.tensor_scalar(g.whole[:, 2:4, :], whole, BIG, -BIG, ALU.mult, ALU.add))


def project_phase(nc, g, query, Wq, bq, Wk, bk, Wv, bv):
    with ExitStack() as ctx:
        sb = lambda name, shape, dt: sbuf(ctx, nc, name, shape, dt)
        sem = semaphores(ctx, nc, "")
        Wt = sb("p_W", [128, 2, 3, D], FP)
        bias = sb("p_bias", [P, 3 * D], FP)
        qe = sb("p_qe", [P, D], FP)
        stats = sb("p_stats", [P, NU, 6], FP)
        mv = sb("p_mv", [P, NU, 2], FP)
        std = sb("p_std", [P, NU], FP)
        rstd = sb("p_rstd", [P, NU], FP)
        norm = sb("p_norm", [P, NU, D], FP)
        enh = sb("p_enh", [P, NU, D], FP)
        enhT = sb("p_enhT", [128, NU, 2, P], FP)
        qkv = sb("p_qkv", [P, NU, 3 * D], FP)
        rest = sb("p_rest", [P, NU, D], FP)
        psT = [ctx.enter_context(nc.psum_tensor(f"p_psT{s}", [128, 512], FP)) for s in range(2)]
        psM = [[ctx.enter_context(nc.psum_tensor(f"p_psM{s}{c}", [128, 512], FP)) for c in range(2)] for s in range(2)]
        w_loaded = sem("p_w_loaded")
        var_ready = sem("p_var_ready")
        std_ready = sem("p_std_ready")
        norm_ready = sem("p_norm_ready")
        h_ready = sem("p_h_ready")
        enh_ready = sem("p_enh_ready")
        enhT_in_psum = sem("p_enhT_in_psum")
        enhT_ready = sem("p_enhT_ready")
        product_ready = sem("p_product_ready")
        qkv_ready = sem("p_qkv_ready")
        q1_ready = sem("p_q1_ready")
        rest_ready = sem("p_rest_ready")
        q2_ready = sem("p_q2_ready")
        q3_ready = sem("p_q3_ready")
        kv_stored = [sem(f"p_kv_stored{u}") for u in range(NU)]
        waited = sem("p_waited")
        query_ready = sem("p_query_ready")
        dve_own = sem("p_dve_own")
        block = ctx.enter_context(nc.Block())
        HALF = 3 * D // 2
        X2, H2, Q2 = flat(g.X1[:, :, :]), flat(g.Hn[:, :, :]), g.Qs[0:P, :, :, :].rearrange("p t s d -> p (t s d)")
        kvt = g.kv0.rearrange("(t p) d -> p t d", p=P)

        @block.sync
        def _(sp):
            for n, (W, b) in enumerate(((Wq, bq), (Wk, bk), (Wv, bv))):
                sp.dma_start(Wt[:, :, n, :], W.rearrange("(c k) n -> k c n", c=2)).then_inc(w_loaded, 16)
                sp.dma_start(bias[:, n * D:(n + 1) * D], row_bc(b, P)).then_inc(w_loaded, 16)
            sp.dma_start(qe[:, :], row_bc(query, P)).then_inc(w_loaded, 16)

            with sp.Fori(0, NIT) as i:
                for u in range(NU):
                    sp.wait_ge(qkv_ready, i * NU + u + 1)
                    sp.dma_start(kvt[:, bass.ds(i * NU + u, 1), :], qkv[:, u:u + 1, D:3 * D]).then_inc(kv_stored[u], 16)
            for u in range(NU):
                sp.wait_ge(kv_stored[u], 16 * NIT)

        @block.scalar
        def _(act):
            def moments(i):
                act.wait_ge(var_ready, i + 1)
                nc.scalar.activation(std[:, :], mv[:, :, 1], ACT.Sqrt, bias=g.eps[0:P, :]).then_inc(std_ready, 1)

            def relu(i, u):
                act.wait_ge(norm_ready, i * NU + u + 1)
                nc.scalar.activation(tile(H2, i * NU + u, D), norm[:, u, :], ACT.Relu).then_inc(h_ready, 1)

            def move(i, u, first):
                k = i * NU + u
                act.wait_ge(enhT_in_psum, k + 1)
                if not first:
                    act.wait_ge(product_ready, k - NU + 1)
                nc.scalar.copy(flat(enhT[:, u, :, :]), psT[u % 2][:, 0:2 * P]).then_inc(enhT_ready, 1)
                act.wait_ge(qkv_ready, k + 1)
                nc.scalar.copy(Q2[:, bass.ds(k * 3 * D, D)], qkv[:, u, 0:D]).then_inc(q1_ready, 1)
                act.wait_ge(rest_ready, k + 1)
                nc.scalar.copy(Q2[:, bass.ds(k * 3 * D + D, D)], rest[:, u, :]).then_inc(q2_ready, 1)

            def turn(i, first, last):
                if not last:
                    moments(i + 1)
                for u in range(NU):
                    if not last:
                        relu(i + 1, u)
                    move(i, u, first)

            moments(0)
            for u in range(NU):
                relu(0, u)
            turn(0, True, False)
            with act.Fori(1, NIT - 1) as i:
                turn(i, False, False)
            turn(NIT - 1, False, True)

        @block.gpsimd
        def _(pool):
            with pool.Fori(0, NIT) as i:
                for u in range(NU):
                    k = i * NU + u
                    pool.wait_ge(q1_ready, k + 1)
                    nc.gpsimd.tensor_tensor(rest[:, u, :], qkv[:, u, 0:D], Q2[:, bass.ds(k * 3 * D, D)],
                                            ALU.subtract).then_inc(rest_ready, 1)
                    pool.wait_ge(q2_ready, k + 1)
                    nc.gpsimd.tensor_tensor(Q2[:, bass.ds(k * 3 * D + 2 * D, D)], rest[:, u, :],
                                            Q2[:, bass.ds(k * 3 * D + D, D)], ALU.subtract).then_inc(q3_ready, 1)

        @block.vector
        def _(dve):
            t = Tally(dve, dve_own)
            LN = 2

            def moments(i):
                t.turn(i, LN)
                for u in range(NU):
                    ins = nc.vector.bn_stats(stats[:, u, :], tile(X2, i * NU + u, D))
                t.done(ins)
                dve.sem_inc(waited, 1)
                for u in range(NU):
                    ins = nc.vector.bn_aggr(mv[:, u, :], stats[:, u, :])
                ins.then_inc(var_ready, 1)
                dve.wait_ge(std_ready, i + 1)
                t.done(nc.vector.reciprocal(rstd[:, :], std[:, :]))

            def normalise(i, u, first):
                k = i * NU + u
                if not first:
                    dve.wait_ge(h_ready, k - NU + 1)
                nc.vector.tensor_scalar(norm[:, u, :], tile(X2, k, D), mv[:, u, 0:1], rstd[:, u:u + 1],
                                        ALU.subtract, ALU.mult).then_inc(norm_ready, 1)
                dve.wait_ge(norm_ready, k + 1)
                if not first:
                    dve.wait_ge(enhT_in_psum, k - NU + 1)
                nc.vector.scalar_tensor_tensor(enh[:, u, :], norm[:, u, :], 0.0, qe[:, :], ALU.max,
                                               ALU.add).then_inc(enh_ready, 1)

            def move(i, u, first):
                k = i * NU + u
                dve.wait_ge(product_ready, k + 1)
                if not first:
                    dve.wait_ge(kv_stored[u], 16 * i)
                    dve.wait_ge(q3_ready, k - NU + 1)
                for c in range(2):
                    cols = slice(c * HALF, (c + 1) * HALF)
                    ins = nc.vector.tensor_tensor(qkv[:, u, cols], psM[u % 2][c][0:P, 0:HALF], bias[:, cols], ALU.add)
                ins.then_inc(qkv_ready, 1)

            def turn(i, first, last):
                if not last:
                    moments(i + 1)
                for u in range(NU):
                    if not last:
                        normalise(i + 1, u, False)
                    move(i, u, first)

            dve.wait_ge(w_loaded, 16 * 7)
            nc.vector.tensor_scalar(qe[:, :], qe[:, :], 0.1, None, ALU.mult).then_inc(query_ready, 1)
            dve.wait_ge(query_ready, 1)
            moments(0)
            for u in range(NU):
                normalise(0, u, True)
            turn(0, True, False)
            with dve.Fori(1, NIT - 1) as i:
                turn(i, False, False)
            turn(NIT - 1, False, True)

        @block.tensor
        def _(pe):
            pe.wait_ge(w_loaded, 16 * 7)

            def project(i, first):
                for u in range(NU):
                    k = i * NU + u
                    pe.wait_ge(enh_ready, k + 1)
                    if not first or u >= 2:
                        pe.wait_ge(enhT_ready, k - back(u) + 1)
                    for c in range(2):
                        ins = nc.tensor.transpose(psT[u % 2][:, c * P:(c + 1) * P], enh[:, u, c * 128:(c + 1) * 128],
                                                  g.eye(P))
                    ins.then_inc(enhT_in_psum, 1)
                    pe.wait_ge(enhT_ready, k + 1)
                    if not first or u >= 2:
                        pe.wait_ge(qkv_ready, k - back(u) + 1)
                    for b in range(2):
                        for c in range(2):
                            ins = nc.tensor.matmul(psM[u % 2][b][0:P, 0:HALF], enhT[:, u, c, :],
                                                   Wt[:, c, :, :].rearrange("k n d -> k (n d)")[:, b * HALF:(b + 1) * HALF],
                                                   start=(c == 0), stop=(c == 1))
                    ins.then_inc(product_ready, 1)

            loop(pe, NIT, project)


def score_phase(nc, g, layer, table, rel_w):
    L = f"s{layer}_"
    with ExitStack() as ctx:
        sb = lambda name, shape, dt: sbuf(ctx, nc, L + name, shape, dt)
        sem = semaphores(ctx, nc, L)
        parts = 2 if layer == 0 else 1
        kv = sb("kv", [128, U, 2, 2 * D], FP)
        idx = sb("idx", [128, U, 2], I32)
        mb = sb("mb", [P, U, parts * EW], BF)
        dist = sb("dist", [P, U, parts * EW], BF)
        hot = sb("hot", [P, U, parts * EW], BF)
        keyr = sb("keyr", [128, 2, 2 * D], FP) if layer == 0 else None
        prod = sb("prod", [128, 2, 2 * D], FP)
        relf = sb("relf", [NREL, DK], FP) if layer == 0 else None
        rel = sb("rel", [NREL, 3, D], BF) if layer == 0 else None
        psQ = [ctx.enter_context(nc.psum_tensor(f"{L}psQ{s}", [128, 512], FP)) for s in range(2)]
        psR = [ctx.enter_context(nc.psum_tensor(f"{L}psR{s}", [128, 512], FP)) for s in range(2)]
        gathered = [sem(f"gathered{u}") for u in range(U)]
        meta_loaded = [sem(f"meta_loaded{u}") for u in range(U)]
        v_stored = [sem(f"v_stored{u}") for u in range(U)]
        idx_ready = sem("idx_ready")
        waited = sem("waited")
        dist_ready = sem("dist_ready")
        hot_ready = sem("hot_ready")
        query_ready = sem("query_ready")
        key_read = sem("key_read")
        keyr_ready = sem("keyr_ready")
        prod_ready = sem("prod_ready")
        score_ready = sem("score_ready")
        rel_loaded = sem("rel_loaded")
        rel_ready = sem("rel_ready")
        dve_own = sem("dve_own")
        block = ctx.enter_context(nc.Block())
        idx_all = flat((g.idx0 if layer == 0 else g.idx1)[:, :, :])
        meta2 = g.meta.rearrange("k a e -> k (a e)")
        S2 = g.S[:, :, :, :].rearrange("p k f h -> p (k f h)")
        Q2 = g.Qs[0:P, :, :, :].rearrange("p t s d -> p (t s d)")
        vst = g.vst.rearrange("k p f d -> p k f d")

        @block.gpsimd
        def _(pool):
            def gather(i, first):
                for u in range(U):
                    k = i * U + u
                    if not first:
                        pool.wait_ge(v_stored[u], 16 * i)
                        pool.wait_ge(key_read if layer == 0 else prod_ready, k - U + 1)
                    nc.gpsimd.tensor_copy(idx[:, u, :], idx_all[:, bass.ds(k * 2, 2)]).then_inc(idx_ready, 1)
                    pool.wait_ge(idx_ready, k + 1)
                    pool.sem_inc(waited, 1)
                    for f in range(2):
                        nc.gpsimd.indirect_dma_start(
                            out=kv[:, u, f, :], out_offset=None, in_=table[:, :],
                            in_offset=bass.IndirectOffsetOnAxis(ap=idx[:, u, f:f + 1], axis=0)).then_inc(gathered[u], 16)

            loop(pool, ITERS, gather)

        @block.sync
        def _(sp):
            if layer == 0:
                sp.dma_start(relf[:, :], rel_w).then_inc(rel_loaded, 16)

            def move(i, first):
                for u in range(U):
                    k = i * U + u
                    if not first:
                        sp.wait_ge(dist_ready, k - U + 1)
                    sp.dma_start(mb[:, u, :], meta2[bass.ds(k, 1), 0:parts * EW].partition_broadcast(P)
                                 if False else meta2[bass.ds(k, 1), 0:parts * EW].to_broadcast([P, parts * EW])) \
                        .then_inc(meta_loaded[u], 16)
                for u in range(U):
                    k = i * U + u
                    sp.wait_ge(gathered[u], 32 * (i + 1))
                    sp.dma_start(vst[:, bass.ds(k, 1), :, :].rearrange("p k f d -> p (k f) d"), kv[:, u, :, D:2 * D]) \
                        .then_inc(v_stored[u], 16)

            loop(sp, ITERS, move)
            for u in range(U):
                sp.wait_ge(v_stored[u], 16 * ITERS)

        @block.scalar
        def _(act):
            def one_hot(i, first):
                for u in range(U):
                    k = i * U + u
                    act.wait_ge(meta_loaded[u], 16 * (i + 1))
                    nc.scalar.activation(dist[:, u, :], mb[:, u, :], ACT.Abs, bias=g.negpart[0:P, :]) \
                        .then_inc(dist_ready, 1)
                    act.wait_ge(dist_ready, k + 1)
                    if not first:
                        act.wait_ge(query_ready, k - U + 1)
                    nc.scalar.activation(hot[:, u, :], dist[:, u, :], ACT.Relu, bias=g.ones[0:P, 0:1], scale=-1.0) \
                        .then_inc(hot_ready, 1)

            loop(act, ITERS, one_hot)

        @block.tensor
        def _(pe):
            if layer == 0:
                pe.wait_ge(rel_ready, 1)

            def look_up(i, first):
                for u in range(U):
                    k = i * U + u
                    base = pe.value_load(g.tile_q[0:1, bass.ds(k, 1)], min_val=0, max_val=(NT - 1) * 3 * D)
                    pe.wait_ge(hot_ready, k + 1)
                    if not first or u >= 2:
                        pe.wait_ge(prod_ready, k - 1)
                    for f in range(2):
                        cols = slice(f * 128, f * 128 + 128)
                        if layer == 0:
                            for s in range(3):
                                nc.tensor.matmul(psR[u % 2][:, f * D:(f + 1) * D],
                                                 hot[0:NREL, u, EW + f * 128:EW + f * 128 + 128], rel[:, s, :],
                                                 start=(s == 0), stop=(s == 2))
                        for s in range(3):
                            ins = nc.tensor.matmul(psQ[u % 2][:, f * D:(f + 1) * D], hot[:, u, cols],
                                                   Q2[:, bass.ds(base + s * D, D)], start=(s == 0), stop=(s == 2))
                    ins.then_inc(query_ready, 1)

            loop(pe, ITERS, look_up)

        @block.vector
        def _(dve):
            if layer == 0:
                t = Tally(dve, dve_own)
                dve.wait_ge(rel_loaded, 16)
                t.done(nc.vector.tensor_scalar(relf[:, :], relf[:, :], 0.2, None, ALU.mult))
                for s in range(3):
                    t.done(nc.vector.tensor_copy(rel[:, s, 0:DK], relf[:, :]))
                    if s < 2:
                        t.done(nc.vector.tensor_tensor(relf[:, :], relf[:, :], rel[:, s, 0:DK], ALU.subtract))
                for h in range(1, H):
                    ins = nc.vector.tensor_copy(rel[:, :, h * DK:(h + 1) * DK], rel[:, :, 0:DK])
                ins.then_inc(rel_ready, 1)

            def score(i, first):
                for u in range(U):
                    k = i * U + u
                    s = u % 2
                    keys = kv[:, u, :, 0:D]
                    dve.wait_ge(gathered[u], 32 * (i + 1))
                    dve.wait_ge(query_ready, k + 1)
                    q = psQ[s][:, :].rearrange("p (f d) -> p f d", f=2)
                    k3 = keyr[:, s, :].rearrange("p (f d) -> p f d", f=2) if layer == 0 else None
                    p3 = prod[:, s, :].rearrange("p (f d) -> p f d", f=2)
                    if layer == 0:
                        nc.vector.tensor_tensor(k3, keys, psR[s][:, :].rearrange("p (f d) -> p f d", f=2), ALU.add) \
                            .then_inc(key_read, 1)
                        dve.wait_ge(key_read, k + 1)
                        nc.vector.tensor_tensor(p3, k3, q, ALU.mult).then_inc(prod_ready, 1)
                        dve.wait_ge(prod_ready, k + 1)
                    else:
                        nc.vector.tensor_tensor(p3, keys, q, ALU.mult).then_inc(prod_ready, 1)
                        dve.wait_ge(prod_ready, k + 1)
                    nc.vector.reduce_sum(S2[:, bass.ds(k * 2 * H, 2 * H)],
                                         prod[:, s, :].rearrange("p (c e) -> p c e", e=DK), axis=AX.X) \
                        .then_inc(score_ready, 1)

            loop(dve, ITERS, score)


def softmax_phase(nc, g, layer):
    L = f"m{layer}_"
    rels = NR if layer == 1 else 1
    cols = H * rels
    XS, FS = 4, 2
    with ExitStack() as ctx:
        sb = lambda name, shape, dt: sbuf(ctx, nc, L + name, shape, dt)
        sem = semaphores(ctx, nc, L)
        row = lambda h: slice(h * SLOTS, (h + 1) * SLOTS)
        sc = sb("sc", [Q, H * SLOTS], FP)
        sel = sb("sel", [Q, H * SLOTS], FP)
        fwd = sb("fwd", [Q, FS, SLOTS], FP)
        etm_b = sb("etm_b", [Q, NR * SLOTS], BF) if layer == 1 else None
        ends = sb("ends", [Q, 2, 32], FP)
        endsT = sb("endsT", [32, 2, Q], FP)
        carry = sb("carry", [32, 2, Q + 2], FP)
        into = sb("into", [Q, 2, 32], FP)
        in_q = 16
        qs = g.Qs[0:Q, :, :, :].rearrange("p t s d -> p (t s d)").bitcast(FP)
        seg_tensors = [(sel[:, :], cols)] if layer == 0 else [(qs[:, 0:in_q * SLOTS], in_q),
                                                             (flat(g.acc[0:Q, :, :])[:, 0:(cols - in_q) * SLOTS], cols - in_q)]
        masked = flat(g.acc[0:Q, :, :])[:, (cols - in_q) * SLOTS:(cols - in_q + XS) * SLOTS] \
            .rearrange("q (x e) -> q x e", x=XS) if layer == 1 else None
        psS = [ctx.enter_context(nc.psum_tensor(f"{L}psS{h}", [128, 512], FP)) for h in range(H)]
        psE = ctx.enter_context(nc.psum_tensor(f"{L}psE", [128, 512], FP))
        psI = ctx.enter_context(nc.psum_tensor(f"{L}psI", [128, 512], FP))
        psW = [ctx.enter_context(nc.psum_tensor(f"{L}psW{n}", [128, 512], FP)) for n in range(2)]
        rows_ready = sem("rows_ready")
        scores_ready = sem("scores_ready")
        bias_ready = sem("bias_ready")
        masked_ready = sem("masked_ready")
        fwd_ready = sem("fwd_ready")
        seg_ready = sem("seg_ready")
        after_in = sem("after_in")
        before_in = sem("before_in")
        selected = sem("selected")
        ends_ready = sem("ends_ready")
        ends_turned = sem("ends_turned")
        carry_ready = sem("carry_ready")
        carry_turned = sem("carry_turned")
        shifted = sem("shifted")
        exp_ready = sem("exp_ready")
        inverted = sem("inverted")
        weights_ready = sem("weights_ready")
        w_turned = sem("w_turned")
        w_moved = sem("w_moved")
        dve_own = sem("dve_own")
        block = ctx.enter_context(nc.Block())
        Sv = g.S[:, :, :, :].rearrange("p (q b) f h -> p h b f q", b=2)
        Wv = g.W[:, :, :, :].rearrange("p (q b) f h -> p h b f q", b=2)

        def seg(c):
            if layer == 1 and c >= in_q:
                return seg_tensors[1][0][:, (c - in_q) * SLOTS:(c - in_q + 1) * SLOTS]
            return seg_tensors[0][0][:, c * SLOTS:(c + 1) * SLOTS]

        def source(c):
            return masked[:, c % XS, :] if layer == 1 else sc[:, row(c)]

        @block.tensor
        def _(pe):
            for h in range(H):
                for b in range(2):
                    for f in range(2):
                        n = 2 * b + f
                        ins = nc.tensor.transpose(psS[h][0:Q, n * 128:(n + 1) * 128], Sv[:, h, b, f, :], g.eye(128))
                ins.then_inc(rows_ready, 1)
            for turn in range(2):
                pe.wait_ge(ends_ready, turn + 1)
                for n in range(2):
                    ins = nc.tensor.transpose(psE[0:32, n * 128:n * 128 + Q], ends[:, n, :], g.eye(Q))
                ins.then_inc(ends_turned, 1)
                pe.wait_ge(carry_ready, turn + 1)
                for n in range(2):
                    ins = nc.tensor.transpose(psI[0:Q, n * 32:(n + 1) * 32], carry[:, n, 1:1 + Q], g.eye(32))
                ins.then_inc(carry_turned, 1)
            for h in range(H):
                pe.wait_ge(weights_ready, h + 1)
                if h >= 2:
                    pe.wait_ge(w_moved, h - 1)
                for n in range(4):
                    ins = nc.tensor.transpose(psW[h % 2][:, n * Q:(n + 1) * Q],
                                              sc[:, h * SLOTS + n * 128:h * SLOTS + (n + 1) * 128], g.eye(Q))
                ins.then_inc(w_turned, 1)

        @block.scalar
        def _(act):
            for h in range(H):
                act.wait_ge(rows_ready, h + 1)
                nc.scalar.activation(sc[:, row(h)], psS[h][0:Q, :], ACT.Copy, scale=DK ** -0.5 if layer == 0 else 1.0) \
                    .then_inc(scores_ready, 1)
            for h in range(H):
                act.wait_ge(shifted, h + 1)
                nc.scalar.activation(sc[:, row(h)], sel[:, row(h)], ACT.Exp).then_inc(exp_ready, 1)
            for h in range(H):
                act.wait_ge(w_turned, h + 1)
                nc.scalar.copy(Wv[:, h], psW[h % 2][:, 0:4 * Q].rearrange("p (b f q) -> p b f q", b=2, f=2)) \
                    .then_inc(w_moved, 1)

        if layer == 1:
            @block.gpsimd
            def _(pool):
                pool.wait_ge(bias_ready, 1)
                for kind in range(2):
                    for c in range(cols):
                        h, r = c // NR, c % NR
                        pool.wait_ge(exp_ready if kind else scores_ready, h + 1)
                        n = kind * cols + c
                        if n >= XS:
                            pool.wait_ge(fwd_ready, n - XS + 1)
                        nc.gpsimd.tensor_tensor(masked[:, c % XS, :], sc[:, row(h)], (g.etm if kind else etm_b)[:, row(r)],
                                                ALU.mult if kind else ALU.add).then_inc(masked_ready, 1)

        @block.vector
        def _(dve):
            t = Tally(dve, dve_own)

            def reduce_rows(kind):
                def back_scan(c):
                    dve.wait_ge(fwd_ready, kind * cols + c + 1)
                    if kind == 0:
                        ins = nc.vector.tensor_tensor_scan(seg(c)[:, ::-1], g.next_b[:, ::-1], fwd[:, c % FS, ::-1], -BIG,
                                                           ALU.add, ALU.max)
                    else:
                        ins = nc.vector.tensor_tensor_scan(seg(c)[:, ::-1], g.next_in[:, ::-1], fwd[:, c % FS, ::-1], 0.0,
                                                           ALU.mult, ALU.max)
                    ins.then_inc(seg_ready, 1)

                for c in range(cols):
                    if layer == 1:
                        dve.wait_ge(masked_ready, kind * cols + c + 1)
                    else:
                        dve.wait_ge(exp_ready if kind else scores_ready, c + 1)
                    if kind * cols + c >= FS:
                        dve.wait_ge(seg_ready, kind * cols + c - FS + 1)
                    if kind == 0:
                        ins = nc.vector.tensor_tensor_scan(fwd[:, c % FS, :], g.same_b[:, :], source(c), -BIG,
                                                           ALU.add, ALU.max)
                    else:
                        ins = nc.vector.tensor_tensor_scan(fwd[:, c % FS, :], g.same[:, :], source(c), 0.0,
                                                           ALU.mult, ALU.add)
                    ins.then_inc(fwd_ready, 1)
                    if c > 0:
                        back_scan(c - 1)
                back_scan(cols - 1)

            def carries(kind):
                least = 0.0 if kind else -BIG
                op = (ALU.mult, ALU.add) if kind else (ALU.add, ALU.max)
                w = 0 if kind else 2
                dve.wait_ge(seg_ready, (kind + 1) * cols)
                at = 0
                for tensor, n in seg_tensors:
                    by_column = tensor.rearrange("q (c e) -> q c e", e=SLOTS)
                    for end in range(2):
                        ins = nc.vector.tensor_copy(ends[:, end, at:at + n], by_column[:, :, end * (SLOTS - 1)])
                    at += n
                ins.then_inc(ends_ready, 1)
                t.done(nc.vector.memset(carry[:, :, :], least))
                dve.wait_ge(ends_turned, kind + 1)
                t.done(nc.vector.tensor_copy(endsT[:, :, :],
                                             psE[0:32, 0:256].rearrange("c (n q) -> c n q", n=2)[:, :, 0:Q]))
                t.done(nc.vector.tensor_tensor_scan(carry[:, 0, 0:Q][:, ::-1], g.whole[:, w + 1, ::-1], endsT[:, 0, ::-1],
                                                    least, op[0], op[1]))
                nc.vector.tensor_tensor_scan(carry[:, 1, 2:Q + 2], g.whole[:, w, :], endsT[:, 1, :],
                                             least, op[0], op[1]).then_inc(carry_ready, 1)
                dve.wait_ge(carry_turned, kind + 1)
                t.done(nc.vector.tensor_copy(flat(into[:, :, :]), psI[0:Q, 0:64]))

            def add_carries(kind, finish):
                n0 = kind * cols
                op = (ALU.mult, ALU.add) if kind else (ALU.add, ALU.max)

                def after(c):
                    nc.vector.scalar_tensor_tensor(seg(c), (g.sm if kind else g.sm_b)[:, :], into[:, 0, c:c + 1], seg(c),
                                                   op[0], op[1]).then_inc(after_in, 1)

                def before(c):
                    dve.wait_ge(after_in, n0 + c + 1)
                    nc.vector.scalar_tensor_tensor(seg(c), (g.pm if kind else g.pm_b)[:, :], into[:, 1, c:c + 1], seg(c),
                                                   op[0], op[1]).then_inc(before_in, 1)

                def select(c):
                    h, r = c // rels, c % rels
                    dve.wait_ge(before_in, n0 + c + 1)
                    if layer == 1:
                        if r > 0:
                            dve.wait_ge(selected, n0 + c)
                            nc.vector.copy_predicated(sel[:, row(h)], g.etm[:, row(r)].bitcast(mybir.dt.uint16), seg(c)).then_inc(selected, 1)
                        else:
                            nc.vector.tensor_copy(sel[:, row(h)], seg(c)).then_inc(selected, 1)
                        if r == rels - 1:
                            dve.wait_ge(selected, n0 + c + 1)
                    if r == rels - 1:
                        finish(h)

                for c in range(cols + 2):
                    if c < cols:
                        after(c)
                    if 1 <= c <= cols:
                        before(c - 1)
                    if c >= 2:
                        select(c - 2)

            def shift(h):
                nc.vector.tensor_tensor(sel[:, row(h)], sc[:, row(h)], sel[:, row(h)], ALU.subtract).then_inc(shifted, 1)

            def divide(h):
                nc.vector.reciprocal(sel[:, row(h)], sel[:, row(h)]).then_inc(inverted, 1)
                dve.wait_ge(inverted, h + 1)
                nc.vector.tensor_tensor(sc[:, row(h)], sc[:, row(h)], sel[:, row(h)], ALU.mult).then_inc(weights_ready, 1)

            t.done(nc.vector.memset(ends[:, :, :], 0.0))
            if layer == 1:
                nc.vector.tensor_scalar(etm_b[:, :], g.etm[:, :], BIG, -BIG, ALU.mult, ALU.add).then_inc(bias_ready, 1)
            reduce_rows(0)
            carries(0)
            add_carries(0, shift)
            dve.wait_ge(exp_ready, H)
            reduce_rows(1)
            carries(1)
            add_carries(1, divide)


def aggregate_phase(nc, g, layer):
    L = f"a{layer}_"
    with ExitStack() as ctx:
        sb = lambda name, shape, dt: sbuf(ctx, nc, L + name, shape, dt)
        sem = semaphores(ctx, nc, L)
        width = ACCW if layer == 0 else D
        turns = STEPS // RING
        v = sb("v", [128, RING, 2, ACCW], FP)
        diff = sb("diff", [128, HOTS, 2, P], BF)
        dist = sb("dist", [128, HOTS, 2, P], BF)
        hot = sb("hot", [128, HOTS, 2, P], FP)
        psA = [ctx.enter_context(nc.psum_tensor(f"{L}psA{s}", [128, 512], FP)) for s in range(HOTS)]
        v_loaded = [sem(f"v_loaded{u}") for u in range(RING)]
        diff_ready = sem("diff_ready")
        dist_ready = sem("dist_ready")
        hot_ready = sem("hot_ready")
        weighted = sem("weighted")
        sum_ready = sem("sum_ready")
        added = sem("added")
        zeroed = sem("zeroed")
        block = ctx.enter_context(nc.Block())
        vst = g.vst.rearrange("k p f d -> p k f d")
        acc2 = flat(g.acc[:, :, :])
        W3 = g.W[:, :, :, :].rearrange("p k f h -> p (k f h)")
        dcol, ecol = flat(g.dcol[:, :, :]), flat(g.ecol[:, :, :])
        iota = g.iota[:, :].rearrange("p (f n) -> p f n", f=2)

        @block.sync
        def _(sp):
            def load(i, first):
                for u in range(RING):
                    k = i * RING + u
                    if not first:
                        sp.wait_ge(sum_ready, k - RING + 1)
                    sp.dma_start(v[:, u, :, 0:D], vst[:, bass.ds(k, 1), :, :].rearrange("p k f d -> p (k f) d")) \
                        .then_inc(v_loaded[u], 16)

            loop(sp, turns, load)

        @block.gpsimd
        def _(pool):
            def distance(i, first):
                for u in range(RING):
                    k = i * RING + u
                    if not first or u >= HOTS:
                        pool.wait_ge(dist_ready, k - HOTS + 1)
                    nc.gpsimd.tensor_tensor(diff[:, u % HOTS, :, :], iota,
                                            dcol[:, bass.ds(k * 2, 2)].unsqueeze(2).to_broadcast([128, 2, P]),
                                            ALU.subtract).then_inc(diff_ready, 1)

            loop(pool, turns, distance)

        @block.scalar
        def _(act):
            def one_hot(k, s, first):
                act.wait_ge(dist_ready, k + 1)
                if not first:
                    act.wait_ge(sum_ready, k - HOTS + 1)
                nc.scalar.activation(hot[:, s, :, :], dist[:, s, :, :], ACT.Relu, bias=g.ones[:, 0:1], scale=-1.0) \
                    .then_inc(hot_ready, 1)

            def turn(i, first):
                for u in range(RING):
                    k = i * RING + u
                    act.wait_ge(diff_ready, k + 1)
                    if not first or u >= HOTS:
                        act.wait_ge(hot_ready, k - HOTS + 1)
                    nc.scalar.activation(dist[:, u % HOTS, :, :], diff[:, u % HOTS, :, :], ACT.Abs) \
                        .then_inc(dist_ready, 1)
                    if not (first and u == 0):
                        one_hot(k - 1, (u - 1) % HOTS, first and u - 1 < HOTS)

            loop(act, turns, turn)
            one_hot(STEPS - 1, HOTS - 1, False)

        @block.tensor
        def _(pe):
            def add_up(i, first):
                for u in range(RING):
                    k = i * RING + u
                    pe.wait_ge(hot_ready, k + 1)
                    pe.wait_ge(weighted, k + 1)
                    if not first or u >= HOTS:
                        pe.wait_ge(added, k - HOTS + 1)
                    for f in range(2):
                        ins = nc.tensor.matmul(psA[u % HOTS][0:P, 0:width], hot[:, u % HOTS, f, :], v[:, u, f, 0:width],
                                               start=(f == 0), stop=(f == 1))
                    ins.then_inc(sum_ready, 1)

            loop(pe, turns, add_up)

        @block.vector
        def _(dve):
            nc.vector.memset(acc2, 0.0).then_inc(zeroed, 1)
            dve.wait_ge(zeroed, 1)

            def node_tiles(i):
                most = (NT - 1) * ACCW
                word = dve.value_load(g.tiles_acc[0:1, bass.ds(i, 1)], min_val=0, max_val=2 ** (RING_BIT + RING))
                at = [(word & (2 ** RING_BIT - 1)).with_bounds(min_val=0, max_val=most)]
                for u in range(1, RING):
                    at.append((at[-1] + ((word >> (RING_BIT + u - 1)) & 1) * ACCW).with_bounds(min_val=0, max_val=most))
                return at

            def add(k, s, base, start):
                dve.wait_ge(sum_ready, k + 1)
                if not start:
                    dve.wait_ge(added, k)
                nc.vector.tensor_tensor(acc2[:, bass.ds(base, width)], acc2[:, bass.ds(base, width)],
                                        psA[s][0:P, 0:width], ALU.add).then_inc(added, 1)

            def turn(i, first):
                at = node_tiles(i)
                for u in range(RING):
                    k = i * RING + u
                    dve.wait_ge(v_loaded[u], 16 * (i + 1))
                    if layer == 0:
                        nc.vector.tensor_tensor(v[:, u, :, D:ACCW], iota[:, :, 0:NR],
                                                ecol[:, bass.ds(k * 2, 2)].unsqueeze(2).to_broadcast([128, 2, NR]),
                                                ALU.is_equal)
                    rows = v[:, u, :, 0:D].rearrange("p f (h e) -> p f h e", h=H)
                    nc.vector.tensor_tensor(rows, rows,
                                            W3[:, bass.ds(k * 2 * H, 2 * H)].rearrange("p (f h) -> p f h", f=2)
                                            .unsqueeze(3).to_broadcast([128, 2, H, DK]),
                                            ALU.mult).then_inc(weighted, 1)
                    if not first or u >= LAG:
                        add(k - LAG, (u - LAG) % HOTS, at[u], first and u == LAG)

            loop(dve, turns, turn)
            at = node_tiles(turns)
            for u in range(LAG):
                add(STEPS - LAG + u, (RING - LAG + u) % HOTS, at[u], False)


class Types:

    def __init__(self, ctx, nc):
        self.hot = sbuf(ctx, nc, "type_hot", [NTY, N], FP)
        self.row = sbuf(ctx, nc, "type_row", [128, N], BF)


def layer0_output_phase(nc, g, ty, Wo, bo, gamma, beta, node_type):
    with ExitStack() as ctx:
        sb = lambda name, shape, dt: sbuf(ctx, nc, "o_" + name, shape, dt)
        sem = semaphores(ctx, nc, "o_")
        Wt = sb("W", [128, 2, D], FP)
        bob, gab, beb = sb("bo", [P, D], FP), sb("gamma", [P, D], FP), sb("beta", [P, D], FP)
        types = g.Qs[:, :, :, :].rearrange("p t s d -> p (t s d)")[:, 0:2 * N].bitcast(I32)
        deg = sb("deg", [P, NT], FP)
        alone = sb("alone", [P, NT], FP)
        v0 = sb("v0", [P, NU, D], FP)
        msg = sb("msg", [P, NU, D], FP)
        msgT = sb("msgT", [128, NU, 2, P], FP)
        hb = sb("hb", [P, NU, D], FP)
        xb = sb("xb", [P, NU, D], FP)
        y = sb("y", [P, NU, D], FP)
        stats = sb("stats", [P, NU, 6], FP)
        mv = sb("mv", [P, NU, 2], FP)
        std = sb("std", [P, NU], FP)
        rstd = sb("rstd", [P, NU], FP)
        psT = [ctx.enter_context(nc.psum_tensor(f"o_psT{s}", [128, 512], FP)) for s in range(2)]
        psO = [ctx.enter_context(nc.psum_tensor(f"o_psO{s}", [128, 512], FP)) for s in range(2)]
        loaded = sem("loaded")
        types_loaded = sem("types_loaded")
        v_loaded = sem("v_loaded")
        msg_ready = sem("msg_ready")
        msgT_in_psum = sem("msgT_in_psum")
        msgT_ready = sem("msgT_ready")
        out_in_psum = sem("out_in_psum")
        y_ready = sem("y_ready")
        hb_ready = sem("hb_ready")
        xb_ready = sem("xb_ready")
        var_ready = sem("var_ready")
        std_ready = sem("std_ready")
        x1_ready = sem("x1_ready")
        norm_ready = sem("norm_ready")
        h_ready = sem("h_ready")
        waited = sem("waited")
        start_own = sem("start_own")
        dve_own = sem("dve_own")
        block = ctx.enter_context(nc.Block())
        X2, H2, A2 = flat(g.X1[:, :, :]), flat(g.Hn[:, :, :]), flat(g.acc[:, :, :])
        v0t = g.kv0.rearrange("(t p) d -> p t d", p=P)

        @block.sync
        def _(sp):
            sp.dma_start(Wt[:, :, :], Wo.rearrange("(c k) n -> k c n", c=2)).then_inc(loaded, 16)
            for dst_, vec in ((bob, bo), (gab, gamma), (beb, beta)):
                sp.dma_start(dst_[:, :], row_bc(vec, P)).then_inc(loaded, 16)
            sp.dma_start(types, row_bc(node_type, 128)).then_inc(types_loaded, 16)

            def load(i, first):
                if not first:
                    sp.wait_ge(msg_ready, i * NU)
                sp.dma_start(v0[:, :, :], v0t[:, bass.ds(i * NU, NU), D:2 * D]).then_inc(v_loaded, 16)

            loop(sp, NIT, load)

        @block.gpsimd
        def _(pool):
            pool.wait_ge(loaded, 64)

            def add(i, first):
                for u in range(NU):
                    k = i * NU + u
                    if not first:
                        pool.wait_ge(y_ready, k - NU + 1)
                    nc.gpsimd.tensor_tensor(hb[:, u, :], tile(H2, k, D), bob[:, :], ALU.add).then_inc(hb_ready, 1)
                    if not first:
                        pool.wait_ge(x1_ready, k - NU + 1)
                    nc.gpsimd.tensor_tensor(xb[:, u, :], tile(X2, k, D), beb[:, :], ALU.add).then_inc(xb_ready, 1)

            loop(pool, NIT, add)

        @block.scalar
        def _(act):
            def turn(i, first):
                for u in range(NU):
                    k = i * NU + u
                    act.wait_ge(msgT_in_psum, k + 1)
                    if not first:
                        act.wait_ge(out_in_psum, k - NU + 1)
                    nc.scalar.copy(flat(msgT[:, u, :, :]), psT[u % 2][:, 0:2 * P]).then_inc(msgT_ready, 1)
                for n in range(2):
                    act.wait_ge(var_ready, i * 2 + n + 1)
                    nc.scalar.activation(std[:, :], mv[:, :, 1], ACT.Sqrt, bias=g.eps[0:P, :]).then_inc(std_ready, 1)
                for u in range(NU):
                    k = i * NU + u
                    act.wait_ge(norm_ready, k + 1)
                    nc.scalar.activation(tile(H2, k, D), y[:, u, :], ACT.Relu).then_inc(h_ready, 1)

            loop(act, NIT, turn)

        @block.tensor
        def _(pe):
            pe.wait_ge(loaded, 64)

            def turn(i, first):
                for u in range(NU):
                    k = i * NU + u
                    pe.wait_ge(msg_ready, k + 1)
                    if not first or u >= 2:
                        pe.wait_ge(msgT_ready, k - back(u) + 1)
                    for c in range(2):
                        ins = nc.tensor.transpose(psT[u % 2][:, c * P:(c + 1) * P], msg[:, u, c * 128:(c + 1) * 128],
                                                  g.eye(P))
                    ins.then_inc(msgT_in_psum, 1)
                    pe.wait_ge(msgT_ready, k + 1)
                    if not first or u >= 2:
                        pe.wait_ge(y_ready, k - back(u) + 1)
                    for c in range(2):
                        ins = nc.tensor.matmul(psO[u % 2][0:P, 0:D], msgT[:, u, c, :], Wt[:, c, :],
                                               start=(c == 0), stop=(c == 1))
                    ins.then_inc(out_in_psum, 1)

            loop(pe, NIT, turn)

        @block.vector
        def _(dve):
            s = Tally(dve, start_own)
            t = Tally(dve, dve_own)
            dve.wait_ge(types_loaded, 16)
            s.done(nc.vector.tensor_copy(ty.row[:, :], types))
            s.done(nc.vector.tensor_scalar(ty.hot[:, :], ty.row[0:NTY, :], g.part[0:NTY, :], None, ALU.is_equal))
            s.done(nc.vector.tensor_copy(g.cnt[:, :, :], g.acc[:, :, D:ACCW]))
            s.done(nc.vector.reduce_sum(deg[:, :], g.cnt[:, :, :], axis=AX.X))
            s.done(nc.vector.tensor_scalar(alone[:, :], deg[:, :], 0.5, None, ALU.is_lt))
            dve.wait_ge(loaded, 64)

            def statistics(i, n):
                for u in range(NU):
                    ins = nc.vector.bn_stats(stats[:, u, :], y[:, u, :] if n == 0 else tile(X2, i * NU + u, D))
                t.done(ins)
                dve.sem_inc(waited, 1)
                for u in range(NU):
                    ins = nc.vector.bn_aggr(mv[:, u, :], stats[:, u, :])
                ins.then_inc(var_ready, 1)
                dve.wait_ge(std_ready, i * 2 + n + 1)
                t.done(nc.vector.reciprocal(rstd[:, :], std[:, :]))

            def turn(i, first):
                t.turn(i, 2 * 2 + 2)
                dve.wait_ge(v_loaded, 16 * (i + 1))
                for u in range(NU):
                    k = i * NU + u
                    if not first:
                        dve.wait_ge(msgT_in_psum, k - NU + 1)
                    nc.vector.scalar_tensor_tensor(msg[:, u, :], v0[:, u, :], alone[:, bass.ds(k, 1)],
                                                   A2[:, bass.ds(k * ACCW, D)], ALU.mult, ALU.add).then_inc(msg_ready, 1)
                for u in range(NU):
                    k = i * NU + u
                    dve.wait_ge(out_in_psum, k + 1)
                    dve.wait_ge(hb_ready, k + 1)
                    if not first:
                        dve.wait_ge(h_ready, k - NU + 1)
                    nc.vector.tensor_tensor(y[:, u, :], psO[u % 2][0:P, 0:D], hb[:, u, :], ALU.add).then_inc(y_ready, 1)
                dve.wait_ge(y_ready, i * NU + NU)
                dve.sem_inc(waited, 1)
                statistics(i, 0)
                for u in range(NU):
                    ins = nc.vector.scalar_tensor_tensor(msg[:, u, :], y[:, u, :], mv[:, u, 0:1], gab[:, :],
                                                         ALU.subtract, ALU.mult)
                t.done(ins)
                for u in range(NU):
                    k = i * NU + u
                    dve.wait_ge(xb_ready, k + 1)
                    nc.vector.scalar_tensor_tensor(tile(X2, k, D), msg[:, u, :], rstd[:, u:u + 1], xb[:, u, :],
                                                   ALU.mult, ALU.add).then_inc(x1_ready, 1)
                dve.wait_ge(x1_ready, i * NU + NU)
                dve.sem_inc(waited, 1)
                statistics(i, 1)
                for u in range(NU):
                    nc.vector.tensor_scalar(y[:, u, :], tile(X2, i * NU + u, D), mv[:, u, 0:1], rstd[:, u:u + 1],
                                            ALU.subtract, ALU.mult).then_inc(norm_ready, 1)
                t.done(nc.vector.memset(deg[:, 0:1], 0.0))

            loop(dve, NIT, turn)


def typed_project_phase(nc, g, ty, Wk, bk, Wq, bq, Wv, bv, rel_att, rel_msg, rel_pri):
    with ExitStack() as ctx:
        sb = lambda name, shape, dt: sbuf(ctx, nc, "t_" + name, shape, dt)
        sem = semaphores(ctx, nc, "t_")
        HALF = 3 * D // 2
        KC = D // 128
        Wt = sb("W", [128, KC, NTY, 3 * D], FP)
        bt = sb("b", [NTY, 3 * D], FP)
        R = sb("R", [128, 2, H // 2, NR * DK], FP)
        pri = sb("pri", [128, H // 2, NR], FP)
        hm = sb("hm", [128, 2, NTY, KC * P], FP)
        hs = sb("hs", [P, 2, D], FP)
        types = sb("types", [NTY, 2, P], FP)
        qkv = sb("qkv", [P, 2, 3 * D], FP)
        rest = sb("rest", [P, 2, D], FP)
        kvT = sb("kvT", [128, 2, 4 * P], FP)
        T = flat(g.acc[:, :, :])[:, 0:2 * NR * 2 * D].rearrange("p (s n) -> p s n", s=2)
        psH = ctx.enter_context(nc.psum_tensor("t_psH", [128, 512], FP))
        psM = [ctx.enter_context(nc.psum_tensor(f"t_psM{c}", [128, 512], FP)) for c in range(2)]
        psK = ctx.enter_context(nc.psum_tensor("t_psK", [128, 512], FP))
        psR = [ctx.enter_context(nc.psum_tensor(f"t_psR{c}", [128, 512], FP)) for c in range(4)]
        loaded = sem("loaded")
        scaled = sem("scaled")
        hs_ready = sem("hs_ready")
        hT_in_psum = sem("hT_in_psum")
        hm_ready = sem("hm_ready")
        product_ready = sem("product_ready")
        qkv_ready = sem("qkv_ready")
        q1_ready = sem("q1_ready")
        rest_ready = sem("rest_ready")
        q2_ready = sem("q2_ready")
        q3_ready = sem("q3_ready")
        kvT_in_psum = sem("kvT_in_psum")
        kvT_ready = sem("kvT_ready")
        rel_in_psum = sem("rel_in_psum")
        rel_by_dve = sem("rel_by_dve")
        rel_by_act = sem("rel_by_act")
        stored = [sem(f"stored{u}") for u in range(NU)]
        block = ctx.enter_context(nc.Block())
        H2, Q2 = flat(g.Hn[:, :, :]), g.Qs[0:P, :, :, :].rearrange("p t s d -> p (t s d)")
        table = g.kv1.rearrange("(t p r) d -> p t (r d)", p=P, r=NR)
        n_loads = 3 * (NTY + 1) + 2 * H + H

        def turns(eng, body):
            body(0, True, False)
            with eng.Fori(1, NIT - 1) as i:
                body(i, False, False)
            body(NIT - 1, False, True)

        def rel_out(s, m):
            return T[:, s, :].rearrange("p (r c h e) -> p c h r e", r=NR, c=2, h=H)[:, m // H, m % H]

        def rel_in(m):
            return psR[m % 4][0:P, 0:NR * DK].rearrange("p (r e) -> p r e", r=NR)

        @block.sync
        def _(sp):
            for n, (W, b) in enumerate(((Wq, bq), (Wk, bk), (Wv, bv))):
                for ty_ in range(NTY):
                    sp.dma_start(Wt[:, :, ty_, n * D:(n + 1) * D], W[ty_].rearrange("(c k) n -> k c n", c=KC)) \
                        .then_inc(loaded, 16)
                sp.dma_start(bt[:, n * D:(n + 1) * D], b).then_inc(loaded, 16)
            for n, rel in enumerate((rel_att, rel_msg)):
                for h in range(H):
                    sp.dma_start(R[(h % 2) * DK:(h % 2 + 1) * DK, n, h // 2, :].rearrange("d (r e) -> d r e", r=NR),
                                 rel[:, h, :, :].rearrange("r d e -> d r e")).then_inc(loaded, 16)
            for h in range(H):
                sp.dma_start(pri[(h % 2) * DK:(h % 2 + 1) * DK, h // 2, :],
                             rel_pri[:, h:h + 1].rearrange("r a -> a r").to_broadcast([DK, NR]),
                             allow_slow_non_contiguous=True).then_inc(loaded, 16)

            with sp.Fori(0, NIT) as i:
                for u in range(NU):
                    k = i * NU + u
                    sp.wait_ge(rel_by_dve, 4 * k + 4)
                    sp.wait_ge(rel_by_act, 4 * k + 4)
                    sp.dma_start(table[:, bass.ds(k, 1), :], T[:, u % 2, :].rearrange("p (a n) -> p a n", a=1)) \
                        .then_inc(stored[u], 16)
            for u in range(NU):
                sp.wait_ge(stored[u], 16 * NIT)

        def table_slot_free(eng, i, u, first):
            if u >= 2:
                eng.wait_ge(stored[u - 2], 16 * (i + 1))
            elif not first:
                eng.wait_ge(stored[(u - back(u)) % NU], 16 * i)

        @block.gpsimd
        def _(pool):
            def stage(i, u, first):
                k = i * NU + u
                if not first or u >= 2:
                    pool.wait_ge(product_ready, k - back(u) + 1)
                nc.gpsimd.tensor_copy(types[:, u % 2, :], ty.hot[:, bass.ds(k * P, P)])
                nc.gpsimd.tensor_copy(hs[:, u % 2, :], tile(H2, k, D)).then_inc(hs_ready, 1)

            def body(i, first, last):
                for u in range(NU):
                    k = i * NU + u
                    if u < NU - 1:
                        stage(i, u + 1, first)
                    elif not last:
                        stage(i + 1, 0, False)
                    pool.wait_ge(q1_ready, k + 1)
                    nc.gpsimd.tensor_tensor(rest[:, u % 2, :], qkv[:, u % 2, 0:D], Q2[:, bass.ds(k * 3 * D, D)],
                                            ALU.subtract).then_inc(rest_ready, 1)
                    pool.wait_ge(q2_ready, k + 1)
                    nc.gpsimd.tensor_tensor(Q2[:, bass.ds(k * 3 * D + 2 * D, D)], rest[:, u % 2, :],
                                            Q2[:, bass.ds(k * 3 * D + D, D)], ALU.subtract).then_inc(q3_ready, 1)

            stage(0, 0, True)
            turns(pool, body)

        @block.tensor
        def _(pe):
            pe.wait_ge(loaded, 16 * n_loads)
            pe.wait_ge(scaled, 1)

            def turn_input(i, u, first):
                k = i * NU + u
                if not (first and u == 0):
                    pe.wait_ge(hm_ready, k)
                pe.wait_ge(hs_ready, k + 1)
                for c in range(KC):
                    ins = nc.tensor.transpose(psH[:, c * P:(c + 1) * P], hs[:, u % 2, c * 128:(c + 1) * 128], g.eye(P))
                ins.then_inc(hT_in_psum, 1)

            def relate(k, s, start):
                pe.wait_ge(kvT_ready, k + 1)
                for m in range(2 * H):
                    h = m % H
                    if not start or m >= 4:
                        (pe.wait_ge(rel_by_dve, 4 * k + m // 2 - 1) if m % 2 == 0 else
                         pe.wait_ge(rel_by_act, 4 * k + m // 2 - 1))
                    rows = slice((h % 2) * DK, (h % 2 + 1) * DK)
                    col = (m // H) * 2 + h // 2
                    nc.tensor.matmul(psR[m % 4][0:P, 0:NR * DK], kvT[rows, s, col * P:(col + 1) * P],
                                     R[rows, m // H, h // 2, :], start=True, stop=True).then_inc(rel_in_psum, 1)

            def body(i, first, last):
                for u in range(NU):
                    k = i * NU + u
                    pe.wait_ge(hm_ready, k + 1)
                    if not (first and u == 0):
                        pe.wait_ge(qkv_ready, k)
                    for b in range(2):
                        cols = slice(b * HALF, (b + 1) * HALF)
                        nc.tensor.matmul(psM[b][0:P, 0:HALF], types[:, u % 2, :], bt[:, cols],
                                         start=True, stop=False)
                        for n in range(NTY):
                            for c in range(KC):
                                ins = nc.tensor.matmul(psM[b][0:P, 0:HALF], hm[:, u % 2, n, c * P:(c + 1) * P],
                                                       Wt[:, c, n, cols], start=False,
                                                       stop=(n == NTY - 1 and c == KC - 1))
                    ins.then_inc(product_ready, 1)
                    if not (first and u == 0):
                        relate(k - 1, 1 if u in (2, 4) else 0, first and u == 1)
                    if u < NU - 1:
                        turn_input(i, u + 1, first)
                    elif not last:
                        turn_input(i + 1, 0, False)
                    pe.wait_ge(qkv_ready, k + 1)
                    if not (first and u == 0):
                        pe.wait_ge(kvT_ready, k)
                    for c in range(4):
                        ins = nc.tensor.transpose(psK[:, c * P:(c + 1) * P],
                                                  qkv[:, u % 2, D + c * 128:D + (c + 1) * 128], g.eye(P))
                    ins.then_inc(kvT_in_psum, 1)

            turn_input(0, 0, True)
            turns(pe, body)
            relate(NT - 1, 0, False)

        @block.vector
        def _(dve):
            dve.wait_ge(loaded, 16 * n_loads)
            for n in range(H // 2):
                keys = R[:, 0, n, :].rearrange("d (r e) -> d r e", r=NR)
                ins = nc.vector.scalar_tensor_tensor(keys, keys, DK ** -0.5, pri[:, n, :].unsqueeze(2).to_broadcast([128, NR, DK]),
                                                     ALU.mult, ALU.mult)
            ins.then_inc(scaled, 1)

            def mask(i, u, first):
                k = i * NU + u
                dve.wait_ge(hT_in_psum, k + 1)
                if not first or u >= 2:
                    dve.wait_ge(product_ready, k - back(u) + 1)
                row = ty.row[:, bass.ds(k * P, P)].unsqueeze(1).to_broadcast([128, KC, P])
                for n in range(NTY):
                    ins = nc.vector.scalar_tensor_tensor(hm[:, u % 2, n, :].rearrange("p (c n) -> p c n", c=KC), row,
                                                         float(n), psH[:, 0:KC * P].rearrange("p (c n) -> p c n", c=KC),
                                                         ALU.is_equal, ALU.mult)
                ins.then_inc(hm_ready, 1)

            def related(i, u, first):
                k = i * NU + u
                table_slot_free(dve, i, u, first)
                for j in range(4):
                    dve.wait_ge(rel_in_psum, 8 * k + 2 * j + 1)
                    nc.vector.tensor_copy(rel_out(u % 2, 2 * j), rel_in(2 * j)).then_inc(rel_by_dve, 1)

            def body(i, first, last):
                for u in range(NU):
                    k = i * NU + u
                    if u > 0:
                        related(i, u - 1, first)
                    elif not first:
                        related(i - 1, NU - 1, False)
                    if u < NU - 1:
                        mask(i, u + 1, first)
                    elif not last:
                        mask(i + 1, 0, False)
                    dve.wait_ge(kvT_in_psum, k + 1)
                    if not first or u >= 2:
                        dve.wait_ge(rel_in_psum, 8 * (k - back(u)) + 8)
                    nc.vector.tensor_copy(kvT[:, u % 2, :], psK[:, 0:4 * P]).then_inc(kvT_ready, 1)

            mask(0, 0, True)
            turns(dve, body)
            related(NIT - 1, NU - 1, False)

        @block.scalar
        def _(act):
            def related(i, u, first):
                k = i * NU + u
                table_slot_free(act, i, u, first)
                for j in range(4):
                    act.wait_ge(rel_in_psum, 8 * k + 2 * j + 2)
                    nc.scalar.copy(rel_out(u % 2, 2 * j + 1), rel_in(2 * j + 1)).then_inc(rel_by_act, 1)

            def body(i, first, last):
                for u in range(NU):
                    k = i * NU + u
                    act.wait_ge(product_ready, k + 1)
                    if not first or u >= 2:
                        act.wait_ge(q3_ready, k - back(u) + 1)
                        act.wait_ge(kvT_in_psum, k - back(u) + 1)
                    for b in range(2):
                        ins = nc.scalar.copy(qkv[:, u % 2, b * HALF:(b + 1) * HALF], psM[b][0:P, 0:HALF])
                    ins.then_inc(qkv_ready, 1)
                    act.wait_ge(qkv_ready, k + 1)
                    nc.scalar.copy(Q2[:, bass.ds(k * 3 * D, D)], qkv[:, u % 2, 0:D]).then_inc(q1_ready, 1)
                    if u > 0:
                        related(i, u - 1, first)
                    elif not first:
                        related(i - 1, NU - 1, False)
                    act.wait_ge(rest_ready, k + 1)
                    nc.scalar.copy(Q2[:, bass.ds(k * 3 * D + D, D)], rest[:, u % 2, :]).then_inc(q2_ready, 1)

            turns(act, body)
            related(NIT - 1, NU - 1, False)


def layer1_output_phase(nc, g, ty, Wa, ba, skip, ln_g, ln_b, out):
    with ExitStack() as ctx:
        sb = lambda name, shape, dt: sbuf(ctx, nc, "f_" + name, shape, dt)
        sem = semaphores(ctx, nc, "f_")
        KC = D // 128
        Wt = sb("W", [128, KC, NTY, D], FP)
        bt = sb("b", [NTY, D], FP)
        gb = sb("gb", [NTY, 2 * D], FP)
        gate = sb("gate", [NTY, 1], FP)
        some = sb("some", [P, NT, NR], FP)
        nrel = sb("nrel", [P, NT], FP)
        rn = sb("rn", [P, NT], FP)
        has = sb("has", [P, NT], FP)
        alone = sb("alone", [P, NT], FP)
        alpha = sb("alpha", [P, NT], FP)
        keep = sb("keep", [P, NT], FP)
        types = sb("types", [NTY, NU, P], FP)
        agg = sb("agg", [P, NU, D], FP)
        free = g.Qs[:, :, :, :].rearrange("p t s d -> p (t s d)").bitcast(FP)
        n_am = NU * NTY * KC * P
        am = free[:, 0:n_am].rearrange("p (u n m) -> p u n m", u=NU, n=NTY)
        hk = sb("hk", [P, NU, D], FP)
        hx = sb("hx", [P, NU, D], FP)
        y = free[0:P, n_am:n_am + NU * D].rearrange("p (u d) -> p u d", u=NU)
        z = free[0:P, n_am + NU * D:n_am + 2 * NU * D].rearrange("p (u d) -> p u d", u=NU)
        stats = sb("stats", [P, NU, 6], FP)
        mv = sb("mv", [P, NU, 2], FP)
        std = sb("std", [P, NU], FP)
        rstd = sb("rstd", [P, NU], FP)
        psT = [ctx.enter_context(nc.psum_tensor(f"f_psT{s}", [128, 512], FP)) for s in range(2)]
        psO = [ctx.enter_context(nc.psum_tensor(f"f_psO{s}", [128, 512], FP)) for s in range(2)]
        psG = [ctx.enter_context(nc.psum_tensor(f"f_psG{s}", [128, 512], FP)) for s in range(2)]
        psA = ctx.enter_context(nc.psum_tensor("f_psA", [128, 512], FP))
        loaded = sem("loaded")
        skip_exp = sem("skip_exp")
        gate_ready = sem("gate_ready")
        alpha_in_psum = sem("alpha_in_psum")
        scalars_ready = sem("scalars_ready")
        types_ready = sem("types_ready")
        agg_ready = sem("agg_ready")
        hk_ready = sem("hk_ready")
        hx_ready = sem("hx_ready")
        aggT_in_psum = sem("aggT_in_psum")
        am_ready = sem("am_ready")
        out_in_psum = sem("out_in_psum")
        gb_in_psum = sem("gb_in_psum")
        y_ready = sem("y_ready")
        var_ready = sem("var_ready")
        std_ready = sem("std_ready")
        scaled = sem("scaled")
        z_ready = sem("z_ready")
        result_ready = sem("result_ready")
        stored = sem("stored")
        waited = sem("waited")
        start_own = sem("start_own")
        dve_own = sem("dve_own")
        block = ctx.enter_context(nc.Block())
        X2, H2, A2 = flat(g.X1[:, :, :]), flat(g.Hn[:, :, :]), flat(g.acc[:, :, :])
        outt = out.rearrange("(t p) d -> p t d", p=P)

        @block.sync
        def _(sp):
            for n in range(NTY):
                sp.dma_start(Wt[:, :, n, :], Wa[n].rearrange("(c k) n -> k c n", c=KC)).then_inc(loaded, 16)
            sp.dma_start(bt[:, :], ba).then_inc(loaded, 16)
            sp.dma_start(gb[:, 0:D], ln_g).then_inc(loaded, 16)
            sp.dma_start(gb[:, D:2 * D], ln_b).then_inc(loaded, 16)
            sp.dma_start(gate[:, :], skip.rearrange("(n a) -> n a", a=1)).then_inc(loaded, 16)

            with sp.Fori(0, NIT) as i:
                sp.wait_ge(result_ready, i * NU + NU)
                sp.dma_start(outt[:, bass.ds(i * NU, NU), :], z[:, :, :]).then_inc(stored, 16)
            sp.wait_ge(stored, 16 * NIT)

        @block.gpsimd
        def _(pool):
            def turn(i, first):
                for u in range(NU):
                    k = i * NU + u
                    if not first:
                        pool.wait_ge(gb_in_psum, k - NU + 1)
                    nc.gpsimd.tensor_copy(types[:, u, :], ty.hot[:, bass.ds(k * P, P)]).then_inc(types_ready, 1)

            loop(pool, NIT, turn)

        @block.scalar
        def _(act):
            act.wait_ge(loaded, 16 * (NTY + 4))
            nc.scalar.activation(gate[:, :], gate[:, :], ACT.Exp, scale=-1.0).then_inc(skip_exp, 1)
            act.wait_ge(scalars_ready, 1)

            def turn(i, first):
                for u in range(NU):
                    k = i * NU + u
                    if not first:
                        act.wait_ge(aggT_in_psum, k - NU + 1)
                        act.wait_ge(y_ready, k - NU + 1)
                    nc.scalar.activation(agg[:, u, :], A2[:, bass.ds(k * ACCW, D)], ACT.Copy,
                                         scale=rn[:, bass.ds(k, 1)]).then_inc(agg_ready, 1)
                    nc.scalar.activation(hk[:, u, :], tile(H2, k, D), ACT.Copy, scale=keep[:, bass.ds(k, 1)]) \
                        .then_inc(hk_ready, 1)
                act.wait_ge(var_ready, i + 1)
                nc.scalar.activation(std[:, :], mv[:, :, 1], ACT.Sqrt, bias=g.eps[0:P, :]).then_inc(std_ready, 1)

            loop(act, NIT, turn)

        @block.tensor
        def _(pe):
            pe.wait_ge(gate_ready, 1)
            for k in range(NT):
                ins = nc.tensor.matmul(psA[0:P, k:k + 1], ty.hot[:, k * P:(k + 1) * P], gate[:, :], start=True, stop=True)
            ins.then_inc(alpha_in_psum, 1)

            def turn(i, first):
                for u in range(NU):
                    k = i * NU + u
                    pe.wait_ge(agg_ready, k + 1)
                    if not first or u >= 2:
                        pe.wait_ge(am_ready, k - back(u) + 1)
                    for c in range(KC):
                        ins = nc.tensor.transpose(psT[u % 2][:, c * P:(c + 1) * P], agg[:, u, c * 128:(c + 1) * 128],
                                                  g.eye(P))
                    ins.then_inc(aggT_in_psum, 1)
                for u in range(NU):
                    k = i * NU + u
                    pe.wait_ge(am_ready, k + 1)
                    if not first or u >= 2:
                        pe.wait_ge(y_ready, k - back(u) + 1)
                    pe.wait_ge(types_ready, k + 1)
                    nc.tensor.matmul(psO[u % 2][0:P, 0:D], types[:, u, :], bt[:, :], start=True, stop=False)
                    for n in range(NTY):
                        for c in range(KC):
                            ins = nc.tensor.matmul(psO[u % 2][0:P, 0:D], am[:, u, n, c * P:(c + 1) * P], Wt[:, c, n, :],
                                                   start=False, stop=(n == NTY - 1 and c == KC - 1))
                    ins.then_inc(out_in_psum, 1)
                for u in range(NU):
                    k = i * NU + u
                    if not first or u >= 2:
                        pe.wait_ge(z_ready, k - back(u) + 1)
                    nc.tensor.matmul(psG[u % 2][0:P, :], types[:, u, :], gb[:, :], start=True, stop=True) \
                        .then_inc(gb_in_psum, 1)

            loop(pe, NIT, turn)

        @block.vector
        def _(dve):
            s = Tally(dve, start_own)
            t = Tally(dve, dve_own)
            dve.wait_ge(skip_exp, 1)
            s.done(nc.vector.tensor_scalar(gate[:, :], gate[:, :], 1.0, None, ALU.add))
            nc.vector.reciprocal(gate[:, :], gate[:, :]).then_inc(gate_ready, 1)
            s.done(nc.vector.tensor_scalar(some[:, :, :], g.cnt[:, :, :], 0.5, None, ALU.is_ge))
            s.done(nc.vector.reduce_sum(nrel[:, :], some[:, :, :], axis=AX.X))
            s.done(nc.vector.tensor_scalar(has[:, :], nrel[:, :], 0.5, None, ALU.is_ge))
            s.done(nc.vector.tensor_scalar(alone[:, :], has[:, :], -1.0, 1.0, ALU.mult, ALU.add))
            s.done(nc.vector.tensor_scalar(nrel[:, :], nrel[:, :], 1.0, None, ALU.max))
            s.done(nc.vector.reciprocal(rn[:, :], nrel[:, :]))
            dve.wait_ge(alpha_in_psum, 1)
            s.done(nc.vector.tensor_copy(alpha[:, :], psA[0:P, 0:NT]))
            nc.vector.tensor_scalar(keep[:, :], alpha[:, :], -1.0, 1.0, ALU.mult, ALU.add).then_inc(scalars_ready, 1)

            def turn(i, first):
                t.turn(i, 3)
                for u in range(NU):
                    k = i * NU + u
                    dve.wait_ge(aggT_in_psum, k + 1)
                    if not first:
                        dve.wait_ge(out_in_psum, k - NU + 1)
                    row = ty.row[:, bass.ds(k * P, P)].unsqueeze(1).to_broadcast([128, KC, P])
                    for n in range(NTY):
                        ins = nc.vector.scalar_tensor_tensor(am[:, u, n, :].rearrange("p (c n) -> p c n", c=KC), row,
                                                             float(n),
                                                             psT[u % 2][:, 0:KC * P].rearrange("p (c n) -> p c n", c=KC),
                                                             ALU.is_equal, ALU.mult)
                    ins.then_inc(am_ready, 1)
                for u in range(NU):
                    k = i * NU + u
                    dve.wait_ge(out_in_psum, k + 1)
                    dve.wait_ge(hk_ready, k + 1)
                    nc.vector.scalar_tensor_tensor(y[:, u, :], psO[u % 2][0:P, 0:D], alpha[:, bass.ds(k, 1)], hk[:, u, :],
                                                   ALU.mult, ALU.add).then_inc(y_ready, 1)
                for u in range(NU):
                    k = i * NU + u
                    nc.vector.scalar_tensor_tensor(hx[:, u, :], tile(H2, k, D), alone[:, bass.ds(k, 1)], tile(X2, k, D),
                                                   ALU.mult, ALU.add).then_inc(hx_ready, 1)
                dve.wait_ge(y_ready, i * NU + NU)
                dve.sem_inc(waited, 1)
                for u in range(NU):
                    ins = nc.vector.bn_stats(stats[:, u, :], y[:, u, :])
                t.done(ins)
                dve.sem_inc(waited, 1)
                for u in range(NU):
                    ins = nc.vector.bn_aggr(mv[:, u, :], stats[:, u, :])
                ins.then_inc(var_ready, 1)
                dve.wait_ge(std_ready, i + 1)
                t.done(nc.vector.reciprocal(rstd[:, :], std[:, :]))
                for u in range(NU):
                    ins = nc.vector.tensor_scalar(y[:, u, :], y[:, u, :], mv[:, u, 0:1], rstd[:, u:u + 1],
                                                  ALU.subtract, ALU.mult)
                t.done(ins)
                if not first:
                    dve.wait_ge(stored, 16 * i)
                for u in range(NU):
                    k = i * NU + u
                    dve.wait_ge(gb_in_psum, k + 1)
                    nc.vector.tensor_tensor(y[:, u, :], y[:, u, :], psG[u % 2][0:P, 0:D], ALU.mult).then_inc(scaled, 1)
                    dve.wait_ge(scaled, k + 1)
                    nc.vector.tensor_tensor(z[:, u, :], y[:, u, :], psG[u % 2][0:P, D:2 * D], ALU.add).then_inc(z_ready, 1)
                    dve.wait_ge(z_ready, k + 1)
                    dve.wait_ge(hx_ready, k + 1)
                    nc.vector.scalar_tensor_tensor(z[:, u, :], z[:, u, :], has[:, bass.ds(k, 1)], hx[:, u, :],
                                                   ALU.mult, ALU.add).then_inc(result_ready, 1)

            loop(dve, NIT, turn)


def gnn(nc, x, src, dst, et6, et64, node_type, query, Wq0, bq0, Wk0, bk0, Wv0, bv0, rel_w, Wo, bo, gamma, beta,
        Wk1, bk1, Wq1, bq1, Wv1, bv1, Wa, ba, rel_pri, rel_att, rel_msg, skip, ln_g, ln_b, out):
    with ExitStack() as ctx:
        g = Persistent(ctx, nc)
        order_phase(nc, g, src, dst, et6, et64)
        setup_phase(nc, g, x)
        project_phase(nc, g, query, Wq0, bq0, Wk0, bk0, Wv0, bv0)
        with ExitStack() as edges:
            g.edge_tensors(edges, nc, 0)
            score_phase(nc, g, 0, g.kv0, rel_w)
            softmax_phase(nc, g, 0)
            aggregate_phase(nc, g, 0)
        ty = Types(ctx, nc)
        layer0_output_phase(nc, g, ty, Wo, bo, gamma, beta, node_type)
        typed_project_phase(nc, g, ty, Wk1, bk1, Wq1, bq1, Wv1, bv1, rel_att, rel_msg, rel_pri)
        with ExitStack() as edges:
            g.edge_tensors(edges, nc, 1)
            score_phase(nc, g, 1, g.kv1, None)
            softmax_phase(nc, g, 1)
            aggregate_phase(nc, g, 1)
        layer1_output_phase(nc, g, ty, Wa, ba, skip, ln_g, ln_b, out)


_INS = ['x', 'src', 'dst', 'edge_type_6', 'edge_type_64', 'node_type_3', 'L0_gnn_query_emb', 'L0_gnn_Wq', 'L0_gnn_bq',
        'L0_gnn_Wk', 'L0_gnn_bk', 'L0_gnn_Wv', 'L0_gnn_bv', 'L0_gnn_rel_w', 'L0_gnn_Wo', 'L0_gnn_bo', 'L0_gnn_gamma',
        'L0_gnn_beta', 'L1_gnn_Wk', 'L1_gnn_bk', 'L1_gnn_Wq', 'L1_gnn_bq', 'L1_gnn_Wv', 'L1_gnn_bv', 'L1_gnn_Wa',
        'L1_gnn_ba', 'L1_gnn_rel_pri', 'L1_gnn_rel_att', 'L1_gnn_rel_msg', 'L1_gnn_skip', 'L1_gnn_ln_g', 'L1_gnn_ln_b']


def kernel(**inputs):
    import numpy as _np
    import concourse.bacc as _bacc
    from concourse import mybir as _mybir
    from concourse.bass_utils import run_bass_kernel_spmd as _run

    nc = _bacc.Bacc("TRN2", target_bir_lowering=False, num_devices=1)
    arrays, args = {}, []
    for name in _INS:
        a = _np.ascontiguousarray(inputs[name])
        arrays[f"in_{name}_dram"] = a
        args.append(nc.dram_tensor(f"in_{name}_dram", a.shape, _mybir.dt.from_np(a.dtype), kind="ExternalInput").ap())
    args.append(nc.dram_tensor("out_0_dram", (N, D), _mybir.dt.float32, kind="ExternalOutput").ap())
    gnn(nc, *args)
    r = _run(nc, [arrays], core_ids=[0])
    return r.results[0]["out_0_dram"]
```

```python
import concourse.bass as bass
from concourse import mybir
from contextlib import ExitStack

FP = mybir.dt.float32
BF = mybir.dt.bfloat16
I32 = mybir.dt.int32
ALU = mybir.AluOpType
ACT = mybir.ActivationFunctionType
AX = mybir.AxisListType

N = 3125
E = 50000
D = 256
H = 4
DK = D // H
NR = 6
NREL = 64
NTY = 3
TROWS = 3 * NTY
P = 125
NT = N // P
EW = 256
NROW = -(-E // EW)
STEPS = NROW + NT - 1
Q = STEPS // 2
SLOTS = 2 * EW
U = 4
ITERS = STEPS // U
RING = 10
HOTS = 5
TILE_BIT = 5
RING_BIT = 13
BY_POOL = (2, 5, 8)
LAG = 4
NU = 5
NIT = NT // NU
ACCW = D + NR
BIG = 1.0e30
EPS = 1e-05
FAR = 4000
assert FAR >= N + P and NT * P == N and STEPS % 2 == 0 and ITERS * U == STEPS and Q <= 128
assert STEPS % RING == 0 and RING % HOTS == 0 and LAG < HOTS
assert NT * (D + NR) < 2 ** RING_BIT and RING_BIT + RING < 24 and NT < 2 ** TILE_BIT
assert 2 * NREL <= 128


class Tally:

    def __init__(self, eng, sem):
        self.eng, self.sem, self.n, self.at = eng, sem, 0, 0

    def done(self, ins):
        self.n += 1
        ins.then_inc(self.sem, 1)
        self.eng.wait_ge(self.sem, self.at + self.n)

    def turn(self, i, each):
        self.at, self.n = i * each, 0


def sbuf(ctx, nc, name, shape, dt):
    return ctx.enter_context(nc.sbuf_tensor(name, shape, dt))


def semaphores(ctx, nc, prefix):
    made = []

    def sem(name):
        made.append(nc.alloc_semaphore(prefix + name))
        return made[-1]

    def give_back():
        nc.clear_and_free_semaphores(made)
        nc.all_engine_barrier()

    ctx.callback(give_back)
    return sem


class Persistent:

    def __init__(self, ctx, nc):
        self.ident = sbuf(ctx, nc, "ident_wide", [128, 132], FP)
        self.part = sbuf(ctx, nc, "part", [128, 1], FP)
        self.negpart = sbuf(ctx, nc, "negpart", [128, 1], FP)
        self.negrel = sbuf(ctx, nc, "negrel", [128, 1], FP)
        self.iota = sbuf(ctx, nc, "iota", [128, 2 * P], FP)
        self.ones = sbuf(ctx, nc, "ones", [128, 128], FP)
        self.eps = sbuf(ctx, nc, "eps", [128, 1], FP)
        self.tiles_q = sbuf(ctx, nc, "tiles_q", [1, ITERS], I32)
        self.tiles_acc = sbuf(ctx, nc, "tiles_acc", [1, STEPS // RING + 1], I32)
        self.idx0 = sbuf(ctx, nc, "idx0", [128, STEPS, 2], I32)
        self.idx1 = sbuf(ctx, nc, "idx1", [128, STEPS, 2], I32)
        self.dcol = sbuf(ctx, nc, "dcol", [128, STEPS, 2], FP)
        self.ecol = sbuf(ctx, nc, "ecol", [128, STEPS, 2], FP)
        self.same = sbuf(ctx, nc, "same", [Q, SLOTS], BF)
        self.same_b = sbuf(ctx, nc, "same_b", [Q, SLOTS], BF)
        self.next_b = sbuf(ctx, nc, "next_b", [Q, SLOTS], BF)
        self.next_in = sbuf(ctx, nc, "next_in", [Q, SLOTS], BF)
        self.pm = sbuf(ctx, nc, "pm", [Q, SLOTS], BF)
        self.sm = sbuf(ctx, nc, "sm", [Q, SLOTS], BF)
        self.pm_b = sbuf(ctx, nc, "pm_b", [Q, SLOTS], BF)
        self.sm_b = sbuf(ctx, nc, "sm_b", [Q, SLOTS], BF)
        self.etm = sbuf(ctx, nc, "etm", [Q, NR * SLOTS], BF)
        self.whole = sbuf(ctx, nc, "whole", [32, 4, Q], FP)
        self.Hn = sbuf(ctx, nc, "Hn", [P, NT, D], FP)
        self.X1 = sbuf(ctx, nc, "X1", [P, NT, D], FP)
        self.Qs = sbuf(ctx, nc, "Qs", [128, NT, 3, D], BF)
        self.acc = sbuf(ctx, nc, "acc", [P, NT, ACCW], FP)
        self.cnt = sbuf(ctx, nc, "cnt", [P, NT, NR], FP)
        dram = lambda name, shape, dt: nc.dram_tensor(name, shape, dt, kind="Internal").ap()
        self.edges = dram("edges", [NROW, 4, EW], I32)
        self.meta = dram("meta", [STEPS, 2, EW], BF)
        self.kv0 = dram("kv0", [N, 2 * D], FP)
        self.kv1 = dram("kv1", [N * NR, 2 * D], FP)
        self.vst = dram("vst", [STEPS, 128, 2, D], FP)

    def edge_tensors(self, ctx, nc, layer):
        self.S = sbuf(ctx, nc, f"S{layer}", [128, STEPS, 2, H], FP)
        self.W = sbuf(ctx, nc, f"W{layer}", [128, STEPS, 2, H], FP)

    def eye(self, n):
        return self.ident[0:n, 1:1 + n]


def back(u):
    return {0: 1, 1: 3}.get(u, 2)


def flat(ap):
    return ap.rearrange("p a b -> p (a b)")


def tile(t2d, t, width):
    return t2d[:, bass.ds(t * width, width)]


def loop(eng, count, body):
    body(0, True)
    with eng.Fori(1, count) as i:
        body(i, False)


def turns(eng, body):
    body(0, True, False)
    with eng.Fori(1, NIT - 1) as i:
        body(i, False, False)
    body(NIT - 1, False, True)


def row_bc(vec, n):
    return vec.rearrange("(a d) -> a d", a=1).partition_broadcast(n)


def order_phase(nc, g, src, dst, et6, et64):
    with ExitStack() as ctx:
        sb = lambda name, shape, dt: sbuf(ctx, nc, "r_" + name, shape, dt)
        sem = semaphores(ctx, nc, "r_")
        OW = 400
        OP = E // OW
        QF = NROW // 2
        CROWS = 7
        CH, CHUNKS = CROWS * EW, NROW // CROWS
        GRID = 2048.0
        JB = 4
        assert OP * OW == E and CHUNKS * CROWS == NROW and NROW % 2 == 0 and CH < GRID and FAR <= 4096
        padi = sb("padi", [1, 2, EW], I32)
        here = sb("here", [OP, OW], I32)
        after = sb("after", [OP, OW], I32)
        falls = sb("falls", [OP, OW], FP)
        fall = sb("fall", [OP, 1], FP)
        ones = sb("ones", [OP, 1], FP)
        unsorted = sb("unsorted", [1, 1], I32)
        fields = sb("fields", [QF, 2, 4, EW], I32)
        fieldsT = sb("fieldsT", [QF, 4, SLOTS], I32)
        dstf = sb("dstf", [QF, SLOTS], FP)
        chunk = sb("chunk", [QF, CROWS, EW], I32)
        keys = sb("keys", [QF, CH], FP)
        place = sb("place", [QF, CH], FP)
        ahead = sb("ahead", [QF, SLOTS], FP)
        bar = sb("bar", [QF, SLOTS], FP)
        less = g.Qs[0:QF, :, :, :].rearrange("p t s d -> p (t s d)").bitcast(FP)[:, 0:JB * CH] \
            .rearrange("p (j e) -> p j e", j=JB)
        count = sb("count", [QF, JB], FP)
        rank = sb("rank", [QF, SLOTS], FP)
        row = sb("row", [QF, SLOTS], FP)
        where = sb("where", [QF, 4, SLOTS], I32)
        where1 = sb("where1", [QF, 4], I32)
        value1 = sb("value1", [QF, 4], I32)
        psF = ctx.enter_context(nc.psum_tensor("r_psF", [128, 512], FP))
        pad_ready = sem("pad_ready")
        after_padded = sem("after_padded")
        dst_loaded = sem("dst_loaded")
        edges_stored = sem("edges_stored")
        fall_ready = sem("fall_ready")
        falls_counted = sem("falls_counted")
        flag_ready = sem("flag_ready")
        fields_loaded = sem("fields_loaded")
        chunk_loaded = sem("chunk_loaded")
        places_ready = sem("places_ready")
        chunk_used = sem("chunk_used")
        where_ready = sem("where_ready")
        picked = sem("picked")
        scattered = [sem(f"scattered{a}") for a in range(4)]
        waited = sem("waited")
        pool_waited = sem("pool_waited")
        dve_own = sem("dve_own")
        turn_own = sem("turn_own")
        rank_own = sem("rank_own")
        end_own = sem("end_own")
        block = ctx.enter_context(nc.Block())
        full = NROW - 1
        rest = E - full * EW

        @block.sync
        def _(sp):
            sp.dma_start(here[:, :], dst.rearrange("(p w) -> p w", w=OW)).then_inc(dst_loaded, 16)
            sp.wait_ge(after_padded, 1)
            sp.dma_start(after[0:OP - 1, :], dst[1:1 + (OP - 1) * OW].rearrange("(p w) -> p w", w=OW)) \
                .then_inc(dst_loaded, 16)
            sp.dma_start(after[OP - 1:OP, 0:OW - 1], dst[1 + (OP - 1) * OW:E].rearrange("(p w) -> p w", p=1)) \
                .then_inc(dst_loaded, 16)
            for a, arr in enumerate((dst, src, et64, et6)):
                sp.dma_start(g.edges[0:full, a, :], arr[0:full * EW].rearrange("(r e) -> r e", e=EW)).then_inc(edges_stored, 16)
                sp.dma_start(g.edges[full:NROW, a, 0:rest], arr[full * EW:E].rearrange("(r e) -> r e", r=1)) \
                    .then_inc(edges_stored, 16)
            sp.wait_ge(pad_ready, 1)
            sp.dma_start(g.edges[full:NROW, 0, rest:EW], padi[0:1, 0, rest:EW]).then_inc(edges_stored, 16)
            sp.dma_start(g.edges[full:NROW, 1:3, rest:EW],
                         padi[0:1, 1:2, rest:EW].to_broadcast([1, 2, EW - rest])).then_inc(edges_stored, 16)
            sp.dma_start(g.edges[full:NROW, 3, rest:EW], padi[0:1, 1, rest:EW]).then_inc(edges_stored, 16)
            sp.wait_ge(edges_stored, 16 * 11)
            sp.wait_ge(flag_ready, 1)
            sort = sp.value_load(unsorted[0:1, 0:1], min_val=0, max_val=1)
            with sp.If(sort > 0):
                sp.dma_start(fields[:, :, :, :], g.edges.rearrange("(q b) a e -> q b a e", b=2)).then_inc(fields_loaded, 16)

                def load(c, first):
                    if not first:
                        sp.wait_ge(chunk_used, c)
                    sp.dma_start(chunk[:, :, :], g.edges[bass.ds(c * CROWS, CROWS), 0, :].partition_broadcast(QF)) \
                        .then_inc(chunk_loaded, 16)

                loop(sp, CHUNKS, load)

        @block.tensor
        def _(pe):
            pe.wait_ge(fall_ready, 1)
            nc.tensor.matmul(psF[0:1, 0:1], fall[:, :], ones[:, :], start=True, stop=True).then_inc(falls_counted, 1)

        @block.gpsimd
        def _(pool):
            pool.wait_ge(flag_ready, 1)
            sort = pool.value_load(unsorted[0:1, 0:1], min_val=0, max_val=1)
            with pool.If(sort > 0):
                nc.gpsimd.iota(place[:, :], pattern=[[1, CH]], base=0, channel_multiplier=0,
                               allow_small_or_imprecise_dtypes=True)
                nc.gpsimd.iota(ahead[:, :], pattern=[[1, SLOTS]], base=0, channel_multiplier=SLOTS,
                               allow_small_or_imprecise_dtypes=True).then_inc(places_ready, 1)
                pool.wait_ge(where_ready, 1)

                def scatter(j, first):
                    if not first:
                        for a in range(4):
                            pool.wait_ge(scattered[a], 16 * j)
                    nc.gpsimd.tensor_copy(where1[:, :], where[:, :, bass.ds(j, 1)].rearrange("q a e -> q (a e)")) \
                        .then_inc(picked, 1)
                    nc.gpsimd.tensor_copy(value1[:, :], fieldsT[:, :, bass.ds(j, 1)].rearrange("q a e -> q (a e)")) \
                        .then_inc(picked, 1)
                    pool.wait_ge(picked, 2 * j + 2)
                    pool.sem_inc(pool_waited, 1)
                    for a in range(4):
                        nc.gpsimd.indirect_dma_start(
                            out=g.edges.rearrange("r a (e o) -> (r a e) o", o=1),
                            out_offset=bass.IndirectOffsetOnAxis(ap=where1[:, a:a + 1], axis=0),
                            in_=value1[:, a:a + 1], in_offset=None).then_inc(scattered[a], 16)

                loop(pool, SLOTS, scatter)
                for a in range(4):
                    pool.wait_ge(scattered[a], 16 * SLOTS)

        @block.vector
        def _(dve):
            t = Tally(dve, dve_own)
            t.done(nc.vector.memset(after[:, :], FAR))
            nc.vector.memset(ones[:, :], 1.0).then_inc(after_padded, 1)
            t.done(nc.vector.memset(padi[:, 0, :], FAR))
            nc.vector.memset(padi[:, 1, :], 0).then_inc(pad_ready, 1)
            dve.wait_ge(dst_loaded, 48)
            t.done(nc.vector.tensor_tensor(falls[:, :], here[:, :], after[:, :], ALU.is_gt))
            nc.vector.reduce_sum(fall[:, :], falls[:, :], axis=AX.X).then_inc(fall_ready, 1)
            dve.wait_ge(falls_counted, 1)
            nc.vector.tensor_scalar(unsorted[:, :], psF[0:1, 0:1], 1.0, None, ALU.min).then_inc(flag_ready, 1)
            dve.wait_ge(flag_ready, 1)
            sort = dve.value_load(unsorted[0:1, 0:1], min_val=0, max_val=1)
            with dve.If(sort > 0):
                dve.wait_ge(fields_loaded, 16)
                dve.wait_ge(places_ready, 1)
                e = Tally(dve, end_own)
                for b in range(2):
                    ins = nc.vector.tensor_copy(fieldsT[:, :, b * EW:(b + 1) * EW], fields[:, b, :, :])
                e.done(ins)
                e.done(nc.vector.tensor_copy(dstf[:, :], fieldsT[:, 0, :]))
                e.done(nc.vector.tensor_scalar(place[:, :], place[:, :], 1.0 / GRID, None, ALU.mult))
                e.done(nc.vector.memset(rank[:, :], 0.0))

                def turn(c, first):
                    m = Tally(dve, turn_own)
                    m.turn(c, 4)
                    dve.wait_ge(chunk_loaded, 16 * c + 16)
                    nc.vector.tensor_tensor(keys[:, :], chunk[:, :, :].rearrange("q r e -> q (r e)"), place[:, :],
                                            ALU.add).then_inc(chunk_used, 1)
                    m.done(nc.vector.tensor_scalar(bar[:, :], ahead[:, :], 0.0, float(CH), ALU.max, ALU.min))
                    m.done(nc.vector.tensor_scalar(bar[:, :], bar[:, :], 1.0 / GRID, None, ALU.mult))
                    m.done(nc.vector.tensor_tensor(bar[:, :], bar[:, :], dstf[:, :], ALU.add))
                    m.done(nc.vector.tensor_scalar(ahead[:, :], ahead[:, :], -float(CH), None, ALU.add))
                    dve.wait_ge(chunk_used, c + 1)
                    dve.sem_inc(waited, 1)

                    with dve.Fori(0, SLOTS // JB) as j:
                        r = Tally(dve, rank_own)
                        r.turn(c * (SLOTS // JB) + j, 3)
                        r.done(nc.vector.tensor_tensor(
                            less[:, :, :], keys[:, :].unsqueeze(1).to_broadcast([QF, JB, CH]),
                            bar[:, bass.ds(j * JB, JB)].unsqueeze(2).to_broadcast([QF, JB, CH]), ALU.is_lt))
                        r.done(nc.vector.reduce_sum(count[:, :], less[:, :, :], axis=AX.X))
                        r.done(nc.vector.tensor_tensor(rank[:, bass.ds(j * JB, JB)], rank[:, bass.ds(j * JB, JB)],
                                                       count[:, :], ALU.add))

                loop(dve, CHUNKS, turn)
                e.done(nc.vector.tensor_scalar(row[:, :], rank[:, :], -(EW - 1) / 2, 1.0 / EW, ALU.add, ALU.mult))
                e.done(nc.vector.tensor_scalar(row[:, :], row[:, :], 1.5 * 2 ** 23, 1.5 * 2 ** 23, ALU.add, ALU.subtract))
                e.done(nc.vector.scalar_tensor_tensor(rank[:, :], row[:, :], 3.0 * EW, rank[:, :], ALU.mult, ALU.add))
                for a in range(4):
                    e.done(nc.vector.tensor_scalar(where[:, a, :], rank[:, :], float(a * EW), None, ALU.add))
                dve.sem_inc(where_ready, 1)


def setup_phase(nc, g, x):
    with ExitStack() as ctx:
        sb = lambda name, shape, dt: sbuf(ctx, nc, name, shape, dt)
        ps = lambda name, shape: ctx.enter_context(nc.psum_tensor(name, shape, FP))
        sem = semaphores(ctx, nc, "e_")
        lasti = sb("lasti", [1, NROW], I32)
        last = sb("last", [1, NROW], FP)
        below = sb("below", [NT, NROW], FP)
        thr = sb("thr", [NT, 1], FP)
        start = sb("start", [NT, 1], FP)
        kio = sb("kio", [NT, STEPS], FP)
        M = sb("M", [NT, STEPS], FP)
        krow = sb("krow", [Q, 2], FP)
        jcol = sb("jcol", [Q, 2], FP)
        jP = sb("jP", [Q, 2], FP)
        word_q = sb("word_q", [1, ITERS], FP)
        jlag = sb("jlag", [1, STEPS + RING + 1], FP)
        jstep = sb("jstep", [1, STEPS + RING], FP)
        word = sb("word", [1, STEPS // RING + 1], FP)
        rowi = sb("rowi", [Q, 2], I32)
        rowf = sb("rowf", [Q, 2], FP)
        ER = sb("ER", [Q, 2, 4, EW], I32)
        EF = sb("EF", [Q, 4, 2, EW], FP)
        dloc = sb("dloc", [Q, 2, EW], FP)
        valid = sb("valid", [Q, 2, EW], FP)
        key = sb("key", [Q, SLOTS], FP)
        se = sb("se", [Q, SLOTS], FP)
        ne = sb("ne", [Q, SLOTS], FP)
        metab = sb("metab", [Q, 2, 2, EW], BF)
        wbc = sb("wbc", [Q, 2, 32], FP)
        psA = ps("psA", [128, 512])
        psB = ps("psB", [128, 512])
        psC = ps("psC", [128, 512])
        psT = [ps(f"psT{n}", [128, 512]) for n in range(4)]
        const_ready = sem("const_ready")
        last_loaded = sem("last_loaded")
        last_ready = sem("last_ready")
        last_bc = sem("last_bc")
        m_ready = sem("m_ready")
        j_ready = sem("j_ready")
        rowi_ready = sem("rowi_ready")
        rows_loaded = [sem("rows_loaded0"), sem("rows_loaded1")]
        key_ready = sem("key_ready")
        key_shifted = sem("key_shifted")
        cols_in_ready = sem("cols_in_ready")
        cols_ready = sem("cols_ready")
        wbc_ready = sem("wbc_ready")
        whole_ready = sem("whole_ready")
        meta_ready = sem("meta_ready")
        meta_stored = sem("meta_stored")
        x_loaded = sem("x_loaded")
        pool_own = sem("pool_own")
        dve_own = sem("dve_own")
        block = ctx.enter_context(nc.Block())
        full = NROW - 1

        @block.gpsimd
        def _(pool):
            t = Tally(pool, pool_own)
            t.done(nc.gpsimd.memset(g.ident[:, :], 0.0))
            t.done(nc.gpsimd.affine_select(out=g.ident[:, :], in_=g.ident[:, :], compare_op=ALU.not_equal, fill=1.0,
                                           base=1, pattern=[[-1, 132]], channel_multiplier=1))
            t.done(nc.gpsimd.iota(g.part[:, :], pattern=[[0, 1]], base=0, channel_multiplier=1,
                                  allow_small_or_imprecise_dtypes=True))
            t.done(nc.gpsimd.iota(g.iota[:, :], pattern=[[0, 2], [1, P]], base=0, channel_multiplier=0,
                                  allow_small_or_imprecise_dtypes=True))
            t.done(nc.gpsimd.iota(thr[:, :], pattern=[[0, 1]], base=0, channel_multiplier=P,
                                  allow_small_or_imprecise_dtypes=True))
            t.done(nc.gpsimd.iota(kio[:, :], pattern=[[1, STEPS]], base=0, channel_multiplier=0,
                                  allow_small_or_imprecise_dtypes=True))
            nc.gpsimd.iota(krow[:, :], pattern=[[1, 2]], base=0, channel_multiplier=2,
                           allow_small_or_imprecise_dtypes=True).then_inc(const_ready, 1)
            for b in range(2):
                pool.wait_ge(rowi_ready, 1)
                nc.gpsimd.indirect_dma_start(
                    out=ER[:, b, :, :].rearrange("q a e -> q (a e)"), out_offset=None,
                    in_=g.edges.rearrange("r a e -> r (a e)"),
                    in_offset=bass.IndirectOffsetOnAxis(ap=rowi[:, b:b + 1], axis=0)).then_inc(rows_loaded[b], 16)

        @block.sync
        def _(sp):
            sp.dma_start(lasti[0:1, 0:full], g.edges[0:full, 0, EW - 1:EW].rearrange("r a -> a r"),
                         allow_slow_non_contiguous=True).then_inc(last_loaded, 16)
            sp.wait_ge(meta_ready, 1)
            for b in range(2):
                sp.dma_start(g.meta.rearrange("(q b) a e -> b q a e", b=2)[b], metab[:, b, :, :]).then_inc(meta_stored, 16)
            sp.wait_ge(meta_stored, 32)

        @block.scalar
        def _(act):
            act.dma_start(g.X1[:, :, :], x.rearrange("(t p) d -> p t d", p=P)).then_inc(x_loaded, 16)
            act.wait_ge(x_loaded, 16)

        @block.tensor
        def _(pe):
            pe.wait_ge(last_ready, 1)
            nc.tensor.matmul(psA[:, 0:NROW], g.ones[0:1, :], last[0:1, :], start=True, stop=True).then_inc(last_bc, 1)
            pe.wait_ge(m_ready, 1)
            Mb = M[:, :].rearrange("n (q b) -> n b q", b=2)
            for b in range(2):
                nc.tensor.matmul(psB[0:Q, b:b + 1], Mb[:, b, :], g.ones[0:NT, 0:1], start=True, stop=True)
            nc.tensor.matmul(psC[:, 0:STEPS], g.ones[0:NT, :], M[:, :], start=True, stop=True).then_inc(j_ready, 1)
            pe.wait_ge(key_ready, 1)
            nc.tensor.matmul(psA[0:Q, 0:1], g.ident[0:Q, 0:Q], key[:, SLOTS - 1:SLOTS], start=True, stop=True)
            nc.tensor.matmul(psA[0:Q, 1:2], g.ident[0:Q, 2:2 + Q], key[:, 0:1], start=True, stop=True) \
                .then_inc(key_shifted, 1)
            pe.wait_ge(cols_in_ready, 1)
            for n, rows in enumerate((EF[:, 1], EF[:, 0], dloc, EF[:, 3])):
                rows = rows[:, :, :]
                for b in range(2):
                    for f in range(2):
                        ins = nc.tensor.transpose(psT[n][:, (2 * b + f) * Q:(2 * b + f + 1) * Q],
                                                  rows[:, b, f * 128:f * 128 + 128], g.eye(Q))
            ins.then_inc(cols_ready, 1)
            pe.wait_ge(wbc_ready, 1)
            for n in range(2):
                ins = nc.tensor.transpose(psB[0:32, 128 * n:128 * n + Q], wbc[:, n, :], g.eye(Q))
            ins.then_inc(whole_ready, 1)

        @block.vector
        def _(dve):
            t = Tally(dve, dve_own)
            t.done(nc.vector.memset(g.ones[:, :], 1.0))
            t.done(nc.vector.memset(g.eps[:, :], EPS))
            t.done(nc.vector.memset(last[:, :], float(FAR)))
            dve.wait_ge(last_loaded, 16)
            t.done(nc.vector.tensor_copy(last[0:1, 0:full], lasti[0:1, 0:full]))
            nc.vector.memset(ne[:, :], 0.0).then_inc(last_ready, 1)
            dve.wait_ge(const_ready, 1)
            dve.wait_ge(last_bc, 1)
            t.done(nc.vector.tensor_scalar(g.negpart[:, :], g.part[:, :], -1.0, None, ALU.mult))
            t.done(nc.vector.tensor_scalar(g.negrel[:, :], g.part[:, :], float(NREL), float(NREL), ALU.is_ge, ALU.mult))
            t.done(nc.vector.tensor_tensor(g.negrel[:, :], g.negrel[:, :], g.part[:, :], ALU.subtract))
            t.done(nc.vector.tensor_scalar(below[:, :], psA[0:NT, 0:NROW], thr[:, 0:1], None, ALU.is_lt))
            t.done(nc.vector.reduce_sum(start[:, :], below[:, :], axis=AX.X))
            t.done(nc.vector.tensor_tensor(start[:, :], start[:, :], g.part[0:NT, :], ALU.add))
            nc.vector.tensor_scalar(M[:, :], kio[:, :], start[:, 0:1], None, ALU.is_ge).then_inc(m_ready, 1)
            dve.wait_ge(j_ready, 1)
            t.done(nc.vector.tensor_scalar(jcol[:, :], psB[0:Q, 0:2], -1.0, None, ALU.add))
            t.done(nc.vector.tensor_tensor(rowf[:, :], krow[:, :], jcol[:, :], ALU.subtract))
            nc.vector.tensor_copy(rowi[:, :], rowf[:, :]).then_inc(rowi_ready, 1)
            t.done(nc.vector.tensor_scalar(jP[:, :], jcol[:, :], float(P), None, ALU.mult))
            t.done(nc.vector.memset(jlag[:, :], 0.0))
            t.done(nc.vector.memset(jlag[:, LAG + STEPS:], NT - 1.0))
            t.done(nc.vector.tensor_scalar(jlag[:, LAG:LAG + STEPS], psC[0:1, 0:STEPS], -1.0, None, ALU.add))
            t.done(nc.vector.tensor_tensor(jstep[:, :], jlag[:, 1:], jlag[:, 0:-1], ALU.subtract))
            t.done(nc.vector.tensor_scalar(word[:, :], jlag[:, 0:-1:RING], float(ACCW), None, ALU.mult))
            for u in range(1, RING):
                t.done(nc.vector.scalar_tensor_tensor(word[:, :], jstep[:, u - 1::RING], 2.0 ** (RING_BIT + u - 1),
                                                      word[:, :], ALU.mult, ALU.add))
            t.done(nc.vector.tensor_copy(g.tiles_acc[:, :], word[:, :]))
            t.done(nc.vector.tensor_copy(word_q[:, :], jlag[:, LAG:LAG + STEPS:U]))
            for u in range(1, U):
                t.done(nc.vector.scalar_tensor_tensor(word_q[:, :], jstep[:, LAG + u - 1:LAG + STEPS:U],
                                                      2.0 ** (TILE_BIT + u - 1), word_q[:, :], ALU.mult, ALU.add))
            t.done(nc.vector.tensor_copy(g.tiles_q[:, :], word_q[:, :]))
            for b in range(2):
                dve.wait_ge(rows_loaded[b], 16)
                t.done(nc.vector.tensor_copy(EF[:, :, b, :], ER[:, b, :, :]))
            for b in range(2):
                t.done(nc.vector.tensor_scalar(dloc[:, b, :], EF[:, 0, b, :], jP[:, b:b + 1], None, ALU.subtract))
            t.done(nc.vector.tensor_scalar(valid[:, :, :], dloc[:, :, :], 0.0, None, ALU.is_ge))
            t.done(nc.vector.scalar_tensor_tensor(valid[:, :, :], dloc[:, :, :], float(P - 1), valid[:, :, :],
                                                  ALU.is_le, ALU.mult))
            t.done(nc.vector.tensor_copy(metab[:, :, 0, :], dloc[:, :, :]))
            nc.vector.tensor_copy(metab[:, :, 1, :], EF[:, 2, :, :]).then_inc(meta_ready, 1)
            kv = key[:, :].rearrange("q (b e) -> q b e", b=2)
            t.done(nc.vector.scalar_tensor_tensor(kv, EF[:, 0, :, :], 2.0, valid[:, :, :], ALU.add, ALU.mult))
            t.done(nc.vector.tensor_scalar(key[:, :], key[:, :], -1.0, None, ALU.add))
            nc.vector.memset(se[:, 0:1], 0.0).then_inc(key_ready, 1)
            t.done(nc.vector.scalar_tensor_tensor(EF[:, 0, :, :], EF[:, 1, :, :], float(NR), EF[:, 3, :, :],
                                                  ALU.mult, ALU.add))
            nc.vector.memset(wbc[:, :, :], 0.0).then_inc(cols_in_ready, 1)
            for r in range(NR):
                er = EF[:, 3, :, :].rearrange("q b e -> q (b e)")
                t.done(nc.vector.tensor_scalar(g.etm[:, r * SLOTS:(r + 1) * SLOTS], er, float(r), None, ALU.is_equal))
            dve.wait_ge(key_shifted, 1)
            t.done(nc.vector.tensor_tensor(se[:, 1:SLOTS], key[:, 1:SLOTS], key[:, 0:SLOTS - 1], ALU.is_equal))
            t.done(nc.vector.tensor_tensor(se[:, 0:1], psA[0:Q, 0:1], key[:, 0:1], ALU.is_equal))
            t.done(nc.vector.tensor_copy(ne[:, 0:SLOTS - 1], se[:, 1:SLOTS]))
            t.done(nc.vector.tensor_copy(g.next_in[:, :], ne[:, :]))
            t.done(nc.vector.tensor_tensor(ne[:, SLOTS - 1:SLOTS], psA[0:Q, 1:2], key[:, SLOTS - 1:SLOTS], ALU.is_equal))
            t.done(nc.vector.tensor_copy(g.same[:, :], se[:, :]))
            t.done(nc.vector.tensor_scalar(g.same_b[:, :], se[:, :], BIG, -BIG, ALU.mult, ALU.add))
            t.done(nc.vector.tensor_scalar(g.next_b[:, :], ne[:, :], BIG, -BIG, ALU.mult, ALU.add))
            t.done(nc.vector.tensor_tensor_scan(g.pm[:, :], se[:, :], se[:, :], 1.0, ALU.mult, ALU.min))
            t.done(nc.vector.tensor_tensor_scan(g.sm[:, ::-1], ne[:, ::-1], ne[:, ::-1], 1.0, ALU.mult, ALU.min))
            t.done(nc.vector.tensor_scalar(g.pm_b[:, :], g.pm[:, :], BIG, -BIG, ALU.mult, ALU.add))
            t.done(nc.vector.tensor_scalar(g.sm_b[:, :], g.sm[:, :], BIG, -BIG, ALU.mult, ALU.add))
            t.done(nc.vector.tensor_copy(wbc[:, 0, :], g.pm[:, SLOTS - 1:SLOTS].to_broadcast([Q, 32])))
            nc.vector.tensor_copy(wbc[:, 1, :], g.sm[:, 0:1].to_broadcast([Q, 32])).then_inc(wbc_ready, 1)
            dve.wait_ge(cols_ready, 1)
            for n, col in enumerate((g.idx0, g.idx1, g.dcol, g.ecol)):
                t.done(nc.vector.tensor_copy(col[:, :, :].rearrange("p (q b) f -> p b f q", b=2),
                                             psT[n][:, 0:4 * Q].rearrange("p (b f q) -> p b f q", b=2, f=2)))
            dve.wait_ge(whole_ready, 1)
            whole = psB[0:32, 0:256].rearrange("p (n q) -> p n q", n=2)[:, :, 0:Q]
            t.done(nc.vector.tensor_copy(g.whole[:, 0:2, :], whole))
            t.done(nc.vector.tensor_scalar(g.whole[:, 2:4, :], whole, BIG, -BIG, ALU.mult, ALU.add))


def project_phase(nc, g, query, Wq, bq, Wk, bk, Wv, bv):
    with ExitStack() as ctx:
        sb = lambda name, shape, dt: sbuf(ctx, nc, name, shape, dt)
        sem = semaphores(ctx, nc, "")
        Wt = sb("p_W", [128, 2, 3, D], FP)
        bias = sb("p_bias", [P, 3 * D], FP)
        qe = sb("p_qe", [P, D], FP)
        stats = sb("p_stats", [P, NU, 6], FP)
        mv = sb("p_mv", [P, NU, 2], FP)
        std = sb("p_std", [P, NU], FP)
        rstd = sb("p_rstd", [P, NU], FP)
        norm = sb("p_norm", [P, NU, D], FP)
        enh = sb("p_enh", [P, NU, D], FP)
        enhT = sb("p_enhT", [128, NU, 2, P], FP)
        qkv = sb("p_qkv", [P, NU, 3 * D], FP)
        rest = sb("p_rest", [P, NU, D], FP)
        psT = [ctx.enter_context(nc.psum_tensor(f"p_psT{s}", [128, 512], FP)) for s in range(2)]
        psM = [[ctx.enter_context(nc.psum_tensor(f"p_psM{s}{c}", [128, 512], FP)) for c in range(2)] for s in range(2)]
        w_loaded = sem("p_w_loaded")
        var_ready = sem("p_var_ready")
        std_ready = sem("p_std_ready")
        norm_ready = sem("p_norm_ready")
        h_ready = sem("p_h_ready")
        enh_ready = sem("p_enh_ready")
        enhT_in_psum = sem("p_enhT_in_psum")
        enhT_ready = sem("p_enhT_ready")
        product_ready = sem("p_product_ready")
        qkv_ready = sem("p_qkv_ready")
        q1_ready = sem("p_q1_ready")
        rest_ready = sem("p_rest_ready")
        q2_ready = sem("p_q2_ready")
        q3_ready = sem("p_q3_ready")
        kv_stored = [sem(f"p_kv_stored{u}") for u in range(NU)]
        waited = sem("p_waited")
        query_ready = sem("p_query_ready")
        dve_own = sem("p_dve_own")
        block = ctx.enter_context(nc.Block())
        HALF = 3 * D // 2
        X2, H2, Q2 = flat(g.X1[:, :, :]), flat(g.Hn[:, :, :]), g.Qs[0:P, :, :, :].rearrange("p t s d -> p (t s d)")
        kvt = g.kv0.rearrange("(t p) d -> p t d", p=P)

        @block.sync
        def _(sp):
            for n, (W, b) in enumerate(((Wq, bq), (Wk, bk), (Wv, bv))):
                sp.dma_start(Wt[:, :, n, :], W.rearrange("(c k) n -> k c n", c=2)).then_inc(w_loaded, 16)
                sp.dma_start(bias[:, n * D:(n + 1) * D], row_bc(b, P)).then_inc(w_loaded, 16)
            sp.dma_start(qe[:, :], row_bc(query, P)).then_inc(w_loaded, 16)

            with sp.Fori(0, NIT) as i:
                for u in range(NU):
                    sp.wait_ge(qkv_ready, i * NU + u + 1)
                    sp.dma_start(kvt[:, bass.ds(i * NU + u, 1), :], qkv[:, u:u + 1, D:3 * D]).then_inc(kv_stored[u], 16)
            for u in range(NU):
                sp.wait_ge(kv_stored[u], 16 * NIT)

        @block.scalar
        def _(act):
            def moments(i):
                act.wait_ge(var_ready, i + 1)
                nc.scalar.activation(std[:, :], mv[:, :, 1], ACT.Sqrt, bias=g.eps[0:P, :]).then_inc(std_ready, 1)

            def relu(i, u):
                act.wait_ge(norm_ready, i * NU + u + 1)
                nc.scalar.activation(tile(H2, i * NU + u, D), norm[:, u, :], ACT.Relu).then_inc(h_ready, 1)

            def move(i, u, first):
                k = i * NU + u
                act.wait_ge(enhT_in_psum, k + 1)
                if not first:
                    act.wait_ge(product_ready, k - NU + 1)
                nc.scalar.copy(flat(enhT[:, u, :, :]), psT[u % 2][:, 0:2 * P]).then_inc(enhT_ready, 1)

            def split(i, u):
                k = i * NU + u
                act.wait_ge(qkv_ready, k + 1)
                nc.scalar.copy(Q2[:, bass.ds(k * 3 * D, D)], qkv[:, u, 0:D]).then_inc(q1_ready, 1)
                act.wait_ge(rest_ready, k + 1)
                nc.scalar.copy(Q2[:, bass.ds(k * 3 * D + D, D)], rest[:, u, :]).then_inc(q2_ready, 1)

            def turn(i, first, last):
                if not last:
                    moments(i + 1)
                for u in range(NU):
                    if not last:
                        relu(i + 1, u)
                    if u < NU - 1:
                        move(i, u + 1, first)
                    elif not last:
                        move(i + 1, 0, False)
                    split(i, u)

            moments(0)
            for u in range(NU):
                relu(0, u)
            move(0, 0, True)
            turn(0, True, False)
            with act.Fori(1, NIT - 1) as i:
                turn(i, False, False)
            turn(NIT - 1, False, True)

        @block.gpsimd
        def _(pool):
            with pool.Fori(0, NIT) as i:
                for u in range(NU):
                    k = i * NU + u
                    pool.wait_ge(q1_ready, k + 1)
                    nc.gpsimd.tensor_tensor(rest[:, u, :], qkv[:, u, 0:D], Q2[:, bass.ds(k * 3 * D, D)],
                                            ALU.subtract).then_inc(rest_ready, 1)
                    pool.wait_ge(q2_ready, k + 1)
                    nc.gpsimd.tensor_tensor(Q2[:, bass.ds(k * 3 * D + 2 * D, D)], rest[:, u, :],
                                            Q2[:, bass.ds(k * 3 * D + D, D)], ALU.subtract).then_inc(q3_ready, 1)

        @block.vector
        def _(dve):
            t = Tally(dve, dve_own)
            LN = 2

            def moments(i):
                t.turn(i, LN)
                for u in range(NU):
                    ins = nc.vector.bn_stats(stats[:, u, :], tile(X2, i * NU + u, D))
                t.done(ins)
                dve.sem_inc(waited, 1)
                for u in range(NU):
                    ins = nc.vector.bn_aggr(mv[:, u, :], stats[:, u, :])
                ins.then_inc(var_ready, 1)
                dve.wait_ge(std_ready, i + 1)
                t.done(nc.vector.reciprocal(rstd[:, :], std[:, :]))

            def normalise(i, u, first):
                k = i * NU + u
                if not first:
                    dve.wait_ge(h_ready, k - NU + 1)
                nc.vector.tensor_scalar(norm[:, u, :], tile(X2, k, D), mv[:, u, 0:1], rstd[:, u:u + 1],
                                        ALU.subtract, ALU.mult).then_inc(norm_ready, 1)
                dve.wait_ge(norm_ready, k + 1)
                if not first:
                    dve.wait_ge(enhT_in_psum, k - NU + 1)
                nc.vector.scalar_tensor_tensor(enh[:, u, :], norm[:, u, :], 0.0, qe[:, :], ALU.max,
                                               ALU.add).then_inc(enh_ready, 1)

            def move(i, u, first):
                k = i * NU + u
                dve.wait_ge(product_ready, k + 1)
                if not first:
                    dve.wait_ge(kv_stored[u], 16 * i)
                    dve.wait_ge(q3_ready, k - NU + 1)
                for c in range(2):
                    cols = slice(c * HALF, (c + 1) * HALF)
                    ins = nc.vector.tensor_tensor(qkv[:, u, cols], psM[u % 2][c][0:P, 0:HALF], bias[:, cols], ALU.add)
                ins.then_inc(qkv_ready, 1)

            def turn(i, first, last):
                if not last:
                    moments(i + 1)
                for u in range(NU):
                    if not last:
                        normalise(i + 1, u, False)
                    move(i, u, first)

            dve.wait_ge(w_loaded, 16 * 7)
            nc.vector.tensor_scalar(qe[:, :], qe[:, :], 0.1, None, ALU.mult).then_inc(query_ready, 1)
            dve.wait_ge(query_ready, 1)
            moments(0)
            for u in range(NU):
                normalise(0, u, True)
            turn(0, True, False)
            with dve.Fori(1, NIT - 1) as i:
                turn(i, False, False)
            turn(NIT - 1, False, True)

        @block.tensor
        def _(pe):
            pe.wait_ge(w_loaded, 16 * 7)

            def turn_input(i, u, first):
                k = i * NU + u
                pe.wait_ge(enh_ready, k + 1)
                if not first or u >= 2:
                    pe.wait_ge(enhT_ready, k - back(u) + 1)
                for c in range(2):
                    ins = nc.tensor.transpose(psT[u % 2][:, c * P:(c + 1) * P], enh[:, u, c * 128:(c + 1) * 128],
                                              g.eye(P))
                ins.then_inc(enhT_in_psum, 1)

            def project(i, first, last):
                for u in range(NU):
                    k = i * NU + u
                    if u < NU - 1:
                        turn_input(i, u + 1, first)
                    elif not last:
                        turn_input(i + 1, 0, False)
                    pe.wait_ge(enhT_ready, k + 1)
                    if not first or u >= 2:
                        pe.wait_ge(qkv_ready, k - back(u) + 1)
                    for b in range(2):
                        for c in range(2):
                            ins = nc.tensor.matmul(psM[u % 2][b][0:P, 0:HALF], enhT[:, u, c, :],
                                                   Wt[:, c, :, :].rearrange("k n d -> k (n d)")[:, b * HALF:(b + 1) * HALF],
                                                   start=(c == 0), stop=(c == 1))
                    ins.then_inc(product_ready, 1)

            turn_input(0, 0, True)
            turns(pe, project)


def score_phase(nc, g, layer, table, rel_w):
    L = f"s{layer}_"
    with ExitStack() as ctx:
        sb = lambda name, shape, dt: sbuf(ctx, nc, L + name, shape, dt)
        sem = semaphores(ctx, nc, L)
        parts = 2 if layer == 0 else 1
        kv = sb("kv", [128, U, 2, 2 * D], FP)
        idx = sb("idx", [128, U, 2], I32)
        meta1 = sb("meta1", [1, U, parts * EW], BF)
        ones1 = sb("ones1", [1, 128], BF)
        dist = sb("dist", [128, U, parts * EW], BF)
        hot = sb("hot", [128, U, parts * EW], BF)
        keyr = sb("keyr", [128, 2, 2 * D], FP) if layer == 0 else None
        prod = sb("prod", [128, 2, 2 * D], FP)
        relf = sb("relf", [2 * NREL, DK], FP) if layer == 0 else None
        relp = sb("relp", [2 * NREL, 3, DK], BF) if layer == 0 else None
        rel = sb("rel", [2 * NREL, 2, D], BF) if layer == 0 else None
        psQ = [ctx.enter_context(nc.psum_tensor(f"{L}psQ{s}", [128, 512], FP)) for s in range(2)]
        psR = [ctx.enter_context(nc.psum_tensor(f"{L}psR{s}", [128, 512], FP)) for s in range(2)]
        psB = [ctx.enter_context(nc.psum_tensor(f"{L}psB{s}", [128, 512], FP)) for s in range(2)]
        gathered = [sem(f"gathered{u}") for u in range(U)]
        meta_loaded = [sem(f"meta_loaded{u}") for u in range(U)]
        v_stored = [sem(f"v_stored{u}") for u in range(U)]
        idx_ready = sem("idx_ready")
        waited = sem("waited")
        ones_ready = sem("ones_ready")
        meta_spread = sem("meta_spread")
        dist_ready = sem("dist_ready")
        hot_ready = sem("hot_ready")
        query_ready = sem("query_ready")
        key_read = sem("key_read")
        prod_ready = sem("prod_ready")
        score_ready = sem("score_ready")
        rel_loaded = sem("rel_loaded")
        rel_ready = sem("rel_ready")
        dve_own = sem("dve_own")
        block = ctx.enter_context(nc.Block())
        idx_all = flat((g.idx0 if layer == 0 else g.idx1)[:, :, :])
        meta2 = g.meta.rearrange("k a e -> k (a e)")
        S2 = g.S[:, :, :, :].rearrange("p k f h -> p (k f h)")
        Q2 = g.Qs[0:P, :, :, :].rearrange("p t s d -> p (t s d)")
        vst = g.vst.rearrange("k p f d -> p k f d")

        @block.gpsimd
        def _(pool):
            def place(i, u, first):
                k = i * U + u
                if not first:
                    pool.wait_ge(gathered[u], 32 * i)
                nc.gpsimd.tensor_copy(idx[:, u, :], idx_all[:, bass.ds(k * 2, 2)]).then_inc(idx_ready, 1)

            def gather(i, first, last):
                for u in range(U):
                    k = i * U + u
                    if u + 1 < U:
                        place(i, u + 1, first)
                    elif not last:
                        place(i + 1, 0, False)
                    if not first:
                        pool.wait_ge(v_stored[u], 16 * i)
                        pool.wait_ge(key_read if layer == 0 else prod_ready, k - U + 1)
                    pool.wait_ge(idx_ready, k + 1)
                    pool.sem_inc(waited, 1)
                    for f in range(2):
                        nc.gpsimd.indirect_dma_start(
                            out=kv[:, u, f, :], out_offset=None, in_=table[:, :],
                            in_offset=bass.IndirectOffsetOnAxis(ap=idx[:, u, f:f + 1], axis=0)).then_inc(gathered[u], 16)

            place(0, 0, True)
            gather(0, True, False)
            with pool.Fori(1, ITERS - 1) as i:
                gather(i, False, False)
            gather(ITERS - 1, False, True)

        @block.sync
        def _(sp):
            if layer == 0:
                for n in range(2):
                    sp.dma_start(relf[n * NREL:(n + 1) * NREL, :], rel_w).then_inc(rel_loaded, 16)

            def load_meta(i, u, first):
                if not first:
                    sp.wait_ge(meta_spread, i * U + u - U + 1)
                sp.dma_start(meta1[:, u, :], meta2[bass.ds(i * U + u, 1), 0:parts * EW]).then_inc(meta_loaded[u], 16)

            def move(i, last):
                for u in range(U):
                    if not last:
                        load_meta(i + 1, u, False)
                    sp.wait_ge(gathered[u], 32 * (i + 1))
                    sp.dma_start(vst[:, bass.ds(i * U + u, 1), :, :].rearrange("p k f d -> p (k f) d"),
                                 kv[:, u, :, D:2 * D]).then_inc(v_stored[u], 16)

            for u in range(U):
                load_meta(0, u, True)
            with sp.Fori(0, ITERS - 1) as i:
                move(i, False)
            move(ITERS - 1, True)
            for u in range(U):
                sp.wait_ge(v_stored[u], 16 * ITERS)

        @block.scalar
        def _(act):
            def one_hot(i, first):
                for u in range(U):
                    k = i * U + u
                    act.wait_ge(meta_spread, k + 1)
                    if not first:
                        act.wait_ge(hot_ready, k - U + 1)
                    if layer == 0:
                        nc.scalar.activation(dist[:, u, EW:2 * EW], psB[u % 2][:, EW:2 * EW], ACT.Abs, bias=g.negrel[:, :])
                    nc.scalar.activation(dist[:, u, 0:EW], psB[u % 2][:, 0:EW], ACT.Abs, bias=g.negpart[:, :]) \
                        .then_inc(dist_ready, 1)
                    act.wait_ge(dist_ready, k + 1)
                    if not first:
                        act.wait_ge(query_ready, k - U + 1)
                    nc.scalar.activation(hot[:, u, :], dist[:, u, :], ACT.Relu, bias=g.ones[:, 0:1], scale=-1.0) \
                        .then_inc(hot_ready, 1)

            loop(act, ITERS, one_hot)

        @block.tensor
        def _(pe):
            pe.wait_ge(ones_ready, 1)
            if layer == 0:
                pe.wait_ge(rel_ready, 1)

            def spread(i, u, first):
                pe.wait_ge(meta_loaded[u], 16 * (i + 1))
                if not first or u >= 2:
                    pe.wait_ge(dist_ready, i * U + u - 1)
                nc.tensor.matmul(psB[u % 2][:, 0:parts * EW], ones1[:, :], meta1[:, u, :], start=True, stop=True) \
                    .then_inc(meta_spread, 1)

            def look_up(i, first, last):
                word = pe.value_load(g.tiles_q[0:1, bass.ds(i, 1)], min_val=0, max_val=2 ** (TILE_BIT + U))
                tiles = [(word & (2 ** TILE_BIT - 1)).with_bounds(min_val=0, max_val=NT - 1)]
                for u in range(1, U):
                    tiles.append((tiles[-1] + ((word >> (TILE_BIT + u - 1)) & 1)).with_bounds(min_val=0, max_val=NT - 1))
                for u in range(U):
                    k = i * U + u
                    if u + 2 < U:
                        spread(i, u + 2, first)
                    elif not last:
                        spread(i + 1, u + 2 - U, False)
                    pe.wait_ge(hot_ready, k + 1)
                    if not first or u >= 2:
                        pe.wait_ge(prod_ready, k - 1)
                    for f in range(2):
                        cols = slice(f * 128, f * 128 + 128)
                        if layer == 0:
                            rcols = slice(EW + f * 128, EW + f * 128 + 128)
                            nc.tensor.matmul(psR[u % 2][:, f * D:(f + 1) * D], hot[:, u, rcols], rel[:, 0, :],
                                             start=True, stop=False)
                            nc.tensor.matmul(psR[u % 2][:, f * D:(f + 1) * D], hot[0:NREL, u, rcols], rel[0:NREL, 1, :],
                                             start=False, stop=True)
                        for s in range(3):
                            ins = nc.tensor.matmul(psQ[u % 2][:, f * D:(f + 1) * D], hot[0:P, u, cols],
                                                   Q2[:, bass.ds(tiles[u] * (3 * D) + s * D, D)],
                                                   start=(s == 0), stop=(s == 2))
                    ins.then_inc(query_ready, 1)

            for u in range(2):
                spread(0, u, True)
            look_up(0, True, False)
            with pe.Fori(1, ITERS - 1) as i:
                look_up(i, False, False)
            look_up(ITERS - 1, False, True)

        @block.vector
        def _(dve):
            nc.vector.memset(ones1[:, :], 1.0).then_inc(ones_ready, 1)
            if layer == 0:
                t = Tally(dve, dve_own)
                dve.wait_ge(rel_loaded, 32)
                t.done(nc.vector.tensor_scalar(relf[:, :], relf[:, :], 0.2, None, ALU.mult))
                for s in range(3):
                    t.done(nc.vector.tensor_copy(relp[:, s, :], relf[:, :]))
                    if s < 2:
                        t.done(nc.vector.tensor_tensor(relf[:, :], relf[:, :], relp[:, s, :], ALU.subtract))
                for h in range(H):
                    head = slice(h * DK, (h + 1) * DK)
                    nc.vector.tensor_copy(rel[0:NREL, 0, head], relp[0:NREL, 0, :])
                    nc.vector.tensor_copy(rel[NREL:2 * NREL, 0, head], relp[NREL:2 * NREL, 1, :])
                    ins = nc.vector.tensor_copy(rel[:, 1, head], relp[:, 2, :])
                ins.then_inc(rel_ready, 1)

            def score(i, first):
                for u in range(U):
                    k = i * U + u
                    s = u % 2
                    keys = kv[:, u, :, 0:D]
                    dve.wait_ge(gathered[u], 32 * (i + 1))
                    dve.wait_ge(query_ready, k + 1)
                    q = psQ[s][:, :].rearrange("p (f d) -> p f d", f=2)
                    k3 = keyr[:, s, :].rearrange("p (f d) -> p f d", f=2) if layer == 0 else None
                    p3 = prod[:, s, :].rearrange("p (f d) -> p f d", f=2)
                    if layer == 0:
                        nc.vector.tensor_tensor(k3, keys, psR[s][:, :].rearrange("p (f d) -> p f d", f=2), ALU.add) \
                            .then_inc(key_read, 1)
                        dve.wait_ge(key_read, k + 1)
                        nc.vector.tensor_tensor(p3, k3, q, ALU.mult).then_inc(prod_ready, 1)
                        dve.wait_ge(prod_ready, k + 1)
                    else:
                        nc.vector.tensor_tensor(p3, keys, q, ALU.mult).then_inc(prod_ready, 1)
                        dve.wait_ge(prod_ready, k + 1)
                    nc.vector.reduce_sum(S2[:, bass.ds(k * 2 * H, 2 * H)],
                                         prod[:, s, :].rearrange("p (c e) -> p c e", e=DK), axis=AX.X) \
                        .then_inc(score_ready, 1)

            loop(dve, ITERS, score)


def softmax_phase(nc, g, layer):
    L = f"m{layer}_"
    rels = NR if layer == 1 else 1
    cols = H * rels
    XS, FS = 4, 2
    with ExitStack() as ctx:
        sb = lambda name, shape, dt: sbuf(ctx, nc, L + name, shape, dt)
        sem = semaphores(ctx, nc, L)
        row = lambda h: slice(h * SLOTS, (h + 1) * SLOTS)
        sc = sb("sc", [Q, H * SLOTS], FP)
        sel = sb("sel", [Q, H * SLOTS], FP)
        fwd = sb("fwd", [Q, FS, SLOTS], FP)
        etm_b = sb("etm_b", [Q, NR * SLOTS], BF) if layer == 1 else None
        ends = sb("ends", [Q, 2, 32], FP)
        endsT = sb("endsT", [32, 2, Q], FP)
        carry = sb("carry", [32, 2, Q + 2], FP)
        into = sb("into", [Q, 2, 32], FP)
        in_q = 16
        qs = g.Qs[0:Q, :, :, :].rearrange("p t s d -> p (t s d)").bitcast(FP)
        seg_tensors = [(sel[:, :], cols)] if layer == 0 else [(qs[:, 0:in_q * SLOTS], in_q),
                                                             (flat(g.acc[0:Q, :, :])[:, 0:(cols - in_q) * SLOTS], cols - in_q)]
        masked = flat(g.acc[0:Q, :, :])[:, (cols - in_q) * SLOTS:(cols - in_q + XS) * SLOTS] \
            .rearrange("q (x e) -> q x e", x=XS) if layer == 1 else None
        psS = [ctx.enter_context(nc.psum_tensor(f"{L}psS{h}", [128, 512], FP)) for h in range(H)]
        psE = ctx.enter_context(nc.psum_tensor(f"{L}psE", [128, 512], FP))
        psI = ctx.enter_context(nc.psum_tensor(f"{L}psI", [128, 512], FP))
        psW = [ctx.enter_context(nc.psum_tensor(f"{L}psW{n}", [128, 512], FP)) for n in range(2)]
        rows_ready = sem("rows_ready")
        scores_ready = sem("scores_ready")
        zeroed = sem("zeroed")
        bias_ready = sem("bias_ready")
        masked_ready = sem("masked_ready")
        fwd_ready = sem("fwd_ready")
        seg_ready = sem("seg_ready")
        after_in = sem("after_in")
        before_in = sem("before_in")
        selected = sem("selected")
        ends_ready = sem("ends_ready")
        ends_turned = sem("ends_turned")
        carry_ready = sem("carry_ready")
        carry_turned = sem("carry_turned")
        shifted = sem("shifted")
        exp_ready = sem("exp_ready")
        inverted = sem("inverted")
        weights_ready = sem("weights_ready")
        w_turned = sem("w_turned")
        w_moved = sem("w_moved")
        dve_own = sem("dve_own")
        block = ctx.enter_context(nc.Block())
        Sv = g.S[:, :, :, :].rearrange("p (q b) f h -> p h b f q", b=2)
        Wv = g.W[:, :, :, :].rearrange("p (q b) f h -> p h b f q", b=2)

        def seg(c):
            if layer == 1 and c >= in_q:
                return seg_tensors[1][0][:, (c - in_q) * SLOTS:(c - in_q + 1) * SLOTS]
            return seg_tensors[0][0][:, c * SLOTS:(c + 1) * SLOTS]

        def source(c):
            return masked[:, c % XS, :] if layer == 1 else sc[:, row(c)]

        @block.tensor
        def _(pe):
            for h in range(H):
                for b in range(2):
                    for f in range(2):
                        n = 2 * b + f
                        ins = nc.tensor.transpose(psS[h][0:Q, n * 128:(n + 1) * 128], Sv[:, h, b, f, :], g.eye(128))
                ins.then_inc(rows_ready, 1)
            for turn in range(2):
                pe.wait_ge(ends_ready, turn + 1)
                for n in range(2):
                    ins = nc.tensor.transpose(psE[0:32, n * 128:n * 128 + Q], ends[:, n, :], g.eye(Q))
                ins.then_inc(ends_turned, 1)
                pe.wait_ge(carry_ready, turn + 1)
                for n in range(2):
                    ins = nc.tensor.transpose(psI[0:Q, n * 32:(n + 1) * 32], carry[:, n, 1:1 + Q], g.eye(32))
                ins.then_inc(carry_turned, 1)
            for h in range(H):
                pe.wait_ge(weights_ready, h + 1)
                if h >= 2:
                    pe.wait_ge(w_moved, h - 1)
                for n in range(4):
                    ins = nc.tensor.transpose(psW[h % 2][:, n * Q:(n + 1) * Q],
                                              sc[:, h * SLOTS + n * 128:h * SLOTS + (n + 1) * 128], g.eye(Q))
                ins.then_inc(w_turned, 1)

        @block.scalar
        def _(act):
            for h in range(H):
                act.wait_ge(rows_ready, h + 1)
                nc.scalar.activation(sc[:, row(h)], psS[h][0:Q, :], ACT.Copy, scale=DK ** -0.5 if layer == 0 else 1.0) \
                    .then_inc(scores_ready, 1)
            for h in range(H):
                act.wait_ge(shifted, h + 1)
                nc.scalar.activation(sc[:, row(h)], sel[:, row(h)], ACT.Exp).then_inc(exp_ready, 1)
            for h in range(H):
                act.wait_ge(w_turned, h + 1)
                nc.scalar.copy(Wv[:, h], psW[h % 2][:, 0:4 * Q].rearrange("p (b f q) -> p b f q", b=2, f=2)) \
                    .then_inc(w_moved, 1)

        if layer == 0:
            @block.gpsimd
            def _(pool):
                nc.gpsimd.memset(flat(g.acc[:, :, :]), 0.0).then_inc(zeroed, 1)
                pool.wait_ge(zeroed, 1)
        else:
            @block.gpsimd
            def _(pool):
                pool.wait_ge(bias_ready, 1)
                for kind in range(2):
                    for c in range(cols):
                        h, r = c // NR, c % NR
                        pool.wait_ge(exp_ready if kind else scores_ready, h + 1)
                        n = kind * cols + c
                        if n >= XS:
                            pool.wait_ge(fwd_ready, n - XS + 1)
                        nc.gpsimd.tensor_tensor(masked[:, c % XS, :], sc[:, row(h)], (g.etm if kind else etm_b)[:, row(r)],
                                                ALU.mult if kind else ALU.add).then_inc(masked_ready, 1)

        @block.vector
        def _(dve):
            t = Tally(dve, dve_own)

            def reduce_rows(kind):
                def back_scan(c):
                    dve.wait_ge(fwd_ready, kind * cols + c + 1)
                    if kind == 0:
                        ins = nc.vector.tensor_tensor_scan(seg(c)[:, ::-1], g.next_b[:, ::-1], fwd[:, c % FS, ::-1], -BIG,
                                                           ALU.add, ALU.max)
                    else:
                        ins = nc.vector.tensor_tensor_scan(seg(c)[:, ::-1], g.next_in[:, ::-1], fwd[:, c % FS, ::-1], 0.0,
                                                           ALU.mult, ALU.max)
                    ins.then_inc(seg_ready, 1)

                for c in range(cols):
                    if layer == 1:
                        dve.wait_ge(masked_ready, kind * cols + c + 1)
                    else:
                        dve.wait_ge(exp_ready if kind else scores_ready, c + 1)
                    if kind * cols + c >= FS:
                        dve.wait_ge(seg_ready, kind * cols + c - FS + 1)
                    if kind == 0:
                        ins = nc.vector.tensor_tensor_scan(fwd[:, c % FS, :], g.same_b[:, :], source(c), -BIG,
                                                           ALU.add, ALU.max)
                    else:
                        ins = nc.vector.tensor_tensor_scan(fwd[:, c % FS, :], g.same[:, :], source(c), 0.0,
                                                           ALU.mult, ALU.add)
                    ins.then_inc(fwd_ready, 1)
                    if c > 0:
                        back_scan(c - 1)
                back_scan(cols - 1)

            def carries(kind):
                least = 0.0 if kind else -BIG
                op = (ALU.mult, ALU.add) if kind else (ALU.add, ALU.max)
                w = 0 if kind else 2
                dve.wait_ge(seg_ready, (kind + 1) * cols)
                at = 0
                for tensor, n in seg_tensors:
                    by_column = tensor.rearrange("q (c e) -> q c e", e=SLOTS)
                    for end in range(2):
                        ins = nc.vector.tensor_copy(ends[:, end, at:at + n], by_column[:, :, end * (SLOTS - 1)])
                    at += n
                ins.then_inc(ends_ready, 1)
                t.done(nc.vector.memset(carry[:, :, :], least))
                dve.wait_ge(ends_turned, kind + 1)
                t.done(nc.vector.tensor_copy(endsT[:, :, :],
                                             psE[0:32, 0:256].rearrange("c (n q) -> c n q", n=2)[:, :, 0:Q]))
                t.done(nc.vector.tensor_tensor_scan(carry[:, 0, 0:Q][:, ::-1], g.whole[:, w + 1, ::-1], endsT[:, 0, ::-1],
                                                    least, op[0], op[1]))
                nc.vector.tensor_tensor_scan(carry[:, 1, 2:Q + 2], g.whole[:, w, :], endsT[:, 1, :],
                                             least, op[0], op[1]).then_inc(carry_ready, 1)
                dve.wait_ge(carry_turned, kind + 1)
                t.done(nc.vector.tensor_copy(flat(into[:, :, :]), psI[0:Q, 0:64]))

            def add_carries(kind, finish):
                n0 = kind * cols
                op = (ALU.mult, ALU.add) if kind else (ALU.add, ALU.max)

                def after(c):
                    nc.vector.scalar_tensor_tensor(seg(c), (g.sm if kind else g.sm_b)[:, :], into[:, 0, c:c + 1], seg(c),
                                                   op[0], op[1]).then_inc(after_in, 1)

                def before(c):
                    dve.wait_ge(after_in, n0 + c + 1)
                    nc.vector.scalar_tensor_tensor(seg(c), (g.pm if kind else g.pm_b)[:, :], into[:, 1, c:c + 1], seg(c),
                                                   op[0], op[1]).then_inc(before_in, 1)

                def select(c):
                    h, r = c // rels, c % rels
                    dve.wait_ge(before_in, n0 + c + 1)
                    if layer == 1:
                        if r > 0:
                            dve.wait_ge(selected, n0 + c)
                            nc.vector.copy_predicated(sel[:, row(h)], g.etm[:, row(r)].bitcast(mybir.dt.uint16), seg(c)).then_inc(selected, 1)
                        else:
                            nc.vector.tensor_copy(sel[:, row(h)], seg(c)).then_inc(selected, 1)
                        if r == rels - 1:
                            dve.wait_ge(selected, n0 + c + 1)
                    if r == rels - 1:
                        finish(h)

                for c in range(cols + 2):
                    if c < cols:
                        after(c)
                    if 1 <= c <= cols:
                        before(c - 1)
                    if c >= 2:
                        select(c - 2)

            def shift(h):
                nc.vector.tensor_tensor(sel[:, row(h)], sc[:, row(h)], sel[:, row(h)], ALU.subtract).then_inc(shifted, 1)

            def divide(h):
                nc.vector.reciprocal(sel[:, row(h)], sel[:, row(h)]).then_inc(inverted, 1)
                dve.wait_ge(inverted, h + 1)
                nc.vector.tensor_tensor(sc[:, row(h)], sc[:, row(h)], sel[:, row(h)], ALU.mult).then_inc(weights_ready, 1)

            t.done(nc.vector.memset(ends[:, :, :], 0.0))
            if layer == 1:
                nc.vector.tensor_scalar(etm_b[:, :], g.etm[:, :], BIG, -BIG, ALU.mult, ALU.add).then_inc(bias_ready, 1)
            reduce_rows(0)
            carries(0)
            add_carries(0, shift)
            dve.wait_ge(exp_ready, H)
            reduce_rows(1)
            carries(1)
            add_carries(1, divide)


def aggregate_phase(nc, g, layer):
    L = f"a{layer}_"
    with ExitStack() as ctx:
        sb = lambda name, shape, dt: sbuf(ctx, nc, L + name, shape, dt)
        sem = semaphores(ctx, nc, L)
        width = ACCW if layer == 0 else D
        turns = STEPS // RING
        v = sb("v", [128, RING, 2, ACCW], FP)
        diff = sb("diff", [128, HOTS, 2, P], BF)
        dist = sb("dist", [128, HOTS, 2, P], BF)
        hot = sb("hot", [128, HOTS, 2, P], FP)
        psA = [ctx.enter_context(nc.psum_tensor(f"{L}psA{s}", [128, 512], FP)) for s in range(HOTS)]
        v_loaded = [sem(f"v_loaded{u}") for u in range(RING)]
        diff_ready = sem("diff_ready")
        dist_ready = sem("dist_ready")
        hot_ready = sem("hot_ready")
        weighted_by_dve = sem("weighted_by_dve")
        weighted_by_pool = sem("weighted_by_pool")
        counts_ready = sem("counts_ready")
        sum_ready = sem("sum_ready")
        added = sem("added")
        zeroed = sem("zeroed")
        block = ctx.enter_context(nc.Block())
        vst = g.vst.rearrange("k p f d -> p k f d")
        acc2 = flat(g.acc[:, :, :])
        W3 = g.W[:, :, :, :].rearrange("p k f h -> p (k f h)")
        dcol, ecol = flat(g.dcol[:, :, :]), flat(g.ecol[:, :, :])
        iota = g.iota[:, :].rearrange("p (f n) -> p f n", f=2)

        def so_far(u, mine):
            return len([s for s in range(u) if (s in BY_POOL) == mine])

        def weigh(eng, k, u):
            rows = v[:, u, :, 0:D].rearrange("p f (h e) -> p f h e", h=H)
            return eng.tensor_tensor(rows, rows,
                                     W3[:, bass.ds(k * 2 * H, 2 * H)].rearrange("p (f h) -> p f h", f=2)
                                     .unsqueeze(3).to_broadcast([128, 2, H, DK]), ALU.mult)

        @block.sync
        def _(sp):
            def load(i, first):
                for u in range(RING):
                    k = i * RING + u
                    if not first:
                        sp.wait_ge(sum_ready, k - RING + 1)
                    sp.dma_start(v[:, u, :, 0:D], vst[:, bass.ds(k, 1), :, :].rearrange("p k f d -> p (k f) d")) \
                        .then_inc(v_loaded[u], 16)

            loop(sp, turns, load)

        @block.gpsimd
        def _(pool):
            def distance(i, first):
                for u in range(RING):
                    k = i * RING + u
                    if not first or u >= HOTS:
                        pool.wait_ge(dist_ready, k - HOTS + 1)
                    nc.gpsimd.tensor_tensor(diff[:, u % HOTS, :, :], iota,
                                            dcol[:, bass.ds(k * 2, 2)].unsqueeze(2).to_broadcast([128, 2, P]),
                                            ALU.subtract).then_inc(diff_ready, 1)
                    if u in BY_POOL:
                        pool.wait_ge(v_loaded[u], 16 * (i + 1))
                        weigh(nc.gpsimd, k, u).then_inc(weighted_by_pool, 1)

            loop(pool, turns, distance)

        @block.scalar
        def _(act):
            def one_hot(k, s, first):
                act.wait_ge(dist_ready, k + 1)
                if not first:
                    act.wait_ge(sum_ready, k - HOTS + 1)
                nc.scalar.activation(hot[:, s, :, :], dist[:, s, :, :], ACT.Relu, bias=g.ones[:, 0:1], scale=-1.0) \
                    .then_inc(hot_ready, 1)

            def turn(i, first):
                for u in range(RING):
                    k = i * RING + u
                    act.wait_ge(diff_ready, k + 1)
                    if not first or u >= HOTS:
                        act.wait_ge(hot_ready, k - HOTS + 1)
                    nc.scalar.activation(dist[:, u % HOTS, :, :], diff[:, u % HOTS, :, :], ACT.Abs) \
                        .then_inc(dist_ready, 1)
                    if not (first and u == 0):
                        one_hot(k - 1, (u - 1) % HOTS, first and u - 1 < HOTS)

            loop(act, turns, turn)
            one_hot(STEPS - 1, HOTS - 1, False)

        @block.tensor
        def _(pe):
            def add_up(i, first):
                for u in range(RING):
                    k = i * RING + u
                    pe.wait_ge(hot_ready, k + 1)
                    if u in BY_POOL:
                        pe.wait_ge(weighted_by_pool, i * len(BY_POOL) + so_far(u, True) + 1)
                        if layer == 0:
                            pe.wait_ge(counts_ready, i * len(BY_POOL) + so_far(u, True) + 1)
                    else:
                        pe.wait_ge(weighted_by_dve, i * (RING - len(BY_POOL)) + so_far(u, False) + 1)
                    if not first or u >= HOTS:
                        pe.wait_ge(added, k - HOTS + 1)
                    for f in range(2):
                        ins = nc.tensor.matmul(psA[u % HOTS][0:P, 0:width], hot[:, u % HOTS, f, :], v[:, u, f, 0:width],
                                               start=(f == 0), stop=(f == 1))
                    ins.then_inc(sum_ready, 1)

            loop(pe, turns, add_up)

        @block.vector
        def _(dve):
            if layer == 1:
                nc.vector.memset(acc2, 0.0).then_inc(zeroed, 1)
                dve.wait_ge(zeroed, 1)

            def node_tiles(i):
                most = (NT - 1) * ACCW
                word = dve.value_load(g.tiles_acc[0:1, bass.ds(i, 1)], min_val=0, max_val=2 ** (RING_BIT + RING))
                at = [(word & (2 ** RING_BIT - 1)).with_bounds(min_val=0, max_val=most)]
                for u in range(1, RING):
                    at.append((at[-1] + ((word >> (RING_BIT + u - 1)) & 1) * ACCW).with_bounds(min_val=0, max_val=most))
                return at

            def add(k, s, base, start):
                dve.wait_ge(sum_ready, k + 1)
                if not start:
                    dve.wait_ge(added, k)
                nc.vector.tensor_tensor(acc2[:, bass.ds(base, width)], acc2[:, bass.ds(base, width)],
                                        psA[s][0:P, 0:width], ALU.add).then_inc(added, 1)

            def turn(i, first):
                at = node_tiles(i)
                for u in range(RING):
                    k = i * RING + u
                    if u not in BY_POOL:
                        dve.wait_ge(v_loaded[u], 16 * (i + 1))
                    if layer == 0:
                        if u in BY_POOL and not first:
                            dve.wait_ge(sum_ready, k - RING + 1)
                        ins = nc.vector.tensor_tensor(v[:, u, :, D:ACCW], iota[:, :, 0:NR],
                                                      ecol[:, bass.ds(k * 2, 2)].unsqueeze(2).to_broadcast([128, 2, NR]),
                                                      ALU.is_equal)
                        if u in BY_POOL:
                            ins.then_inc(counts_ready, 1)
                    if u not in BY_POOL:
                        weigh(nc.vector, k, u).then_inc(weighted_by_dve, 1)
                    if not first or u >= LAG:
                        add(k - LAG, (u - LAG) % HOTS, at[u], first and u == LAG)

            loop(dve, turns, turn)
            at = node_tiles(turns)
            for u in range(LAG):
                add(STEPS - LAG + u, (RING - LAG + u) % HOTS, at[u], False)


class Types:

    def __init__(self, ctx, nc):
        self.hot = sbuf(ctx, nc, "type_hot", [TROWS, N], BF)
        self.row = sbuf(ctx, nc, "type_row", [128, N], BF)
        self.of = sbuf(ctx, nc, "type_of", [TROWS, 1], FP)
        self.later = sbuf(ctx, nc, "later", [TROWS, 2], FP)


def load_three_times(eng, tensor, rows, sem):
    for s in range(3):
        eng.dma_start(tensor[s * NTY:(s + 1) * NTY, :], rows).then_inc(sem, 16)


def split_rows(nc, t, ty, rows, out):
    t.done(nc.vector.tensor_copy(out, rows))
    for s in range(2):
        t.done(nc.vector.scalar_tensor_tensor(rows, out, ty.later[:, s:s + 1], rows, ALU.mult, ALU.add))
        t.done(nc.vector.tensor_copy(out, rows))


def layer0_output_phase(nc, g, ty, Wo, bo, gamma, beta, node_type):
    with ExitStack() as ctx:
        sb = lambda name, shape, dt: sbuf(ctx, nc, "o_" + name, shape, dt)
        sem = semaphores(ctx, nc, "o_")
        Wt = sb("W", [128, 2, D], FP)
        bob, gab, beb = sb("bo", [P, D], FP), sb("gamma", [P, D], FP), sb("beta", [P, D], FP)
        types = g.Qs[:, :, :, :].rearrange("p t s d -> p (t s d)")[:, 0:2 * N].bitcast(I32)
        deg = sb("deg", [P, NT], FP)
        alone = sb("alone", [P, NT], FP)
        v0 = sb("v0", [P, NU, D], FP)
        msg = sb("msg", [P, NU, D], FP)
        msgT = sb("msgT", [128, NU, 2, P], FP)
        hb = sb("hb", [P, NU, D], FP)
        xb = sb("xb", [P, NU, D], FP)
        y = sb("y", [P, NU, D], FP)
        stats = sb("stats", [P, NU, 6], FP)
        norm = sb("norm", [P, NU, D], FP)
        mv = sb("mv", [P, 2, NU, 2], FP)
        std = sb("std", [P, 2, NU], FP)
        rstd = sb("rstd", [P, 2, NU], FP)
        psT = [ctx.enter_context(nc.psum_tensor(f"o_psT{s}", [128, 512], FP)) for s in range(2)]
        psO = [ctx.enter_context(nc.psum_tensor(f"o_psO{s}", [128, 512], FP)) for s in range(NU)]
        loaded = sem("loaded")
        types_loaded = sem("types_loaded")
        v_loaded = sem("v_loaded")
        msg_ready = sem("msg_ready")
        msgT_in_psum = sem("msgT_in_psum")
        msgT_ready = sem("msgT_ready")
        out_in_psum = sem("out_in_psum")
        y_ready = sem("y_ready")
        hb_ready = sem("hb_ready")
        xb_ready = sem("xb_ready")
        stats_ready = [sem(f"stats_ready{n}") for n in range(2)]
        var_ready = [sem(f"var_ready{n}") for n in range(2)]
        std_ready = [sem(f"std_ready{n}") for n in range(2)]
        rstd_ready = [sem(f"rstd_ready{n}") for n in range(2)]
        gained = sem("gained")
        x1_ready = sem("x1_ready")
        norm_ready = sem("norm_ready")
        h_ready = sem("h_ready")
        waited = sem("waited")
        start_own = sem("start_own")
        block = ctx.enter_context(nc.Block())
        X2, H2, A2 = flat(g.X1[:, :, :]), flat(g.Hn[:, :, :]), flat(g.acc[:, :, :])
        v0t = g.kv0.rearrange("(t p) d -> p t d", p=P)

        @block.sync
        def _(sp):
            sp.dma_start(Wt[:, :, :], Wo.rearrange("(c k) n -> k c n", c=2)).then_inc(loaded, 16)
            for dst_, vec in ((bob, bo), (gab, gamma), (beb, beta)):
                sp.dma_start(dst_[:, :], row_bc(vec, P)).then_inc(loaded, 16)
            sp.dma_start(types, row_bc(node_type, 128)).then_inc(types_loaded, 16)

            def load(i, first):
                if not first:
                    sp.wait_ge(msg_ready, i * NU)
                sp.dma_start(v0[:, :, :], v0t[:, bass.ds(i * NU, NU), D:2 * D]).then_inc(v_loaded, 16)

            loop(sp, NIT, load)

        @block.gpsimd
        def _(pool):
            pool.wait_ge(loaded, 64)

            def add(i, first):
                for u in range(NU):
                    k = i * NU + u
                    if not first:
                        pool.wait_ge(y_ready, k - NU + 1)
                    nc.gpsimd.tensor_tensor(hb[:, u, :], tile(H2, k, D), bob[:, :], ALU.add).then_inc(hb_ready, 1)
                    if not first:
                        pool.wait_ge(x1_ready, k - NU + 1)
                    nc.gpsimd.tensor_tensor(xb[:, u, :], tile(X2, k, D), beb[:, :], ALU.add).then_inc(xb_ready, 1)

            loop(pool, NIT, add)

        @block.scalar
        def _(act):
            def deviation(i, n):
                act.wait_ge(var_ready[n], i + 1)
                nc.scalar.activation(std[:, n, :], mv[:, n, :, 1], ACT.Sqrt, bias=g.eps[0:P, :]).then_inc(std_ready[n], 1)

            def relu(i):
                for u in range(NU):
                    k = i * NU + u
                    act.wait_ge(norm_ready, k + 1)
                    nc.scalar.activation(tile(H2, k, D), norm[:, u, :], ACT.Relu).then_inc(h_ready, 1)

            def move(i, first):
                for u in range(NU):
                    k = i * NU + u
                    act.wait_ge(msgT_in_psum, k + 1)
                    if not first:
                        act.wait_ge(out_in_psum, k - NU + 1)
                    nc.scalar.copy(flat(msgT[:, u, :, :]), psT[u % 2][:, 0:2 * P]).then_inc(msgT_ready, 1)

            def turn(i, first, last):
                if not first:
                    deviation(i - 1, 1)
                deviation(i, 0)
                if not first:
                    relu(i - 1)
                if not last:
                    move(i + 1, False)

            move(0, True)
            turns(act, turn)
            deviation(NIT - 1, 1)
            relu(NIT - 1)

        @block.tensor
        def _(pe):
            pe.wait_ge(loaded, 64)

            def turn_input(k, u, first):
                pe.wait_ge(msg_ready, k + 1)
                if not first or u >= 2:
                    pe.wait_ge(msgT_ready, k - back(u) + 1)
                for c in range(2):
                    ins = nc.tensor.transpose(psT[u % 2][:, c * P:(c + 1) * P], msg[:, u, c * 128:(c + 1) * 128],
                                              g.eye(P))
                ins.then_inc(msgT_in_psum, 1)

            def turn(i, first):
                turn_input(i * NU, 0, first)
                for u in range(NU):
                    k = i * NU + u
                    if u < NU - 1:
                        turn_input(k + 1, u + 1, first)
                    pe.wait_ge(msgT_ready, k + 1)
                    if not first:
                        pe.wait_ge(y_ready, k - NU + 1)
                    for c in range(2):
                        ins = nc.tensor.matmul(psO[u][0:P, 0:D], msgT[:, u, c, :], Wt[:, c, :],
                                               start=(c == 0), stop=(c == 1))
                    ins.then_inc(out_in_psum, 1)

            loop(pe, NIT, turn)

        @block.vector
        def _(dve):
            s = Tally(dve, start_own)
            dve.wait_ge(types_loaded, 16)
            s.done(nc.vector.tensor_copy(ty.row[:, :], types))
            part = g.part[0:TROWS, :]
            for n in range(2):
                s.done(nc.vector.tensor_scalar(ty.later[:, n:n + 1], part, (n + 1.0) * NTY, -1.0, ALU.is_ge, ALU.mult))
            s.done(nc.vector.scalar_tensor_tensor(ty.of[:, :], ty.later[:, 0:1], float(NTY), part, ALU.mult, ALU.add))
            s.done(nc.vector.scalar_tensor_tensor(ty.of[:, :], ty.later[:, 1:2], float(NTY), ty.of[:, :],
                                                  ALU.mult, ALU.add))
            s.done(nc.vector.tensor_scalar(ty.hot[:, :], ty.row[0:TROWS, :], ty.of[:, :], None, ALU.is_equal))
            s.done(nc.vector.tensor_copy(g.cnt[:, :, :], g.acc[:, :, D:ACCW]))
            s.done(nc.vector.reduce_sum(deg[:, :], g.cnt[:, :, :], axis=AX.X))
            s.done(nc.vector.tensor_scalar(alone[:, :], deg[:, :], 0.5, None, ALU.is_lt))
            dve.wait_ge(loaded, 64)

            def messages(i, first):
                dve.wait_ge(v_loaded, 16 * (i + 1))
                for u in range(NU):
                    k = i * NU + u
                    if not first:
                        dve.wait_ge(msgT_in_psum, k - NU + 1)
                    nc.vector.scalar_tensor_tensor(msg[:, u, :], v0[:, u, :], alone[:, bass.ds(k, 1)],
                                                   A2[:, bass.ds(k * ACCW, D)], ALU.mult, ALU.add).then_inc(msg_ready, 1)

            def moments(i, n, rows, ready):
                dve.wait_ge(ready, i * NU + NU)
                dve.sem_inc(waited, 1)
                for u in range(NU):
                    ins = nc.vector.bn_stats(stats[:, u, :], rows(u))
                ins.then_inc(stats_ready[n], 1)
                dve.wait_ge(stats_ready[n], i + 1)
                dve.sem_inc(waited, 1)
                for u in range(NU):
                    ins = nc.vector.bn_aggr(mv[:, n, u, :], stats[:, u, :])
                ins.then_inc(var_ready[n], 1)

            def invert(i, n):
                dve.wait_ge(std_ready[n], i + 1)
                nc.vector.reciprocal(rstd[:, n, :], std[:, n, :]).then_inc(rstd_ready[n], 1)
                dve.wait_ge(rstd_ready[n], i + 1)

            def normalise(i, first):
                invert(i, 1)
                for u in range(NU):
                    k = i * NU + u
                    if not first:
                        dve.wait_ge(h_ready, k - NU + 1)
                    nc.vector.tensor_scalar(norm[:, u, :], tile(X2, k, D), mv[:, 1, u, 0:1], rstd[:, 1, u:u + 1],
                                            ALU.subtract, ALU.mult).then_inc(norm_ready, 1)

            def turn(i, number):
                for u in range(NU):
                    k = i * NU + u
                    dve.wait_ge(out_in_psum, k + 1)
                    dve.wait_ge(hb_ready, k + 1)
                    nc.vector.tensor_tensor(y[:, u, :], psO[u][0:P, 0:D], hb[:, u, :], ALU.add).then_inc(y_ready, 1)
                moments(i, 0, lambda u: y[:, u, :], y_ready)
                if number != 0:
                    normalise(i - 1, number == 1)
                if number != NIT - 1:
                    messages(i + 1, False)
                invert(i, 0)
                for u in range(NU):
                    nc.vector.scalar_tensor_tensor(y[:, u, :], y[:, u, :], mv[:, 0, u, 0:1], gab[:, :],
                                                   ALU.subtract, ALU.mult).then_inc(gained, 1)
                for u in range(NU):
                    k = i * NU + u
                    dve.wait_ge(gained, k + 1)
                    dve.wait_ge(xb_ready, k + 1)
                    nc.vector.scalar_tensor_tensor(tile(X2, k, D), y[:, u, :], rstd[:, 0, u:u + 1], xb[:, u, :],
                                                   ALU.mult, ALU.add).then_inc(x1_ready, 1)
                moments(i, 1, lambda u: tile(X2, i * NU + u, D), x1_ready)

            messages(0, True)
            turn(0, 0)
            turn(1, 1)
            with dve.Fori(2, NIT - 1) as i:
                turn(i, None)
            turn(NIT - 1, NIT - 1)
            normalise(NIT - 1, False)


def typed_project_phase(nc, g, ty, Wk, bk, Wq, bq, Wv, bv, rel_att, rel_msg, rel_pri):
    with ExitStack() as ctx:
        sb = lambda name, shape, dt: sbuf(ctx, nc, "t_" + name, shape, dt)
        sem = semaphores(ctx, nc, "t_")
        HALF = 3 * D // 2
        KC = D // 128
        Wt = sb("W", [128, KC, NTY, 3 * D], FP)
        bt = sb("b", [TROWS, 3 * D], FP)
        btp = sb("b_parts", [TROWS, 3 * D], BF)
        R = sb("R", [128, 2, H // 2, NR * DK], FP)
        pri = sb("pri", [128, H // 2, NR], FP)
        hm = sb("hm", [128, 2, NTY, KC * P], FP)
        types = sb("types", [TROWS, 2, P], BF)
        hs = sb("hs", [P, 2, D], FP)
        qkv = sb("qkv", [P, 2, 3 * D], FP)
        rest = sb("rest", [P, 2, D], FP)
        kvT = sb("kvT", [128, 2, 4 * P], FP)
        T = flat(g.acc[:, :, :])[:, 0:2 * NR * 2 * D].rearrange("p (s n) -> p s n", s=2)
        psH = ctx.enter_context(nc.psum_tensor("t_psH", [128, 512], FP))
        psM = [ctx.enter_context(nc.psum_tensor(f"t_psM{c}", [128, 512], FP)) for c in range(2)]
        psK = ctx.enter_context(nc.psum_tensor("t_psK", [128, 512], FP))
        psR = [ctx.enter_context(nc.psum_tensor(f"t_psR{c}", [128, 512], FP)) for c in range(4)]
        loaded = sem("loaded")
        bias_loaded = sem("bias_loaded")
        bias_ready = sem("bias_ready")
        rel_loaded = sem("rel_loaded")
        scaled = sem("scaled")
        start_own = sem("start_own")
        hs_ready = sem("hs_ready")
        hT_in_psum = sem("hT_in_psum")
        hm_ready = sem("hm_ready")
        product_ready = sem("product_ready")
        qkv_ready = sem("qkv_ready")
        q1_ready = sem("q1_ready")
        rest_ready = sem("rest_ready")
        q2_ready = sem("q2_ready")
        q3_ready = sem("q3_ready")
        kvT_in_psum = sem("kvT_in_psum")
        kvT_ready = sem("kvT_ready")
        rel_in_psum = sem("rel_in_psum")
        rel_by_dve = sem("rel_by_dve")
        rel_by_act = sem("rel_by_act")
        stored = [sem(f"stored{u}") for u in range(NU)]
        block = ctx.enter_context(nc.Block())
        H2, Q2 = flat(g.Hn[:, :, :]), g.Qs[0:P, :, :, :].rearrange("p t s d -> p (t s d)")
        table = g.kv1.rearrange("(t p r) d -> p t (r d)", p=P, r=NR)

        def rel_out(s, m):
            return T[:, s, :].rearrange("p (r c h e) -> p c h r e", r=NR, c=2, h=H)[:, m // H, m % H]

        def rel_in(m):
            return psR[m % 4][0:P, 0:NR * DK].rearrange("p (r e) -> p r e", r=NR)

        @block.sync
        def _(sp):
            for n, (W, b) in enumerate(((Wq, bq), (Wk, bk), (Wv, bv))):
                for c in range(KC):
                    sp.dma_start(Wt[:, c, :, n * D:(n + 1) * D], W[:, c * 128:(c + 1) * 128, :].rearrange("t k n -> k t n")) \
                        .then_inc(loaded, 16)
                load_three_times(sp, bt[:, n * D:(n + 1) * D], b, bias_loaded)
            for n, rel in enumerate((rel_att, rel_msg)):
                for h in range(H):
                    sp.dma_start(R[(h % 2) * DK:(h % 2 + 1) * DK, n, h // 2, :].rearrange("d (r e) -> d r e", r=NR),
                                 rel[:, h, :, :].rearrange("r d e -> d r e")).then_inc(rel_loaded, 16)
            for h in range(H):
                sp.dma_start(pri[(h % 2) * DK:(h % 2 + 1) * DK, h // 2, :],
                             rel_pri[:, h:h + 1].rearrange("r a -> a r").to_broadcast([DK, NR]),
                             allow_slow_non_contiguous=True).then_inc(rel_loaded, 16)

            with sp.Fori(0, NIT) as i:
                for u in range(NU):
                    k = i * NU + u
                    sp.wait_ge(rel_by_dve, 4 * k + 4)
                    sp.wait_ge(rel_by_act, 4 * k + 4)
                    sp.dma_start(table[:, bass.ds(k, 1), :], T[:, u % 2, :].rearrange("p (a n) -> p a n", a=1)) \
                        .then_inc(stored[u], 16)
            for u in range(NU):
                sp.wait_ge(stored[u], 16 * NIT)

        def table_slot_free(eng, i, u, first):
            if u >= 2:
                eng.wait_ge(stored[u - 2], 16 * (i + 1))
            elif not first:
                eng.wait_ge(stored[(u - back(u)) % NU], 16 * i)

        @block.gpsimd
        def _(pool):
            def stage(i, u, first):
                k = i * NU + u
                if not first or u >= 2:
                    pool.wait_ge(product_ready, k - back(u) + 1)
                nc.gpsimd.tensor_copy(types[:, u % 2, :], ty.hot[:, bass.ds(k * P, P)])
                nc.gpsimd.tensor_copy(hs[:, u % 2, :], tile(H2, k, D)).then_inc(hs_ready, 1)

            def body(i, first, last):
                for u in range(NU):
                    k = i * NU + u
                    if u < NU - 1:
                        stage(i, u + 1, first)
                    elif not last:
                        stage(i + 1, 0, False)
                    pool.wait_ge(q1_ready, k + 1)
                    nc.gpsimd.tensor_tensor(rest[:, u % 2, :], qkv[:, u % 2, 0:D], Q2[:, bass.ds(k * 3 * D, D)],
                                            ALU.subtract).then_inc(rest_ready, 1)
                    pool.wait_ge(q2_ready, k + 1)
                    nc.gpsimd.tensor_tensor(Q2[:, bass.ds(k * 3 * D + 2 * D, D)], rest[:, u % 2, :],
                                            Q2[:, bass.ds(k * 3 * D + D, D)], ALU.subtract).then_inc(q3_ready, 1)

            stage(0, 0, True)
            turns(pool, body)

        @block.tensor
        def _(pe):
            pe.wait_ge(loaded, 16 * 3 * KC)
            pe.wait_ge(bias_ready, 1)

            def turn_input(i, u, first):
                k = i * NU + u
                if not (first and u == 0):
                    pe.wait_ge(hm_ready, k)
                pe.wait_ge(hs_ready, k + 1)
                for c in range(KC):
                    ins = nc.tensor.transpose(psH[:, c * P:(c + 1) * P], hs[:, u % 2, c * 128:(c + 1) * 128], g.eye(P))
                ins.then_inc(hT_in_psum, 1)

            def relate(k, s, start):
                pe.wait_ge(kvT_ready, k + 1)
                if start:
                    pe.wait_ge(scaled, 1)
                for m in range(2 * H):
                    h = m % H
                    if not start or m >= 4:
                        (pe.wait_ge(rel_by_dve, 4 * k + m // 2 - 1) if m % 2 == 0 else
                         pe.wait_ge(rel_by_act, 4 * k + m // 2 - 1))
                    rows = slice((h % 2) * DK, (h % 2 + 1) * DK)
                    col = (m // H) * 2 + h // 2
                    nc.tensor.matmul(psR[m % 4][0:P, 0:NR * DK], kvT[rows, s, col * P:(col + 1) * P],
                                     R[rows, m // H, h // 2, :], start=True, stop=True).then_inc(rel_in_psum, 1)

            def body(i, first, last):
                for u in range(NU):
                    k = i * NU + u
                    pe.wait_ge(hm_ready, k + 1)
                    if not (first and u == 0):
                        pe.wait_ge(qkv_ready, k)
                    for b in range(2):
                        cols = slice(b * HALF, (b + 1) * HALF)
                        nc.tensor.matmul(psM[b][0:P, 0:HALF], types[:, u % 2, :], btp[:, cols],
                                         start=True, stop=False)
                        for n in range(NTY):
                            for c in range(KC):
                                ins = nc.tensor.matmul(psM[b][0:P, 0:HALF], hm[:, u % 2, n, c * P:(c + 1) * P],
                                                       Wt[:, c, n, cols], start=False,
                                                       stop=(n == NTY - 1 and c == KC - 1))
                    ins.then_inc(product_ready, 1)
                    if u < NU - 1:
                        turn_input(i, u + 1, first)
                    elif not last:
                        turn_input(i + 1, 0, False)
                    if not (first and u == 0):
                        relate(k - 1, 1 if u in (2, 4) else 0, first and u == 1)
                    pe.wait_ge(qkv_ready, k + 1)
                    if not (first and u == 0):
                        pe.wait_ge(kvT_ready, k)
                    for c in range(4):
                        ins = nc.tensor.transpose(psK[:, c * P:(c + 1) * P],
                                                  qkv[:, u % 2, D + c * 128:D + (c + 1) * 128], g.eye(P))
                    ins.then_inc(kvT_in_psum, 1)

            turn_input(0, 0, True)
            turns(pe, body)
            relate(NT - 1, 0, False)

        @block.vector
        def _(dve):
            t = Tally(dve, start_own)
            dve.wait_ge(bias_loaded, 16 * 9)
            split_rows(nc, t, ty, bt[:, :], btp[:, :])
            dve.sem_inc(bias_ready, 1)

            def scale():
                dve.wait_ge(rel_loaded, 16 * 3 * H)
                for n in range(H // 2):
                    keys = R[:, 0, n, :].rearrange("d (r e) -> d r e", r=NR)
                    ins = nc.vector.scalar_tensor_tensor(keys, keys, DK ** -0.5,
                                                         pri[:, n, :].unsqueeze(2).to_broadcast([128, NR, DK]),
                                                         ALU.mult, ALU.mult)
                ins.then_inc(scaled, 1)

            def mask(i, u, first):
                k = i * NU + u
                dve.wait_ge(hT_in_psum, k + 1)
                if not first or u >= 2:
                    dve.wait_ge(product_ready, k - back(u) + 1)
                row = ty.row[:, bass.ds(k * P, P)].unsqueeze(1).to_broadcast([128, KC, P])
                for n in range(NTY):
                    ins = nc.vector.scalar_tensor_tensor(hm[:, u % 2, n, :].rearrange("p (c n) -> p c n", c=KC), row,
                                                         float(n), psH[:, 0:KC * P].rearrange("p (c n) -> p c n", c=KC),
                                                         ALU.is_equal, ALU.mult)
                ins.then_inc(hm_ready, 1)

            def related(i, u, first):
                k = i * NU + u
                table_slot_free(dve, i, u, first)
                for j in range(4):
                    dve.wait_ge(rel_in_psum, 8 * k + 2 * j + 1)
                    nc.vector.tensor_copy(rel_out(u % 2, 2 * j), rel_in(2 * j)).then_inc(rel_by_dve, 1)

            def body(i, first, last):
                for u in range(NU):
                    k = i * NU + u
                    if u < NU - 1:
                        mask(i, u + 1, first)
                    elif not last:
                        mask(i + 1, 0, False)
                    if u > 0:
                        related(i, u - 1, first)
                    elif not first:
                        related(i - 1, NU - 1, False)
                    dve.wait_ge(kvT_in_psum, k + 1)
                    if not first or u >= 2:
                        dve.wait_ge(rel_in_psum, 8 * (k - back(u)) + 8)
                    nc.vector.tensor_copy(kvT[:, u % 2, :], psK[:, 0:4 * P]).then_inc(kvT_ready, 1)

            mask(0, 0, True)
            scale()
            turns(dve, body)
            related(NIT - 1, NU - 1, False)

        @block.scalar
        def _(act):
            def related(i, u, first):
                k = i * NU + u
                table_slot_free(act, i, u, first)
                for j in range(4):
                    act.wait_ge(rel_in_psum, 8 * k + 2 * j + 2)
                    nc.scalar.copy(rel_out(u % 2, 2 * j + 1), rel_in(2 * j + 1)).then_inc(rel_by_act, 1)

            def body(i, first, last):
                for u in range(NU):
                    k = i * NU + u
                    act.wait_ge(product_ready, k + 1)
                    if not first or u >= 2:
                        act.wait_ge(q3_ready, k - back(u) + 1)
                        act.wait_ge(kvT_in_psum, k - back(u) + 1)
                    for b in range(2):
                        ins = nc.scalar.copy(qkv[:, u % 2, b * HALF:(b + 1) * HALF], psM[b][0:P, 0:HALF])
                    ins.then_inc(qkv_ready, 1)
                    act.wait_ge(qkv_ready, k + 1)
                    nc.scalar.copy(Q2[:, bass.ds(k * 3 * D, D)], qkv[:, u % 2, 0:D]).then_inc(q1_ready, 1)
                    if u > 0:
                        related(i, u - 1, first)
                    elif not first:
                        related(i - 1, NU - 1, False)
                    act.wait_ge(rest_ready, k + 1)
                    nc.scalar.copy(Q2[:, bass.ds(k * 3 * D + D, D)], rest[:, u % 2, :]).then_inc(q2_ready, 1)

            turns(act, body)
            related(NIT - 1, NU - 1, False)


def layer1_output_phase(nc, g, ty, Wa, ba, skip, ln_g, ln_b, out):
    with ExitStack() as ctx:
        sb = lambda name, shape, dt: sbuf(ctx, nc, "f_" + name, shape, dt)
        sem = semaphores(ctx, nc, "f_")
        KC = D // 128
        Wt = sb("W", [128, KC, NTY, D], FP)
        VW = 3 * D + 1
        by_type = sb("by_type", [TROWS, VW], FP)
        parts = sb("parts", [TROWS, VW], BF)
        gate = by_type[:, 3 * D:VW]
        some = sb("some", [P, NT, NR], FP)
        nrel = sb("nrel", [P, NT], FP)
        rn = sb("rn", [P, NT], FP)
        has = sb("has", [P, NT], FP)
        alone = sb("alone", [P, NT], FP)
        alpha = sb("alpha", [P, NT], FP)
        keep = sb("keep", [P, NT], FP)
        types = sb("types", [TROWS, 2, NU, P], BF)
        agg = sb("agg", [P, NU, D], FP)
        free = g.Qs[:, :, :, :].rearrange("p t s d -> p (t s d)").bitcast(FP)
        n_am = NU * NTY * KC * P
        am = free[:, 0:n_am].rearrange("p (u n m) -> p u n m", u=NU, n=NTY)
        hk = sb("hk", [P, NU, D], FP)
        hx = sb("hx", [P, NU, D], FP)
        y, norm, z = [free[0:P, n_am + n * NU * D:n_am + (n + 1) * NU * D].rearrange("p (u d) -> p u d", u=NU)
                      for n in range(3)]
        gbs = free[0:P, n_am + 3 * NU * D:n_am + 3 * NU * D + 4 * D].rearrange("p (s d) -> p s d", s=2)
        stats = sb("stats", [P, NU, 6], FP)
        mv = sb("mv", [P, NU, 2], FP)
        std = sb("std", [P, NU], FP)
        rstd = sb("rstd", [P, NU], FP)
        psT = [ctx.enter_context(nc.psum_tensor(f"f_psT{s}", [128, 512], FP)) for s in range(2)]
        psO = [ctx.enter_context(nc.psum_tensor(f"f_psO{s}", [128, 512], FP)) for s in range(2)]
        psG = [ctx.enter_context(nc.psum_tensor(f"f_psG{s}", [128, 512], FP)) for s in range(2)]
        psA = ctx.enter_context(nc.psum_tensor("f_psA", [128, 512], FP))
        loaded = sem("loaded")
        w_loaded = sem("w_loaded")
        skip_exp = sem("skip_exp")
        gate_ready = sem("gate_ready")
        alpha_in_psum = sem("alpha_in_psum")
        scalars_ready = sem("scalars_ready")
        types_ready = [sem(f"types_ready{n}") for n in range(2)]
        agg_ready = sem("agg_ready")
        hk_ready = sem("hk_ready")
        hx_ready = sem("hx_ready")
        aggT_in_psum = sem("aggT_in_psum")
        am_ready = sem("am_ready")
        out_in_psum = sem("out_in_psum")
        gb_in_psum = sem("gb_in_psum")
        gb_moved = sem("gb_moved")
        y_ready = sem("y_ready")
        var_ready = sem("var_ready")
        std_ready = sem("std_ready")
        stats_ready = sem("stats_ready")
        rstd_ready = sem("rstd_ready")
        norm_ready = sem("norm_ready")
        scaled = sem("scaled")
        z_ready = sem("z_ready")
        result_ready = sem("result_ready")
        stored = sem("stored")
        waited = sem("waited")
        start_own = sem("start_own")
        block = ctx.enter_context(nc.Block())
        X2, H2, A2 = flat(g.X1[:, :, :]), flat(g.Hn[:, :, :]), flat(g.acc[:, :, :])
        outt = out.rearrange("(t p) d -> p t d", p=P)

        @block.sync
        def _(sp):
            load_three_times(sp, gate, skip.rearrange("(n a) -> n a", a=1), loaded)
            for n, vec in enumerate((ba, ln_g, ln_b)):
                load_three_times(sp, by_type[:, n * D:(n + 1) * D], vec, loaded)
            for n in range(NTY):
                sp.dma_start(Wt[:, :, n, :], Wa[n].rearrange("(c k) n -> k c n", c=KC)).then_inc(w_loaded, 16)

            with sp.Fori(0, NIT) as i:
                sp.wait_ge(result_ready, i * NU + NU)
                sp.dma_start(outt[:, bass.ds(i * NU, NU), :], z[:, :, :]).then_inc(stored, 16)
            sp.wait_ge(stored, 16 * NIT)

        @block.gpsimd
        def _(pool):
            def place_types(n, i, u, done, first):
                k = i * NU + u
                if not first:
                    pool.wait_ge(done, k - NU + 1)
                nc.gpsimd.tensor_copy(types[:, n, u, :], ty.hot[:, bass.ds(k * P, P)]).then_inc(types_ready[n], 1)

            def scale(i, u, first):
                k = i * NU + u
                pool.wait_ge(norm_ready, k + 1)
                pool.wait_ge(gb_moved, k + 1)
                if not first:
                    pool.wait_ge(stored, 16 * i)
                nc.gpsimd.tensor_tensor(z[:, u, :], norm[:, u, :], gbs[:, u % 2, 0:D], ALU.mult).then_inc(scaled, 1)
                pool.wait_ge(scaled, k + 1)
                nc.gpsimd.tensor_tensor(z[:, u, :], z[:, u, :], gbs[:, u % 2, D:2 * D], ALU.add).then_inc(z_ready, 1)

            def turn(i, number):
                for u in range(NU):
                    if number != 0:
                        scale(i - 1, u, number == 1)
                    place_types(1, i, u, gb_in_psum, number == 0)
                    if number != NIT - 1:
                        place_types(0, i + 1, u, out_in_psum, False)

            for u in range(NU):
                place_types(0, 0, u, out_in_psum, True)
            turn(0, 0)
            turn(1, 1)
            with pool.Fori(2, NIT - 1) as i:
                turn(i, None)
            turn(NIT - 1, NIT - 1)
            for u in range(NU):
                scale(NIT - 1, u, False)

        @block.scalar
        def _(act):
            act.wait_ge(loaded, 16 * 12)
            nc.scalar.activation(gate, gate, ACT.Exp, scale=-1.0).then_inc(skip_exp, 1)
            act.wait_ge(scalars_ready, 1)

            def inputs(i, u, first):
                k = i * NU + u
                if not first:
                    act.wait_ge(aggT_in_psum, k - NU + 1)
                nc.scalar.activation(agg[:, u, :], A2[:, bass.ds(k * ACCW, D)], ACT.Copy,
                                     scale=rn[:, bass.ds(k, 1)]).then_inc(agg_ready, 1)
                if not first:
                    act.wait_ge(y_ready, k - NU + 1)
                nc.scalar.activation(hk[:, u, :], tile(H2, k, D), ACT.Copy, scale=keep[:, bass.ds(k, 1)]) \
                    .then_inc(hk_ready, 1)

            def move_factors(i, u, first):
                k = i * NU + u
                act.wait_ge(gb_in_psum, k + 1)
                if not first or u >= 2:
                    act.wait_ge(z_ready, k - back(u) + 1)
                nc.scalar.copy(gbs[:, u % 2, :], psG[u % 2][0:P, :]).then_inc(gb_moved, 1)

            def turn(i, number):
                for u in range(NU):
                    if number != NIT - 1:
                        inputs(i + 1, u, False)
                    if number != 0:
                        move_factors(i - 1, u, number == 1)
                act.wait_ge(var_ready, i + 1)
                nc.scalar.activation(std[:, :], mv[:, :, 1], ACT.Sqrt, bias=g.eps[0:P, :]).then_inc(std_ready, 1)

            for u in range(NU):
                inputs(0, u, True)
            turn(0, 0)
            turn(1, 1)
            with act.Fori(2, NIT - 1) as i:
                turn(i, None)
            turn(NIT - 1, NIT - 1)
            for u in range(NU):
                move_factors(NIT - 1, u, False)

        @block.tensor
        def _(pe):
            pe.wait_ge(gate_ready, 1)
            for k in range(NT):
                ins = nc.tensor.matmul(psA[0:P, k:k + 1], ty.hot[:, k * P:(k + 1) * P], parts[:, 3 * D:VW],
                                       start=True, stop=True)
            ins.then_inc(alpha_in_psum, 1)

            def turn_input(i, u, first):
                k = i * NU + u
                pe.wait_ge(agg_ready, k + 1)
                if not first or u >= 2:
                    pe.wait_ge(am_ready, k - back(u) + 1)
                for c in range(KC):
                    ins = nc.tensor.transpose(psT[u % 2][:, c * P:(c + 1) * P], agg[:, u, c * 128:(c + 1) * 128],
                                              g.eye(P))
                ins.then_inc(aggT_in_psum, 1)

            def norm_factors(i, u, first):
                k = i * NU + u
                if not first or u >= 2:
                    pe.wait_ge(gb_moved, k - back(u) + 1)
                pe.wait_ge(types_ready[1], k + 1)
                nc.tensor.matmul(psG[u % 2][0:P, :], types[:, 1, u, :], parts[:, D:3 * D],
                                 start=True, stop=True).then_inc(gb_in_psum, 1)

            def transform(i, u, first):
                k = i * NU + u
                pe.wait_ge(am_ready, k + 1)
                if not first or u >= 2:
                    pe.wait_ge(y_ready, k - back(u) + 1)
                pe.wait_ge(types_ready[0], k + 1)
                nc.tensor.matmul(psO[u % 2][0:P, 0:D], types[:, 0, u, :], parts[:, 0:D],
                                 start=True, stop=False)
                for n in range(NTY):
                    for c in range(KC):
                        ins = nc.tensor.matmul(psO[u % 2][0:P, 0:D], am[:, u, n, c * P:(c + 1) * P], Wt[:, c, n, :],
                                               start=False, stop=(n == NTY - 1 and c == KC - 1))
                ins.then_inc(out_in_psum, 1)

            def turn(i, number):
                for u in range(NU):
                    transform(i, u, number == 0)
                    if number != NIT - 1:
                        turn_input(i + 1, u, False)
                    if number != 0:
                        norm_factors(i - 1, u, number == 1)

            for u in range(NU):
                turn_input(0, u, True)
            pe.wait_ge(w_loaded, 16 * NTY)
            turn(0, 0)
            turn(1, 1)
            with pe.Fori(2, NIT - 1) as i:
                turn(i, None)
            turn(NIT - 1, NIT - 1)
            for u in range(NU):
                norm_factors(NIT - 1, u, False)

        @block.vector
        def _(dve):
            s = Tally(dve, start_own)
            dve.wait_ge(skip_exp, 1)
            s.done(nc.vector.tensor_scalar(gate, gate, 1.0, None, ALU.add))
            s.done(nc.vector.reciprocal(gate, gate))
            split_rows(nc, s, ty, by_type[:, :], parts[:, :])
            dve.sem_inc(gate_ready, 1)
            s.done(nc.vector.tensor_scalar(some[:, :, :], g.cnt[:, :, :], 0.5, None, ALU.is_ge))
            s.done(nc.vector.reduce_sum(nrel[:, :], some[:, :, :], axis=AX.X))
            s.done(nc.vector.tensor_scalar(has[:, :], nrel[:, :], 0.5, None, ALU.is_ge))
            s.done(nc.vector.tensor_scalar(alone[:, :], has[:, :], -1.0, 1.0, ALU.mult, ALU.add))
            s.done(nc.vector.tensor_scalar(nrel[:, :], nrel[:, :], 1.0, None, ALU.max))
            s.done(nc.vector.reciprocal(rn[:, :], nrel[:, :]))
            dve.wait_ge(alpha_in_psum, 1)
            s.done(nc.vector.tensor_copy(alpha[:, :], psA[0:P, 0:NT]))
            nc.vector.tensor_scalar(keep[:, :], alpha[:, :], -1.0, 1.0, ALU.mult, ALU.add).then_inc(scalars_ready, 1)

            def mask(i, u, first):
                k = i * NU + u
                dve.wait_ge(aggT_in_psum, k + 1)
                if not first:
                    dve.wait_ge(out_in_psum, k - NU + 1)
                row = ty.row[:, bass.ds(k * P, P)].unsqueeze(1).to_broadcast([128, KC, P])
                for n in range(NTY):
                    ins = nc.vector.scalar_tensor_tensor(am[:, u, n, :].rearrange("p (c n) -> p c n", c=KC), row,
                                                         float(n),
                                                         psT[u % 2][:, 0:KC * P].rearrange("p (c n) -> p c n", c=KC),
                                                         ALU.is_equal, ALU.mult)
                ins.then_inc(am_ready, 1)

            def finish(i, u):
                k = i * NU + u
                dve.wait_ge(z_ready, k + 1)
                dve.wait_ge(hx_ready, k + 1)
                nc.vector.scalar_tensor_tensor(z[:, u, :], z[:, u, :], has[:, bass.ds(k, 1)], hx[:, u, :],
                                               ALU.mult, ALU.add).then_inc(result_ready, 1)

            def residual(i, u, first):
                k = i * NU + u
                if not first:
                    dve.wait_ge(result_ready, k - NU + 1)
                nc.vector.scalar_tensor_tensor(hx[:, u, :], tile(H2, k, D), alone[:, bass.ds(k, 1)], tile(X2, k, D),
                                               ALU.mult, ALU.add).then_inc(hx_ready, 1)

            def turn(i, first, last):
                for u in range(NU):
                    k = i * NU + u
                    dve.wait_ge(out_in_psum, k + 1)
                    dve.wait_ge(hk_ready, k + 1)
                    if not first:
                        dve.wait_ge(norm_ready, k - NU + 1)
                    nc.vector.scalar_tensor_tensor(y[:, u, :], psO[u % 2][0:P, 0:D], alpha[:, bass.ds(k, 1)], hk[:, u, :],
                                                   ALU.mult, ALU.add).then_inc(y_ready, 1)
                    if not last:
                        mask(i + 1, u, False)
                    if not first and u > 0:
                        finish(i - 1, u - 1)
                    if u > 0:
                        residual(i, u - 1, first)
                dve.wait_ge(y_ready, i * NU + NU)
                dve.sem_inc(waited, 1)
                for u in range(NU):
                    ins = nc.vector.bn_stats(stats[:, u, :], y[:, u, :])
                ins.then_inc(stats_ready, 1)
                dve.wait_ge(stats_ready, i + 1)
                dve.sem_inc(waited, 1)
                for u in range(NU):
                    ins = nc.vector.bn_aggr(mv[:, u, :], stats[:, u, :])
                ins.then_inc(var_ready, 1)
                if not first:
                    finish(i - 1, NU - 1)
                residual(i, NU - 1, first)
                dve.wait_ge(std_ready, i + 1)
                nc.vector.reciprocal(rstd[:, :], std[:, :]).then_inc(rstd_ready, 1)
                dve.wait_ge(rstd_ready, i + 1)
                for u in range(NU):
                    nc.vector.tensor_scalar(norm[:, u, :], y[:, u, :], mv[:, u, 0:1], rstd[:, u:u + 1],
                                            ALU.subtract, ALU.mult).then_inc(norm_ready, 1)

            for u in range(NU):
                mask(0, u, True)
            turns(dve, turn)
            for u in range(NU):
                finish(NIT - 1, u)


def gnn(nc, x, src, dst, et6, et64, node_type, query, Wq0, bq0, Wk0, bk0, Wv0, bv0, rel_w, Wo, bo, gamma, beta,
        Wk1, bk1, Wq1, bq1, Wv1, bv1, Wa, ba, rel_pri, rel_att, rel_msg, skip, ln_g, ln_b, out):
    with ExitStack() as ctx:
        g = Persistent(ctx, nc)
        order_phase(nc, g, src, dst, et6, et64)
        setup_phase(nc, g, x)
        project_phase(nc, g, query, Wq0, bq0, Wk0, bk0, Wv0, bv0)
        with ExitStack() as edges:
            g.edge_tensors(edges, nc, 0)
            score_phase(nc, g, 0, g.kv0, rel_w)
            softmax_phase(nc, g, 0)
            aggregate_phase(nc, g, 0)
        ty = Types(ctx, nc)
        layer0_output_phase(nc, g, ty, Wo, bo, gamma, beta, node_type)
        typed_project_phase(nc, g, ty, Wk1, bk1, Wq1, bq1, Wv1, bv1, rel_att, rel_msg, rel_pri)
        with ExitStack() as edges:
            g.edge_tensors(edges, nc, 1)
            score_phase(nc, g, 1, g.kv1, None)
            softmax_phase(nc, g, 1)
            aggregate_phase(nc, g, 1)
        layer1_output_phase(nc, g, ty, Wa, ba, skip, ln_g, ln_b, out)


_INS = ['x', 'src', 'dst', 'edge_type_6', 'edge_type_64', 'node_type_3', 'L0_gnn_query_emb', 'L0_gnn_Wq', 'L0_gnn_bq',
        'L0_gnn_Wk', 'L0_gnn_bk', 'L0_gnn_Wv', 'L0_gnn_bv', 'L0_gnn_rel_w', 'L0_gnn_Wo', 'L0_gnn_bo', 'L0_gnn_gamma',
        'L0_gnn_beta', 'L1_gnn_Wk', 'L1_gnn_bk', 'L1_gnn_Wq', 'L1_gnn_bq', 'L1_gnn_Wv', 'L1_gnn_bv', 'L1_gnn_Wa',
        'L1_gnn_ba', 'L1_gnn_rel_pri', 'L1_gnn_rel_att', 'L1_gnn_rel_msg', 'L1_gnn_skip', 'L1_gnn_ln_g', 'L1_gnn_ln_b']


def kernel(**inputs):
    import numpy as _np
    import concourse.bacc as _bacc
    from concourse import mybir as _mybir
    from concourse.bass_utils import run_bass_kernel_spmd as _run

    nc = _bacc.Bacc("TRN2", target_bir_lowering=False, num_devices=1)
    arrays, args = {}, []
    for name in _INS:
        a = _np.ascontiguousarray(inputs[name])
        arrays[f"in_{name}_dram"] = a
        args.append(nc.dram_tensor(f"in_{name}_dram", a.shape, _mybir.dt.from_np(a.dtype), kind="ExternalInput").ap())
    args.append(nc.dram_tensor("out_0_dram", (N, D), _mybir.dt.float32, kind="ExternalOutput").ap())
    gnn(nc, *args)
    r = _run(nc, [arrays], core_ids=[0])
    return r.results[0]["out_0_dram"]
```
